# Optimizing a Trainium2 kernel written in Bass

```python
import numpy as np
import jax
import jax.numpy as jnp

def _softmax(x, axis=-1):
    return jax.nn.softmax(x, axis=axis)

def _gelu(x):
    return jax.nn.gelu(x, approximate=True)

def _silu(x):
    return jax.nn.silu(x)

def _sigmoid(x):
    return jax.nn.sigmoid(x)

def _layernorm(x, axis=-1, eps=1e-05):
    m = jnp.mean(x, axis=axis, keepdims=True)
    v = jnp.var(x, axis=axis, keepdims=True)
    return (x - m) / jnp.sqrt(v + eps)

def _scatter_add(tgt, idx, src, axis=0):
    return tgt.at[idx].add(src)

def _segment_sum(src, seg, n):
    return jax.ops.segment_sum(src, seg, n)
kernel_name = 'mk_hybrid_d1_jaxref_r4_9bca28'

def setup_inputs(seed: int=0):
    np.random.seed(seed)
    _w = jnp.asarray

    def _L0_attn_a_setup():
        import jax, jax.numpy as jnp
        import numpy as np
        H = 16
        G = 4
        MAX_POS = 128
        key = jax.random.key(seed)
        ks = jax.random.split(key, 6)
        B, T, D = (8, 256, 256)
        hd = D // H
        s = 0.02
        return {'x': jax.random.normal(ks[0], (B, T, D), jnp.float32), 'Wq': jax.random.normal(ks[1], (D, D), jnp.float32) * s, 'Wk': jax.random.normal(ks[2], (hd * G, D), jnp.float32) * s, 'Wv': jax.random.normal(ks[3], (hd * G, D), jnp.float32) * s, 'Wo': jax.random.normal(ks[4], (D, D), jnp.float32) * s, 'E': jax.random.normal(ks[5], (2 * MAX_POS - 1, hd), jnp.float32) * s}
    _L0_attn_a_in = _L0_attn_a_setup()

    def _L0_attn_b_setup():
        import math
        import jax, jax.numpy as jnp
        import numpy as np
        EMBED_DIM = 256
        NUM_HEADS = 16
        HEAD_DIM = EMBED_DIM // NUM_HEADS

        def _xavier(key, fan_in, fan_out):
            lim = math.sqrt(6.0 / (fan_in + fan_out))
            return jax.random.uniform(key, (fan_out, fan_in), jnp.float32, -lim, lim)
        key = jax.random.key(seed)
        kx, kq, kk, kv, ko = jax.random.split(key, 5)
        B, L = (4, 512)
        x = jax.random.normal(kx, (B, L, EMBED_DIM), jnp.float32)
        return {'x': x, 'wq': _xavier(kq, EMBED_DIM, EMBED_DIM), 'bq': jnp.zeros((EMBED_DIM,), jnp.float32), 'wk': _xavier(kk, EMBED_DIM, EMBED_DIM), 'bk': jnp.zeros((EMBED_DIM,), jnp.float32), 'wv': _xavier(kv, EMBED_DIM, EMBED_DIM), 'bv': jnp.zeros((EMBED_DIM,), jnp.float32), 'wo': _xavier(ko, EMBED_DIM, EMBED_DIM), 'bo': jnp.zeros((EMBED_DIM,), jnp.float32)}
    _L0_attn_b_in = _L0_attn_b_setup()

    def _L0_ffn_setup():
        import math
        import jax, jax.numpy as jnp
        import numpy as np
        CAPACITY_FACTOR = 1.25
        key = jax.random.key(seed)
        ks = jax.random.split(key, 5)
        B, S, H, F, E = (4, 1024, 256, 256, 32)
        scale_in = 1.0 / math.sqrt(H)
        scale_mid = 1.0 / math.sqrt(F)
        return {'x': jax.random.normal(ks[0], (B, S, H), dtype=jnp.float32), 'w_router': jax.random.normal(ks[1], (H, E), dtype=jnp.float32) * scale_in, 'w_gate': jax.random.normal(ks[2], (E, H, F), dtype=jnp.float32) * scale_in, 'w_up': jax.random.normal(ks[3], (E, H, F), dtype=jnp.float32) * scale_in, 'w_down': jax.random.normal(ks[4], (E, F, H), dtype=jnp.float32) * scale_mid}
    _L0_ffn_in = _L0_ffn_setup()
    _d = {'L0_attn_a_x': _L0_attn_a_in['x'], 'L0_attn_a_Wq': _L0_attn_a_in['Wq'], 'L0_attn_a_Wk': _L0_attn_a_in['Wk'], 'L0_attn_a_Wv': _L0_attn_a_in['Wv'], 'L0_attn_a_Wo': _L0_attn_a_in['Wo'], 'L0_attn_a_E': _L0_attn_a_in['E'], 'L0_attn_b_wq': _L0_attn_b_in['wq'], 'L0_attn_b_bq': _L0_attn_b_in['bq'], 'L0_attn_b_wk': _L0_attn_b_in['wk'], 'L0_attn_b_bk': _L0_attn_b_in['bk'], 'L0_attn_b_wv': _L0_attn_b_in['wv'], 'L0_attn_b_bv': _L0_attn_b_in['bv'], 'L0_attn_b_wo': _L0_attn_b_in['wo'], 'L0_attn_b_bo': _L0_attn_b_in['bo'], 'L0_ffn_w_router': _L0_ffn_in['w_router'], 'L0_ffn_w_gate': _L0_ffn_in['w_gate'], 'L0_ffn_w_up': _L0_ffn_in['w_up'], 'L0_ffn_w_down': _L0_ffn_in['w_down']}
    _x0 = _d['L0_attn_a_x']
    _d['L0_attn_a_x'] = jax.random.normal(jax.random.fold_in(jax.random.key(seed), 1), (8, 1024, 256), dtype=_x0.dtype)
    del _x0
    return _d

def reference(L0_attn_a_x, L0_attn_a_Wq, L0_attn_a_Wk, L0_attn_a_Wv, L0_attn_a_Wo, L0_attn_a_E, L0_attn_b_wq, L0_attn_b_bq, L0_attn_b_wk, L0_attn_b_bk, L0_attn_b_wv, L0_attn_b_bv, L0_attn_b_wo, L0_attn_b_bo, L0_ffn_w_router, L0_ffn_w_gate, L0_ffn_w_up, L0_ffn_w_down):

    def _L0_attn_a_ref(x, Wq, Wk, Wv, Wo, E):
        import jax, jax.numpy as jnp
        import numpy as np
        H = 16
        G = 4
        MAX_POS = 128
        B, T, D = x.shape
        hd = D // H
        r = H // G
        q = (x @ Wq.T).reshape(B, T, H, hd).transpose(0, 2, 1, 3)
        k = (x @ Wk.T).reshape(B, T, G, hd)
        v = (x @ Wv.T).reshape(B, T, G, hd)
        k = jnp.repeat(k, r, axis=2).transpose(0, 2, 1, 3)
        v = jnp.repeat(v, r, axis=2).transpose(0, 2, 1, 3)
        q = q * (1.0 / hd) ** 0.5
        scores = jnp.einsum('bhqd,bhkd->bhqk', q, k)
        pos = jnp.arange(T)
        dist = jnp.clip(pos[None, :] - pos[:, None], -MAX_POS + 1, MAX_POS - 1) + MAX_POS - 1
        R = E[dist]
        bias = jnp.einsum('bhqd,kqd->bhqk', q, R)
        scores = scores + bias
        attn = jax.nn.softmax(scores, axis=-1)
        out = jnp.einsum('bhqk,bhkd->bhqd', attn, v)
        out = out.transpose(0, 2, 1, 3).reshape(B, T, D)
        return out @ Wo.T

    def _L0_attn_b_ref(x, wq, bq, wk, bk, wv, bv, wo, bo):
        import math
        import jax, jax.numpy as jnp
        import numpy as np
        EMBED_DIM = 256
        NUM_HEADS = 16
        HEAD_DIM = EMBED_DIM // NUM_HEADS

        def _xavier(key, fan_in, fan_out):
            lim = math.sqrt(6.0 / (fan_in + fan_out))
            return jax.random.uniform(key, (fan_out, fan_in), jnp.float32, -lim, lim)
        B, L, D = x.shape
        H, Dh = (NUM_HEADS, HEAD_DIM)

        def proj(w, b):
            return (jnp.einsum('bld,ed->ble', x, w) + b).reshape(B, L, H, Dh).transpose(0, 2, 1, 3)
        q, k, v = (proj(wq, bq), proj(wk, bk), proj(wv, bv))
        scale = 1.0 / math.sqrt(H)
        scores = jnp.einsum('bhqd,bhkd->bhqk', q, k) * scale
        attn = jax.nn.softmax(scores, axis=-1)
        out = jnp.einsum('bhqk,bhkd->bhqd', attn, v)
        out = out.transpose(0, 2, 1, 3).reshape(B, L, D)
        return jnp.einsum('bld,ed->ble', out, wo) + bo

    def _L0_ffn_ref(x, w_router, w_gate, w_up, w_down):
        import math
        import jax, jax.numpy as jnp
        import numpy as np
        CAPACITY_FACTOR = 1.25
        B, S, H = x.shape
        E = w_gate.shape[0]
        T = B * S
        C = int(math.ceil(CAPACITY_FACTOR * T / E))
        xt = x.reshape(T, H)
        logits = xt @ w_router
        probs = jax.nn.softmax(logits, axis=-1)
        top1 = jnp.argmax(probs, axis=-1)
        gate = jnp.take_along_axis(probs, top1[:, None], axis=1)[:, 0]
        onehot = jax.nn.one_hot(top1, E, dtype=jnp.int32)
        pos = jnp.cumsum(onehot, axis=0)[jnp.arange(T), top1] - 1
        accepted = pos < C
        slot = jnp.where(accepted, top1 * C + pos, E * C)
        buf = jnp.zeros((E * C + 1, H), dtype=x.dtype).at[slot].set(xt)
        buf = buf[:E * C].reshape(E, C, H)
        g = jnp.einsum('ech,ehf->ecf', buf, w_gate)
        u = jnp.einsum('ech,ehf->ecf', buf, w_up)
        y = jnp.einsum('ecf,efh->ech', jax.nn.silu(g) * u, w_down)
        out_tok = y.reshape(E * C, H)[jnp.clip(slot, 0, E * C - 1)]
        out_tok = jnp.where(accepted[:, None], out_tok * gate[:, None], 0.0)
        return (xt + out_tok).reshape(B, S, H)
    x = L0_attn_a_x
    x = x + _L0_attn_a_ref(_layernorm(x, axis=-1), L0_attn_a_Wq, L0_attn_a_Wk, L0_attn_a_Wv, L0_attn_a_Wo, L0_attn_a_E)
    x = x + _L0_ffn_ref(_layernorm(x, axis=-1), L0_ffn_w_router, L0_ffn_w_gate, L0_ffn_w_up, L0_ffn_w_down)
    x = x + _L0_attn_b_ref(_layernorm(x, axis=-1), L0_attn_b_wq, L0_attn_b_bq, L0_attn_b_wk, L0_attn_b_bk, L0_attn_b_wv, L0_attn_b_bv, L0_attn_b_wo, L0_attn_b_bo)
    x = x + _L0_ffn_ref(_layernorm(x, axis=-1), L0_ffn_w_router, L0_ffn_w_gate, L0_ffn_w_up, L0_ffn_w_down)
    return x

_drawn_inputs = setup_inputs


def setup_inputs(seed=0):
    import zlib

    import numpy as np

    out = dict(_drawn_inputs(seed))
    spreads = {'L0_attn_b_bq': (0.0, 2.0),
     'L0_attn_b_bk': (0.0, 2.0),
     'L0_attn_b_bv': (0.0, 0.443),
     'L0_attn_b_bo': (0.0, 0.435)}
    factors = {'L0_attn_a_Wq': 8.0,
     'L0_attn_a_Wk': 8.0,
     'L0_attn_a_Wv': 8.0,
     'L0_attn_a_Wo': 8.0,
     'L0_attn_a_E': 8.0,
     'L0_attn_b_wq': 3.224}
    for name, (base, spread) in spreads.items():
        noise = np.random.default_rng([zlib.crc32(name.encode()), seed]).standard_normal(out[name].shape)
        drawn = base * np.exp(spread * noise) if base else spread * noise
        out[name] = jnp.asarray(drawn.astype(out[name].dtype))
    for name, factor in factors.items():
        out[name] = (out[name] * factor).astype(out[name].dtype)
    return out
```

```python
from contextlib import ExitStack

import concourse.bass as bass
from concourse import mybir

F32 = mybir.dt.float32
BF16 = mybir.dt.bfloat16
I32 = mybir.dt.int32
U32 = mybir.dt.uint32
ALU = mybir.AluOpType
ACT = mybir.ActivationFunctionType
AX = mybir.AxisListType

P = 128
B, T, D = 8, 1024, 256
N = B * T
NT = N // P
H, HD = 16, 16
G = 4
HG = H // G
MAX_POS = 128
NREL = 2 * MAX_POS - 1
EPS = 1e-5
E = 32
CAP = 320
CHUNK = 512
CT = CHUNK // P
KT = T // P
SPLITS = 6
KR = SPLITS * HD
KM = KR + 3
VW = 2 * HD
REL = NREL - 1 + P
RELROW = 512
UNITS = B * G * 2
HALF = T // 2
STEPS = 16
BODY = 4
MOVES = 8


def semaphores(nc, names, **rings):
    stack, made = ExitStack(), {}
    for name in names.split():
        made[name] = stack.enter_context(nc.semaphore(name))
    every = list(made.values())
    for name, n in rings.items():
        made[name] = [stack.enter_context(nc.semaphore(f"{name}{k}")) for k in range(n)]
        every += made[name]

    def give_back():
        with nc.Block() as block:
            @block.sync
            def _(sp):
                for handle in every:
                    sp.sem_clear(handle)
        stack.close()

    return made, give_back


def wait(eng, sem, count):
    if not isinstance(count, int) or count > 0:
        eng.wait_ge(sem, count)


def wait_apart(eng, s, sem, count):
    wait(eng, sem, count)
    if not isinstance(count, int):
        eng.sem_inc(s["passed"], 1)


def load_transposed(nc, kind, weights, ident):
    s, give_back = semaphores(nc, "w_read w_turned w_copied")
    with ExitStack() as ctx:
        raws = [ctx.enter_context(nc.sbuf_tensor(f"{kind}_raw_{k}", [P, 2, D], F32)) for k in range(len(weights))]
        pt = ctx.enter_context(nc.psum_tensor(f"{kind}_w_pt", [P, 2, 4, P], F32))
        jobs = [(k, a) for k, (w, _, _) in enumerate(weights) for a in range(-(-w.shape[0] // P))]
        with nc.Block() as block:
            @block.sync
            def _(sp):
                for k, (w, _, _) in enumerate(weights):
                    rows = min(P, w.shape[0])
                    sp.dma_start(raws[k][0:rows, 0:w.shape[0] // rows, :],
                                 w.rearrange("(a p) d -> p a d", p=rows)).then_inc(s["w_read"], 16)

            @block.tensor
            def _(pe):
                pe.wait_ge(s["w_read"], 16 * len(weights))
                for n, (k, a) in enumerate(jobs):
                    rows = min(P, weights[k][0].shape[0])
                    wait(pe, s["w_copied"], n - 1)
                    for half in range(2):
                        last = nc.tensor.transpose(pt[:, n % 2, half, 0:rows],
                                                   raws[k][0:rows, a, half * P:(half + 1) * P],
                                                   ident[0:rows, 0:rows])
                    last.then_inc(s["w_turned"], 1)

            @block.vector
            def _(dve):
                for n, (k, a) in enumerate(jobs):
                    w, out, view = weights[k]
                    rows = min(P, w.shape[0])
                    dve.wait_ge(s["w_turned"], n + 1)
                    for half in range(2):
                        dst, src = view(out[:, half, a * rows:(a + 1) * rows], pt[:, n % 2, half, 0:rows])
                        last = nc.vector.tensor_copy(dst, src)
                    last.then_inc(s["w_copied"], 1)
    give_back()


def as_is(dst, src):
    return dst, src


def by_width(dst, src):
    return dst.rearrange("p (d h) -> p d h", d=HD), src.rearrange("p (h d) -> p d h", d=HD)


def by_half_width(dst, src):
    return (dst.rearrange("p (a d j) -> p a d j", a=2, d=HD),
            src.rearrange("p (a j d) -> p a d j", a=2, d=HD))


def normalize_steps(nc, s, xc, stats, mv, rstd, xn, k):
    for t in range(CT):
        last = nc.vector.bn_stats(stats[:, t, :], xc[:, t, :])
    last.then_inc(s["stat"], 1)
    wait_apart(nc.vector, s, s["stat"], 2 * k + 1)
    for t in range(CT):
        last = nc.vector.bn_aggr(mv[:, t, :], stats[:, t, :])
    last.then_inc(s["stat"], 1)
    nc.vector.wait_ge(s["stat"], 2 * k + 2)
    nc.vector.tensor_scalar(rstd[:, 0, :], mv[:, :, 1], EPS, None, ALU.add).then_inc(s["var"], 1)
    nc.vector.wait_ge(s["dev"], k + 1)
    nc.vector.reciprocal(rstd[:, 2, :], rstd[:, 1, :]).then_inc(s["rec"], 1)
    nc.vector.wait_ge(s["rec"], k + 1)
    for t in range(CT):
        last = nc.vector.tensor_scalar(xn[:, t, :], xc[:, t, :], mv[:, t, 0:1], rstd[:, 2, t:t + 1],
                                       ALU.subtract, ALU.mult)
    last.then_inc(s["xn_ready"], 1)


def project(nc, kind, x_dram, X, w, Q, K, V, ident):
    A = kind == "A"
    heads = G if A else H
    nv = heads * HD
    cols = V.shape[4]
    s, give_back = semaphores(nc, "w_in bias_in stat var dev rec xn_ready turned xt_ready mm v_mm q1 qf r1 q2 q3"
                   " v_ready bias_row bias_mm bias_col ones passed", x_in=2, parts_out=4, v_out=2)
    with ExitStack() as ctx:
        def sb(name, shape, dt=F32):
            return ctx.enter_context(nc.sbuf_tensor(f"{kind}p_{name}", shape, dt))

        def psum(name, shape):
            return ctx.enter_context(nc.psum_tensor(f"{kind}p_{name}", shape, F32))

        nk = 64 if A else D
        wqT, wkT, wvT = sb("wqT", [P, 2, D]), sb("wkT", [P, 2, nk]), sb("wvT", [P, 2, nv])
        load_transposed(nc, kind, [(w["q"], wqT, by_width), (w["k"], wkT, by_half_width if A else by_width),
                             (w["v"], wvT, as_is)], ident)
        if A:
            tensors = [(0, P, 0.25, None), (1, P, 0.25, None), (2, nk, 1.0, 0), (2, nk, 1.0, 1)]
        else:
            tensors = [(0, P, 0.25, 0), (1, P, 0.25, 1), (2, P, 1.0, 2), (3, P, 1.0, 3)]
        products = [(wqT, 0, P), (wqT, P, P)] + ([(wkT, 0, nk)] if A else [(wkT, 0, P), (wkT, P, P)])
        xin = sb("xin", [P, 2, CT, D]) if A else None
        stats, mv, rstd = sb("stats", [P, CT, 6]), sb("mv", [P, CT, 2]), sb("rstd", [P, 3, CT])
        xn = sb("xn", [P, 2, CT, D])
        xT = sb("xT", [P, 2, 2, CHUNK])
        parts = sb("parts", [P, 4, 3, CHUNK], BF16)
        full, rest = sb("full", [P, 4, CHUNK]), sb("rest", [P, 4, CHUNK])
        vs = sb("vs", [P, 2, CT, heads, VW])
        brow, bprm, bcol = sb("brow", [1, 2, D]), sb("bprm", [1, 4, P]), sb("bcol", [P, 4])
        one = sb("one", [1, 1])
        bv = sb("bv", [P, nv])
        pT = psum("pT", [P, 2, CHUNK])
        pR = [psum(f"pR{k}", [P, CHUNK]) for k in range(len(products))]
        pV = psum("pV", [P, CT, nv])

        with nc.Block() as block:
            @block.sync
            def _(sp):
                if A:
                    sp.dma_start(brow[0:1, 0, 0:HD], w["E"][0:1, :]).then_inc(s["bias_in"], 16)
                    sp.dma_start(brow[0:1, 1, 0:HD], w["E"][NREL - 1:NREL, :]).then_inc(s["bias_in"], 16)
                else:
                    sp.dma_start(brow[0:1, 0, :], w["bq"].rearrange("(a n) -> a n", a=1)).then_inc(s["bias_in"], 16)
                    sp.dma_start(brow[0:1, 1, :], w["bk"].rearrange("(a n) -> a n", a=1)).then_inc(s["bias_in"], 16)
                    sp.dma_start(bv[:, :], w["bv"].rearrange("(a n) -> a n", a=1).broadcast_to([P, nv])).then_inc(s["w_in"], 16)
                    sp.wait_ge(s["w_in"], 16)

            @block.vector
            def _(dve):
                nc.vector.memset(one[:, :], 1.0)
                nc.vector.memset(vs[:, :, :, :, :], 1.0).then_inc(s["ones"], 1)
                dve.wait_ge(s["bias_in"], 32)
                for k in range(2 if A else 4):
                    if A:
                        dst = bprm[0:1, k, 0:nk].rearrange("o (a d j) -> o a d j", a=2, d=HD)
                        src = brow[0:1, k, 0:HD].unsqueeze(1).unsqueeze(3).broadcast_to([1, 2, HD, 2])
                    else:
                        dst = bprm[0:1, k, :].rearrange("o (d h) -> o d h", d=HD)
                        src = brow[0:1, k // 2, (k % 2) * P:(k % 2 + 1) * P].rearrange("o (h d) -> o d h", d=HD)
                    last = nc.vector.tensor_scalar(dst, src, 1.0 if A or k > 1 else 0.25, None, ALU.mult)
                last.then_inc(s["bias_row"], 1)
                dve.wait_ge(s["bias_mm"], 1)
                rows = nk if A else P
                nc.vector.tensor_copy(bcol[0:rows, 0:2 if A else 4], pT[0:rows, 0, 0:2 if A else 4]).then_inc(s["bias_col"], 1)

            @block.tensor
            def _(pe):
                pe.wait_ge(s["bias_row"], 1)
                rows = nk if A else P
                for k in range(2 if A else 4):
                    last = nc.tensor.matmul(pT[0:rows, 0, k:k + 1], bprm[0:1, k, 0:rows], one[0:1, 0:1],
                                            start=True, stop=True)
                last.then_inc(s["bias_mm"], 1)

        M = len(tensors)

        def part(m, rows, k):
            return parts[0:rows, m, k if m < 2 else 2 - k, :]


        def chunks(eng, stages):
            def body(i):
                for j in (0, 1):
                    for lag, step in stages:
                        k = j + lag
                        if not isinstance(i, int) or 0 <= 2 * i + k < 2 * B:
                            step(2 * i + k, k % 2, i + k // 2)
            body(-1)
            body(0)
            with eng.Fori(1, B - 1) as i:
                body(i)
            body(B - 1)

        with nc.Block() as block:
            @block.sync
            def _(sp):
                def load(c, half, b):
                    wait_apart(sp, s, s["xn_ready"], c - 1)
                    sp.dma_start(xin[:, half, :, :],
                                 x_dram[b, half * HALF:(half + 1) * HALF, :]
                                 .rearrange("(t p) d -> p t d", p=P)).then_inc(s["x_in"][half], 16)

                def store(c, half, b):
                    wait_apart(sp, s, s["v_ready"], c + 1)
                    for g in range(G):
                        sp.dma_start(V[b * 2 + g // 2, :, g % 2, half * CT:(half + 1) * CT, :],
                                     vs[:, half, :, g * (heads // G):(g + 1) * (heads // G), :]
                                     .rearrange("p t h c -> p t (h c)")).then_inc(s["v_out"][half], 16)
                    tok = slice(half * HALF, (half + 1) * HALF)
                    for m, (_, rows, _, _) in enumerate(tensors):
                        wait_apart(sp, s, s["q3"], M * c + (m + 1))
                        if not A or m < 2:
                            dst = [(Q if m < 2 else K)[b * 2 + m % 2, :, :, tok]]
                            src = [parts[:, m, :, :]]
                        else:
                            dst = [K[m - 2, b * 2 + a, :, :, tok] for a in (0, 1)]
                            src = [parts[a * 32:(a + 1) * 32, m, :, :] for a in (0, 1)]
                        for o, i_ in zip(dst, src):
                            sp.dma_start(o.rearrange("s p t -> p s t"), i_).then_inc(s["parts_out"][m], 16)

                chunks(sp, ([(1, load)] if A else []) + [(0, store)])
                for m in range(M):
                    sp.wait_ge(s["parts_out"][m], 16 * 2 * B * (2 if A and m > 1 else 1))
                for half in range(2):
                    sp.wait_ge(s["v_out"][half], 16 * G * B)

            @block.vector
            def _(dve):
                def norm(c, half, b):
                    if A:
                        dve.wait_ge(s["x_in"][half], 16 * (b + 1))
                        xc = xin[:, half, :, :]
                    else:
                        xc = X[:, bass.ds(c * CT, CT), :]
                    wait_apart(dve, s, s["turned"], c - 1)
                    normalize_steps(nc, s, xc, stats, mv, rstd, xn[:, half, :, :], c)

                def split(c, half, b):
                    dve.wait_ge(s["v_mm"], c + 1)
                    wait(dve, s["v_out"][half], 16 * G * b)
                    src = pV[:, :, :].rearrange("p t (h d) -> p t h d", d=HD)
                    for t in range(CT):
                        if A:
                            last = nc.vector.tensor_copy(vs[:, half, t, :, 0:HD], src[:, t])
                        else:
                            last = nc.vector.tensor_tensor(vs[:, half, t, :, 0:HD], src[:, t],
                                                           bv[:, :].rearrange("p (h d) -> p h d", d=HD), ALU.add)
                    last.then_inc(s["v_ready"], 1)
                    for m, (prod, rows, scale, col) in enumerate(tensors):
                        dve.wait_ge(s["mm"], len(products) * c + (prod + 1))
                        wait(dve, s["r1"], M * c + (m + 1 - M))
                        nc.vector.tensor_scalar(full[0:rows, m, :], pR[prod][0:rows, :], scale,
                                                0.0 if col is None else bcol[0:rows, col:col + 1],
                                                ALU.mult, ALU.add).then_inc(s["qf"], 1)
                    for m, (prod, rows, scale, col) in enumerate(tensors):
                        dve.wait_ge(s["q2"], M * c + (m + 1))
                        nc.vector.tensor_tensor(part(m, rows, 2), rest[0:rows, m, :],
                                                part(m, rows, 1), ALU.subtract).then_inc(s["q3"], 1)

                chunks(dve, [(1, norm), (0, split)])

            @block.scalar
            def _(act):
                def root(c, half, b):
                    act.wait_ge(s["var"], c + 1)
                    nc.scalar.sqrt(rstd[:, 1, :], rstd[:, 0, :]).then_inc(s["dev"], 1)

                def copy(c, half, b):
                    act.wait_ge(s["turned"], c + 1)
                    wait(act, s["v_mm"], c - 1)
                    nc.scalar.copy(xT[:, half, :, :], pT[:, :, :]).then_inc(s["xt_ready"], 1)

                def split(c, half, b):
                    for m, (prod, rows, scale, col) in enumerate(tensors):
                        act.wait_ge(s["qf"], M * c + (m + 1))
                        wait(act, s["parts_out"][m], (2 * b + half) * (32 if A and m > 1 else 16))
                        nc.scalar.copy(part(m, rows, 0), full[0:rows, m, :]).then_inc(s["q1"], 1)
                    for m, (prod, rows, scale, col) in enumerate(tensors):
                        act.wait_ge(s["r1"], M * c + (m + 1))
                        nc.scalar.copy(part(m, rows, 1), rest[0:rows, m, :]).then_inc(s["q2"], 1)

                chunks(act, [(1, root), (0, split), (1, copy)])

            @block.gpsimd
            def _(pool):
                def split(c, half, b):
                    for m, (prod, rows, scale, col) in enumerate(tensors):
                        pool.wait_ge(s["q1"], M * c + (m + 1))
                        wait(pool, s["q3"], M * c + (m + 1 - M))
                        nc.gpsimd.tensor_tensor(rest[0:rows, m, :], full[0:rows, m, :],
                                                part(m, rows, 0), ALU.subtract).then_inc(s["r1"], 1)

                chunks(pool, [(0, split)])

            @block.tensor
            def _(pe):
                def turn(c, half, b):
                    pe.wait_ge(s["xn_ready"], c + 1)
                    wait(pe, s["xt_ready"], c)
                    for t in range(CT):
                        for d in range(2):
                            last = nc.tensor.transpose(pT[:, d, t * P:(t + 1) * P],
                                                       xn[:, half, t, d * P:(d + 1) * P], ident[:, :])
                    last.then_inc(s["turned"], 1)

                def multiply(c, half, b):
                    pe.wait_ge(s["xt_ready"], c + 1)
                    wait(pe, s["v_ready"], c)
                    for t in range(CT):
                        for d in range(2):
                            last = nc.tensor.matmul(pV[:, t, :], xT[:, half, d, t * P:(t + 1) * P],
                                                    wvT[:, d, :], start=(d == 0), stop=(d == 1))
                    last.then_inc(s["v_mm"], 1)
                    wait(pe, s["qf"], M * c)
                    for k, (wT, at, rows) in enumerate(products):
                        for d in range(2):
                            last = nc.tensor.matmul(pR[k][0:rows, :], wT[:, d, at:at + rows],
                                                    xT[:, half, d, :], start=(d == 0), stop=(d == 1))
                        last.then_inc(s["mm"], 1)

                chunks(pe, [(0, multiply), (1, turn)])
    give_back()


def relative_rows(nc, emb, rel, relrow, identF):
    s, give_back = semaphores(nc, "e_in e_turned e_copied e_diff e_parts e_placed z_set z_out")
    with ExitStack() as ctx:
        raw = ctx.enter_context(nc.sbuf_tensor("e_raw", [P, 2, HD], F32))
        eT = ctx.enter_context(nc.sbuf_tensor("e_T", [HD, 2 * P], F32))
        diff = ctx.enter_context(nc.sbuf_tensor("e_diff", [HD, 2, REL], F32))
        parts = ctx.enter_context(nc.sbuf_tensor("e_parts", [HD, 3, REL], BF16))
        zeros = ctx.enter_context(nc.sbuf_tensor("e_zeros", [P, STEPS, RELROW], F32))
        pt = ctx.enter_context(nc.psum_tensor("e_pt", [P, 2, P], F32))
        with nc.Block() as block:
            @block.sync
            def _(sp):
                sp.dma_start(raw[:, 0, :], emb[0:P, :]).then_inc(s["e_in"], 16)
                sp.dma_start(raw[0:NREL - P, 1, :], emb[P:NREL, :]).then_inc(s["e_in"], 16)
                sp.wait_ge(s["z_set"], 1)
                for r in range(relrow.shape[0]):
                    sp.dma_start(relrow[r].rearrange("q p c -> p q c"), zeros[:, :, :]).then_inc(s["z_out"], 16)
                sp.wait_ge(s["e_parts"], 3)
                at = 0
                for part, rows in ((2, 1), (1, 1), (0, 1), (1, 1), (0, 1), (0, 1)):
                    sp.dma_start(rel[at:at + HD, :], parts[:, part, :]).then_inc(s["e_placed"], 16)
                    at += HD
                sp.wait_ge(s["e_placed"], 16 * SPLITS)
                sp.wait_ge(s["z_out"], 16 * relrow.shape[0])

            @block.gpsimd
            def _(pool):
                nc.gpsimd.memset(zeros[:, :, :], 0.0).then_inc(s["z_set"], 1)

            @block.tensor
            def _(pe):
                pe.wait_ge(s["e_in"], 32)
                nc.tensor.transpose(pt[0:HD, 0, :], raw[:, 0, :], identF[:, :])
                nc.tensor.transpose(pt[0:HD, 1, 0:NREL - P], raw[0:NREL - P, 1, :],
                                    identF[0:NREL - P, 0:NREL - P]).then_inc(s["e_turned"], 1)

            @block.vector
            def _(dve):
                dve.wait_ge(s["e_turned"], 1)
                nc.vector.tensor_copy(eT[:, 0:NREL], pt[0:HD, :, :].rearrange("p a b -> p (a b)")[:, 0:NREL]).then_inc(s["e_copied"], 1)
                dve.wait_ge(s["e_copied"], 1)
                nc.vector.tensor_scalar(diff[:, 0, 0:NREL - 1], eT[:, 1:NREL], eT[:, 0:1], None, ALU.subtract)
                nc.vector.tensor_scalar(diff[:, 0, NREL - 1:REL], eT[:, NREL - 1:NREL].broadcast_to([HD, P]),
                                        eT[:, 0:1], None, ALU.subtract).then_inc(s["e_diff"], 1)
                dve.wait_ge(s["e_diff"], 1)
                nc.vector.tensor_copy(parts[:, 0, :], diff[:, 0, :]).then_inc(s["e_parts"], 1)
                dve.wait_ge(s["e_parts"], 1)
                nc.vector.tensor_tensor(diff[:, 1, :], diff[:, 0, :], parts[:, 0, :], ALU.subtract).then_inc(s["e_diff"], 1)
                dve.wait_ge(s["e_diff"], 2)
                nc.vector.tensor_copy(parts[:, 1, :], diff[:, 1, :]).then_inc(s["e_parts"], 1)
                dve.wait_ge(s["e_parts"], 2)
                nc.vector.tensor_tensor(parts[:, 2, :], diff[:, 1, :], parts[:, 1, :], ALU.subtract).then_inc(s["e_parts"], 1)
    give_back()


AHEAD_MAX = 24
AHEAD_REL = 34
AHEAD_REL_STORE = 32
AHEAD_REL_LOAD = 27


def attend(nc, kind, Q, K, V, OD, emb, RR, MD, identF, identB):
    A = kind == "A"
    names = "max_full max_free kept nm_ready ms_a ms_ready mt_full mt_copied md_out st_full probs pv_done ot_copied passed"
    rings = dict(qs_in=BODY, m_in=BODY, ks_in=2, v_in=2, od_out=2)
    if A:
        names, rings = names + " rel_full rel_copied band_ready", dict(rings, rel_out=8, bias_in=4)
    s, give_back = semaphores(nc, names, **rings)
    NV = 1 if A else HG
    KV = 2
    with ExitStack() as ctx:
        def sb(name, shape, dt=F32):
            return ctx.enter_context(nc.sbuf_tensor(f"{kind}a_{name}", shape, dt))

        def psum(name, shape):
            return ctx.enter_context(nc.psum_tensor(f"{kind}a_{name}", shape, F32))

        qs = sb("qs", [KM, BODY, HG, HALF], BF16)
        ks = sb("ks", [KM, 2, KV if A else HG, T], BF16)
        vals = sb("vals", [P, 2, KT, NV, VW])
        probs = sb("probs", [P, 4, 2, HALF])
        osb = sb("osb", [P, 2, HALF])
        NPART = 3 if A else 2
        mpart = sb("mpart", [P, 2, HG, 4, NPART])
        nm = sb("nm", [P, 2, HG * 4])
        nrest = sb("nrest", [P, HG * 4])
        ms = sb("ms", [P, 3, HG * 4], BF16)
        mT = sb("mT", [3 * HG * 4, P], BF16)
        if A:
            rel = sb("rel", [KR, REL], BF16)
            relsb = sb("relsb", [P, 2, 2, REL])
            bias = sb("bias", [P, 4, 2, 3 * P])
            near = sb("near", [P, BODY, HG, 4, 3 * P])
            relative_rows(nc, emb, rel, RR, identF)
        pE = psum("pE", [P, 2, 2, HALF])
        pM = psum("pM", [P, 2, HALF])
        pO = psum("pO", [P, HALF])
        pX = psum("pX", [P, HALF])

        with nc.Block() as block:
            @block.vector
            def _(dve):
                nc.vector.memset(ks[KR:KM, :, :, :], 1.0)

        def steps(eng, stages):
            def body(i):
                for k in range(BODY * STEPS):
                    for ahead, every, at, f in stages:
                        kk = k + ahead
                        if kk % every != at:
                            continue
                        if not isinstance(i, int) or 0 <= BODY * STEPS * i + kk < UNITS * STEPS:
                            f(i, kk)
            body(-1)
            body(0)
            with eng.Fori(1, UNITS // BODY - 1) as i:
                body(i)
            body(UNITS // BODY - 1)
            body(UNITS // BODY)

        def unit_of(i, kk):
            return BODY * i + kk // STEPS, (kk // STEPS) % BODY, kk % STEPS

        def step_of(i, kk):
            return BODY * STEPS * i + kk

        def window(kt_or_block, qh_block):
            return [r for r in (-1, 0, 1) if 0 <= qh_block + r < KT]

        with nc.Block() as block:
            @block.sync
            def _(sp):
                def load_queries(i, kk):
                    u, slot, _ = unit_of(i, kk)
                    body = i + kk // (STEPS * BODY)
                    wait_apart(sp, s, s["st_full"], STEPS * (u - BODY + 1))
                    qh, jj = slot % 2, slot // 2
                    at = 0
                    for parts in (3, 2, 1):
                        src = Q.rearrange("i s (d h) t -> i s d h t", d=HD)[
                            body, 0:parts, :, jj * HG:(jj + 1) * HG, qh * HALF:(qh + 1) * HALF]
                        sp.dma_start(qs[at:at + parts * HD, slot, :, :],
                                     src.rearrange("s d h t -> (s d) h t")).then_inc(s["qs_in"][slot], 16)
                        at += parts * HD

                def load_keys(i, kk):
                    u, slot, _ = unit_of(i, kk)
                    body = i + kk // (STEPS * BODY)
                    jj = slot // 2
                    wait_apart(sp, s, s["st_full"], STEPS * (u - 2))
                    at = 0
                    for parts in (3, 2, 1):
                        if A:
                            src = K.rearrange("v i s (d g) t -> i s d g v t", d=HD)[
                                body, 3 - parts:3, :, jj, :, :].rearrange("s d v t -> (s d) v t")
                        else:
                            src = K.rearrange("i s (d h) t -> i s d h t", d=HD)[
                                body, 3 - parts:3, :, jj * HG:(jj + 1) * HG, :].rearrange("s d h t -> (s d) h t")
                        sp.dma_start(ks[at:at + parts * HD, jj, :, :], src).then_inc(s["ks_in"][jj], 16)
                        at += parts * HD

                def load_values(i, kk):
                    u, slot, _ = unit_of(i, kk)
                    body = i + kk // (STEPS * BODY)
                    jj = slot // 2
                    wait_apart(sp, s, s["pv_done"], KT * (u - 2))
                    sp.dma_start(vals[:, jj, :, :, :].rearrange("p k h c -> p (k h c)"),
                                 V[body, :, jj, :, :].rearrange("p k c -> p (k c)")).then_inc(s["v_in"][jj], 16)

                def store_relative(i, kk):
                    u, slot, st = unit_of(i, kk)
                    g = step_of(i, kk)
                    wait_apart(sp, s, s["rel_copied"], g + 1)
                    wait_apart(sp, s, s["max_free"], 2 * (g - 2 * STEPS + 1))
                    sp.dma_start(RR[slot % 2, st - 1:st + 1, :, P + 1:P + 1 + REL].rearrange("q p c -> p q c"),
                                 relsb[:, (kk // 2) % 2, :, :]).then_inc(s["rel_out"][(kk // 2) % 8], 16)

                def load_relative(i, kk):
                    u, slot, st = unit_of(i, kk)
                    body = i + kk // (STEPS * BODY)
                    g = step_of(i, kk)
                    pair = kk // 2
                    wait_apart(sp, s, s["rel_out"][pair % 8], 16 * (4 * i + pair // 8 + 1))
                    wait_apart(sp, s, s["max_free"], 2 * (g - 7))
                    base = RR[slot % 2, st - 1:st + 1, :, :]
                    src = bass.AP(tensor=base.tensor, offset=base.offset + P - 1,
                                  ap=[[RELROW - 1, P], [P * RELROW, 2], [1, 3 * P]])
                    sp.dma_start(bias[:, pair % 4, :, :], src).then_inc(s["bias_in"][pair % 4], 16)

                def store_max(i, kk):
                    u, slot, _ = unit_of(i, kk)
                    wait_apart(sp, s, s["mt_copied"], u + 1)
                    sp.dma_start(MD[slot], mT[:, :]).then_inc(s["md_out"], 16)

                def load_max(i, kk):
                    u, slot, _ = unit_of(i, kk)
                    wait_apart(sp, s, s["md_out"], 16 * (u + 1))
                    wait_apart(sp, s, s["st_full"], STEPS * (u - BODY + 1))
                    sp.dma_start(qs[KR:KM, slot, :, :].rearrange("s h t -> s (h t)"),
                                 MD[slot].rearrange("(s r) q -> s (r q)", s=3)).then_inc(s["m_in"][slot], 16)

                def store_out(i, kk):
                    u, slot, _ = unit_of(i, kk)
                    body = i + kk // (STEPS * BODY)
                    wait_apart(sp, s, s["ot_copied"], u + 1)
                    sp.dma_start(OD[body, slot], osb[:, slot % 2, :]).then_inc(s["od_out"][slot % 2], 16)

                rel_stages = [(AHEAD_REL_STORE, 2, 1, store_relative), (AHEAD_REL_LOAD, 2, 1, load_relative)] if A else []
                steps(sp, rel_stages + [(3 * STEPS - 2, STEPS, 0, load_queries),
                                        (2 * STEPS - 2, 2 * STEPS, 0, load_keys),
                                        (2 * STEPS - 4, 2 * STEPS, 0, load_values),
                                        (5, STEPS, 0, store_max), (3, STEPS, 0, load_max),
                                        (-STEPS - 2, STEPS, 0, store_out)])
                for k in range(2):
                    sp.wait_ge(s["od_out"][k], 16 * UNITS // 2)

            def far_runs(q):
                runs = [(0, 0, q - 1), (1, q + 2, KT - q - 2)]
                return [r for r in runs if r[2] > 0]

            @block.tensor
            def _(pe):
                def relative(i, kk):
                    u, slot, st = unit_of(i, kk)
                    g = step_of(i, kk)
                    if st == 0:
                        wait(pe, s["qs_in"][slot], 48 * (i + kk // (STEPS * BODY) + 1))
                    wait(pe, s["rel_copied"], g)
                    wait(pe, s["mt_copied"], mt_before(i, kk - AHEAD_REL))
                    h, q = st // 4, st % 4
                    nc.tensor.matmul(pX[:, 0:REL], qs[0:KR, slot, h, q * P:(q + 1) * P], rel[:, :],
                                     start=True, stop=True).then_inc(s["rel_full"], 1)

                def mt_before(i, k):
                    return BODY * i + (k + 7 + STEPS - 1) // STEPS

                def maximum(i, kk):
                    u, slot, st = unit_of(i, kk)
                    g = step_of(i, kk)
                    h, qb = st // 4, st % 4
                    q = (slot % 2) * 4 + qb
                    jj = slot // 2
                    body = i + kk // (STEPS * BODY)
                    if st == 0:
                        wait(pe, s["qs_in"][slot], 48 * (body + 1))
                        if slot % 2 == 0:
                            wait(pe, s["ks_in"][jj], 48 * (body + 1))
                    query = qs[0:KR, slot, h, qb * P:(qb + 1) * P]
                    if A:
                        runs = []
                        col = 0
                        for v, first, n in far_runs(q):
                            while n:
                                m = min(n, 4 - col % 4)
                                runs.append((col, v, first, m))
                                col, first, n = col + m, first + m, n - m
                        near_blocks = window(0, q)
                        runs.append((8 - len(near_blocks), 0, q + near_blocks[0], len(near_blocks)))
                        for half in range(2):
                            wait(pe, s["max_free"], 2 * g + (half - 1))
                            for c, v, first, m in [r for r in runs if r[0] // 4 == half]:
                                last = nc.tensor.matmul(pM[:, half, (c % 4) * P:(c % 4 + m) * P], query,
                                                        ks[0:KR, jj, v, first * P:(first + m) * P],
                                                        start=True, stop=True)
                            last.then_inc(s["max_full"], 1)
                    else:
                        for half in range(2):
                            wait(pe, s["max_free"], 2 * g + (half - 1))
                            nc.tensor.matmul(pM[:, half, :], query, ks[0:KR, jj, h, half * HALF:(half + 1) * HALF],
                                             start=True, stop=True).then_inc(s["max_full"], 1)

                def turn_max(i, kk):
                    u, slot, _ = unit_of(i, kk)
                    pe.wait_ge(s["ms_ready"], u + 1)
                    wait(pe, s["mt_copied"], u)
                    if A:
                        wait(pe, s["rel_copied"], min(step_of(i, kk) - 7 + AHEAD_REL + 1, UNITS * STEPS)
                             if isinstance(i, int) else step_of(i, kk) - 7 + AHEAD_REL + 1)
                    nc.tensor.matmul(pX[0:3 * HG * 4, 0:P], ms[:, :, :].rearrange("p s r -> p (s r)"),
                                     identB[:, :], start=True, stop=True).then_inc(s["mt_full"], 1)

                def scores(i, kk):
                    u, slot, st = unit_of(i, kk)
                    g = step_of(i, kk)
                    kt, pair = st // 2, st % 2
                    jj = slot // 2
                    if st == 0:
                        wait(pe, s["m_in"][slot], 16 * (i + kk // (STEPS * BODY) + 1))
                        if A:
                            wait(pe, s["band_ready"], HG * (u + 1))
                    wait(pe, s["probs"], g - 1)
                    for hh in range(2):
                        h = 2 * pair + hh
                        out = pE[:, kk % 2, hh, :]
                        if not A:
                            last = nc.tensor.matmul(out, ks[0:KM, jj, h, kt * P:(kt + 1) * P],
                                                    qs[0:KM, slot, h, :], start=True, stop=True)
                            continue
                        first = (slot % 2) * 4
                        left = [b for b in range(4) if first + b >= kt + 2]
                        right = [b for b in range(4) if first + b <= kt - 2]
                        for v, blocks in ((0, left), (1, right)):
                            if blocks:
                                cols = slice(blocks[0] * P, (blocks[-1] + 1) * P)
                                last = nc.tensor.matmul(out[:, cols], ks[0:KM, jj, v, kt * P:(kt + 1) * P],
                                                        qs[0:KM, slot, h, cols], start=True, stop=True)
                        for b in range(4):
                            r = kt - (first + b)
                            if abs(r) <= 1:
                                last = nc.tensor.transpose(out[:, b * P:(b + 1) * P],
                                                           near[:, slot, h, b, (r + 1) * P:(r + 2) * P], identF[:, :])
                    last.then_inc(s["st_full"], 1)

                def weigh(i, kk):
                    u, slot, st = unit_of(i, kk)
                    g = step_of(i, kk)
                    kt, jj = st // 2, slot // 2
                    if st == 1:
                        if slot % 2 == 0:
                            wait(pe, s["v_in"][jj], 16 * (i + kk // (STEPS * BODY) + 1))
                        wait(pe, s["ot_copied"], u)
                    pe.wait_ge(s["probs"], g + 1)
                    for h in range(HG):
                        last = nc.tensor.matmul(pO[h * VW:(h + 1) * VW, :], vals[:, jj, kt, 0 if A else h, :],
                                                probs[:, (kk - 1 + h // 2) % 4, h % 2, :],
                                                start=(kt == 0), stop=(kt == KT - 1), tile_position=(0, h * VW))
                    last.then_inc(s["pv_done"], 1)

                steps(pe, ([(AHEAD_REL, 1, 0, relative)] if A else [])
                      + [(AHEAD_MAX, 1, 0, maximum), (7, STEPS, 0, turn_max), (0, 1, 0, scores), (-2, 2, 1, weigh)])

            @block.vector
            def _(dve):
                def maximum(i, kk):
                    u, slot, st = unit_of(i, kk)
                    g = step_of(i, kk)
                    h, qb = st // 4, st % 4
                    q = (slot % 2) * 4 + qb
                    s2 = slot % 2
                    if st == 0:
                        wait(dve, s["nm_ready"], HG * (u - 1))
                        if A:
                            wait(dve, s["band_ready"], HG * (u - 1))
                            wait(dve, s["st_full"], STEPS * (u - BODY + 1))
                    part = mpart[:, s2, h, qb, :]
                    dve.wait_ge(s["max_full"], 2 * g + 1)
                    nc.vector.reduce_max(part[:, 0:1], pM[:, 0, :], AX.X).then_inc(s["max_free"], 1)
                    dve.wait_ge(s["max_full"], 2 * g + 2)
                    if A:
                        blocks = window(0, q)
                        far = (4 - len(blocks)) * P
                        lo = (blocks[0] + 1) * P
                        pair = kk // 2
                        wait(dve, s["bias_in"][pair % 4], 16 * (8 * i + pair // 4 + 1))
                        nc.vector.reduce_max(part[:, 1:2], pM[:, 1, 0:far], AX.X)
                        nc.vector.tensor_tensor_reduce(out=near[:, slot, h, qb, lo:lo + len(blocks) * P],
                                                       in0=pM[:, 1, far:HALF],
                                                       in1=bias[:, pair % 4, kk % 2, lo:lo + len(blocks) * P],
                                                       scale=1.0, scalar=-3.0e38, op0=ALU.add, op1=ALU.max,
                                                       accum_out=part[:, 2:3]).then_inc(s["max_free"], 1)
                    else:
                        nc.vector.reduce_max(part[:, 1:2], pM[:, 1, :], AX.X).then_inc(s["max_free"], 1)
                    if qb == 3:
                        dve.wait_ge(s["max_free"], 2 * g + 2)
                        nc.vector.reduce_max(nm[:, s2, h * 4:(h + 1) * 4], mpart[:, s2, h, :, :], AX.X,
                                             negate=True).then_inc(s["nm_ready"], 1)
                    if st == STEPS - 1:
                        dve.wait_ge(s["nm_ready"], HG * (u + 1))
                        wait(dve, s["mt_full"], u)
                        nc.vector.tensor_copy(ms[:, 0, :], nm[:, s2, :]).then_inc(s["ms_a"], 1)
                        dve.wait_ge(s["ms_a"], 3 * u + 1)
                        nc.vector.tensor_tensor(nrest[:, :], nm[:, s2, :], ms[:, 0, :], ALU.subtract).then_inc(s["ms_a"], 1)
                        dve.wait_ge(s["ms_a"], 3 * u + 2)
                        nc.vector.tensor_copy(ms[:, 1, :], nrest[:, :]).then_inc(s["ms_a"], 1)
                        dve.wait_ge(s["ms_a"], 3 * u + 3)
                        nc.vector.tensor_tensor(ms[:, 2, :], nrest[:, :], ms[:, 1, :], ALU.subtract).then_inc(s["ms_ready"], 1)

                steps(dve, [(AHEAD_MAX, 1, 0, maximum)])

            @block.gpsimd
            def _(pool):
                def band(i, kk):
                    u, slot, st = unit_of(i, kk)
                    h, qh = st // 4, slot % 2
                    pool.wait_ge(s["nm_ready"], HG * u + h + 1)
                    edge, lo = (0, P) if qh == 0 else (3, 0)
                    rest = slice(1, 4) if qh == 0 else slice(0, 3)
                    m = nm[:, qh, h * 4:(h + 1) * 4]
                    one = near[:, slot, h, edge, lo:lo + 2 * P]
                    nc.gpsimd.tensor_tensor(one, one, m[:, edge:edge + 1].broadcast_to([P, 2 * P]), ALU.add)
                    three = near[:, slot, h, rest, :]
                    nc.gpsimd.tensor_tensor(three, three, m[:, rest].unsqueeze(2).broadcast_to([P, 3, 3 * P]),
                                            ALU.add).then_inc(s["band_ready"], 1)

                if A:
                    steps(pool, [(AHEAD_MAX, 4, 3, band)])

            @block.scalar
            def _(act):
                def copy_relative(i, kk):
                    g = step_of(i, kk)
                    pair = kk // 2
                    act.wait_ge(s["rel_full"], g + 1)
                    if kk % 2 == 0:
                        wait(act, s["rel_out"][(pair - 2) % 8], 16 * (4 * i + (pair - 2) // 8 + 1))
                    nc.scalar.copy(relsb[:, pair % 2, kk % 2, :], pX[:, 0:REL]).then_inc(s["rel_copied"], 1)

                def copy_max(i, kk):
                    u, slot, _ = unit_of(i, kk)
                    act.wait_ge(s["mt_full"], u + 1)
                    wait(act, s["md_out"], 16 * u)
                    nc.scalar.copy(mT[:, :], pX[0:3 * HG * 4, 0:P]).then_inc(s["mt_copied"], 1)

                def exp(i, kk):
                    g = step_of(i, kk)
                    act.wait_ge(s["st_full"], g + 1)
                    wait(act, s["pv_done"], 32 * i + kk // 2 - 1)
                    nc.scalar.activation(probs[:, kk % 4, :, :], pE[:, kk % 2, :, :], ACT.Exp).then_inc(s["probs"], 1)

                def copy_out(i, kk):
                    u, slot, _ = unit_of(i, kk)
                    act.wait_ge(s["pv_done"], KT * (u + 1))
                    wait(act, s["od_out"][slot % 2], 16 * (2 * i + (kk // STEPS) // 2))
                    nc.scalar.copy(osb[:, slot % 2, :], pO[:, :]).then_inc(s["ot_copied"], 1)

                steps(act, ([(AHEAD_REL, 1, 0, copy_relative)] if A else [])
                      + [(7, STEPS, 0, copy_max), (0, 1, 0, exp), (-STEPS - 2, STEPS, 0, copy_out)])
    give_back()


def chunk_loop(eng, stages, n):
    def body(i):
        for j in range(n):
            for lag, step in stages:
                k = j + lag
                if not isinstance(i, int) or 0 <= n * i + k < 2 * B:
                    step(n * i + k, k % n, k % 2, (n // 2) * i + k // 2, i + k // n)
    body(-1)
    body(0)
    with eng.Fori(1, 2 * B // n - 1) as i:
        body(i)
    body(2 * B // n - 1)


def after_attention(nc, kind, x_dram, X, XN, LG, OD, w, identF):
    A = kind == "A"
    BN = 4
    s, give_back = semaphores(nc, "w_in w_zero w_spread w_turned w_copied ones d_in bounded inverted divided wo_mm"
                   " added stat var dev rec xn_ready passed turned xt_ready routed kept logits summed", o_in=BN, x_in=2)
    with ExitStack() as ctx:
        def sb(name, shape, dt=F32):
            return ctx.enter_context(nc.sbuf_tensor(f"{kind}o_{name}", shape, dt))

        def psum(name, shape):
            return ctx.enter_context(nc.psum_tensor(f"{kind}o_{name}", shape, F32))

        wo = sb("wo", [P, G, D])
        wr = sb("wr", [P, 2, E])
        with ExitStack() as once:
            raw = once.enter_context(nc.sbuf_tensor(f"{kind}o_raw", [P, 2, D], F32))
            spread = once.enter_context(nc.sbuf_tensor(f"{kind}o_spread", [P, 2, H, VW], F32))
            pw = once.enter_context(nc.psum_tensor(f"{kind}o_pw", [P, 2, G, P], F32))
            with nc.Block() as block:
                @block.sync
                def _(sp):
                    sp.dma_start(raw[:, :, :], w["o"].rearrange("(a p) d -> p a d", p=P)).then_inc(s["w_in"], 16)
                    sp.dma_start(wr[:, :, :], w["r"].rearrange("(a p) e -> p a e", p=P)).then_inc(s["w_in"], 16)
                    sp.wait_ge(s["w_in"], 32)

                @block.vector
                def _(dve):
                    nc.vector.memset(spread[:, :, :, :], 0.0).then_inc(s["w_zero"], 1)
                    dve.wait_ge(s["w_zero"], 1)
                    dve.wait_ge(s["w_in"], 32)
                    for a in range(2):
                        last = nc.vector.tensor_copy(spread[:, a, :, 0:HD],
                                                     raw[:, a, :].rearrange("p (h d) -> p h d", d=HD))
                    last.then_inc(s["w_spread"], 1)
                    dve.wait_ge(s["w_turned"], 1)
                    for a in range(2):
                        last = nc.vector.tensor_copy(wo[:, :, a * P:(a + 1) * P], pw[:, a, :, :])
                    last.then_inc(s["w_copied"], 1)

                @block.tensor
                def _(pe):
                    pe.wait_ge(s["w_spread"], 1)
                    for a in range(2):
                        for g in range(G):
                            last = nc.tensor.transpose(pw[:, a, g, :], spread[:, a, g * HG:(g + 1) * HG, :]
                                                       .rearrange("p h c -> p (h c)"), identF[:, :])
                    last.then_inc(s["w_turned"], 1)
        osl, den = sb("osl", [P, BN, G, CHUNK]), sb("den", [P, G, CHUNK])
        xin = sb("xin", [P, 2, CT, D]) if A else None
        stats, mv, rstd = sb("stats", [P, CT, 6]), sb("mv", [P, CT, 2]), sb("rstd", [P, 3, CT])
        xn = sb("xn", [P, CT, D])
        xT = sb("xT", [P, 2, CHUNK])
        borow, ones = sb("borow", [1, D]), sb("ones", [1, P])
        pW = psum("pW", [P, CT, D])
        pT = psum("pT", [P, 2, CHUNK])
        pL = psum("pL", [P, CT, E])

        def tiles(c):
            return bass.ds(c * CT, CT)

        with nc.Block() as block:
            @block.sync
            def _(sp):
                if not A:
                    sp.dma_start(borow[:, :], w["bo"].rearrange("(a n) -> a n", a=1)).then_inc(s["w_in"], 16)

                def load(c, slot, half, b, body):
                    wait_apart(sp, s, s["wo_mm"], c - BN + 1)
                    sp.dma_start(osl[:, slot, :, :],
                                 OD.rearrange("i s p t -> (i s) p t").rearrange("(b g q) p t -> b q p g t", g=G, q=2)
                                 [b, half]).then_inc(s["o_in"][slot], 16)
                    wait_apart(sp, s, s["divided"], c)
                    sp.dma_start(den[0:P - HD, :, :],
                                 OD.rearrange("i s p t -> (i s) p t").rearrange("(b g q) p t -> b q p g t", g=G, q=2)
                                 [b, half, HD:P]).then_inc(s["d_in"], 16)

                def load_x(c, slot, half, b, body):
                    wait_apart(sp, s, s["added"], c - 1)
                    sp.dma_start(xin[:, half, :, :], x_dram[b, half * HALF:(half + 1) * HALF, :]
                                 .rearrange("(t p) d -> p t d", p=P)).then_inc(s["x_in"][half], 16)

                sp.wait_ge(s["ones"], 1)
                chunk_loop(sp, [(3, load)] + ([(1, load_x)] if A else []), BN)

            @block.vector
            def _(dve):
                nc.vector.memset(ones[:, :], 1.0)
                nc.vector.memset(den[P - 32:P, :, :], 1.0).then_inc(s["ones"], 1)

                def divide(c, slot, half, b, body):
                    dve.wait_ge(s["o_in"][slot], 16 * (body + 1))
                    dve.wait_ge(s["d_in"], 16 * (c + 1))
                    nc.vector.tensor_scalar(den[:, :, :], den[:, :, :], 0.5, None, ALU.max).then_inc(s["bounded"], 1)
                    dve.wait_ge(s["bounded"], c + 1)
                    nc.vector.reciprocal(den[:, :, :], den[:, :, :]).then_inc(s["inverted"], 1)
                    dve.wait_ge(s["inverted"], c + 1)
                    nc.vector.tensor_tensor(osl[:, slot, :, :], osl[:, slot, :, :], den[:, :, :],
                                            ALU.mult).then_inc(s["divided"], 1)

                def add(c, slot, half, b, body):
                    dve.wait_ge(s["wo_mm"], c + 1)
                    if A:
                        dve.wait_ge(s["x_in"][half], 16 * (b + 1))
                    nc.vector.tensor_tensor(X[:, tiles(c), :], xin[:, half, :, :] if A else X[:, tiles(c), :],
                                            pW[:, :, :], ALU.add).then_inc(s["added"], 1)
                    dve.wait_ge(s["added"], c + 1)
                    wait(dve, s["turned"], c)
                    wait(dve, s["kept"], c)
                    wait_apart(dve, s, s["summed"], c)
                    normalize_steps(nc, s, X[:, tiles(c), :], stats, mv, rstd, xn, c)

                chunk_loop(dve, [(2, divide), (0, add)], BN)

            @block.gpsimd
            def _(pool):
                def add_normalized(c, slot, half, b, body):
                    pool.wait_ge(s["xn_ready"], c + 1)
                    nc.gpsimd.tensor_tensor(X[:, tiles(c), :], X[:, tiles(c), :], xn[:, :, :], ALU.add).then_inc(s["summed"], 1)

                chunk_loop(pool, [(0, add_normalized)], BN)

            @block.scalar
            def _(act):
                def root(c, slot, half, b, body):
                    act.wait_ge(s["var"], c + 1)
                    nc.scalar.sqrt(rstd[:, 1, :], rstd[:, 0, :]).then_inc(s["dev"], 1)

                def copies(c, slot, half, b, body):
                    act.wait_ge(s["turned"], c + 1)
                    wait(act, s["routed"], c)
                    nc.scalar.copy(xT[:, :, :], pT[:, :, :]).then_inc(s["xt_ready"], 1)
                    nc.scalar.copy(XN[:, tiles(c), :], xn[:, :, :]).then_inc(s["kept"], 1)
                    act.wait_ge(s["routed"], c + 1)
                    nc.scalar.copy(LG[:, tiles(c), :], pL[:, :, :]).then_inc(s["logits"], 1)

                chunk_loop(act, [(0, root), (0, copies)], BN)

            @block.tensor
            def _(pe):
                if not A:
                    pe.wait_ge(s["w_in"], 48)
                pe.wait_ge(s["ones"], 1)

                def project_out(c, slot, half, b, body):
                    pe.wait_ge(s["divided"], c + 1)
                    wait(pe, s["added"], c)
                    for t in range(CT):
                        for g in range(G):
                            last = nc.tensor.matmul(pW[:, t, :], osl[:, slot, g, t * P:(t + 1) * P], wo[:, g, :],
                                                    start=(g == 0), stop=(A and g == G - 1))
                        if not A:
                            last = nc.tensor.matmul(pW[:, t, :], ones[0:1, :], borow[0:1, :], start=False, stop=True)
                    last.then_inc(s["wo_mm"], 1)

                def turn(c, slot, half, b, body):
                    pe.wait_ge(s["xn_ready"], c + 1)
                    wait(pe, s["xt_ready"], c)
                    for t in range(CT):
                        for d in range(2):
                            last = nc.tensor.transpose(pT[:, d, t * P:(t + 1) * P], xn[:, t, d * P:(d + 1) * P],
                                                       identF[:, :])
                    last.then_inc(s["turned"], 1)

                def route(c, slot, half, b, body):
                    pe.wait_ge(s["xt_ready"], c + 1)
                    wait(pe, s["logits"], c)
                    for t in range(CT):
                        for d in range(2):
                            last = nc.tensor.matmul(pL[:, t, :], xT[:, d, t * P:(t + 1) * P], wr[:, d, :],
                                                    start=(d == 0), stop=(d == 1))
                    last.then_inc(s["routed"], 1)

                chunk_loop(pe, [(1, project_out), (0, turn), (0, route)], BN)
    give_back()


def dispatch(nc, name, XN, LG, BUF, gate, gidx, moved, before):
    s, give_back = semaphores(nc, "mask iota v a oh cum")
    with ExitStack() as ctx:
        def sb(label, shape, dt=F32):
            return ctx.enter_context(nc.sbuf_tensor(f"{name}_{label}", shape, dt))

        upper = sb("upper", [P, P], BF16)
        allone = sb("allone", [P, P], BF16)
        ei = sb("ei", [P, E])
        eint = sb("eint", [P, E], I32)
        w1, w2, w3 = (sb(f"w{k}", [P, NT * E]) for k in range(3))
        onehot = sb("onehot", [P, NT * E], BF16)
        small = sb("small", [P, 8, NT])
        sidx = sb("sidx", [P, NT], U32)
        pC = ctx.enter_context(nc.psum_tensor(f"{name}_pC", [P, NT * E], F32))
        pS = ctx.enter_context(nc.psum_tensor(f"{name}_pS", [P, NT * E], F32))

        def te(ap):
            return ap.rearrange("p (t e) -> p t e", e=E)

        def over_e(ap):
            return ap.unsqueeze(2).broadcast_to([P, NT, E])

        with nc.Block() as block:
            @block.gpsimd
            def _(pool):
                nc.gpsimd.memset(upper[:, :], 1.0)
                nc.gpsimd.memset(allone[:, :], 1.0).then_inc(s["mask"], 1)
                pool.wait_ge(s["mask"], 1)
                nc.gpsimd.affine_select(out=upper[:, :], in_=upper[:, :], compare_op=ALU.is_ge, fill=0.0,
                                        base=0, pattern=[[1, P]], channel_multiplier=-1).then_inc(s["mask"], 1)
                nc.gpsimd.iota(eint[:, :], [[1, E]], base=-E, channel_multiplier=0).then_inc(s["iota"], 1)

            @block.scalar
            def _(act):
                act.wait_ge(s["a"], 1)
                nc.scalar.activation(w2[:, :], w1[:, :], ACT.Exp).then_inc(s["a"], 1)

            @block.tensor
            def _(pe):
                pe.wait_ge(s["mask"], 2)
                pe.wait_ge(s["oh"], 1)
                for k in range(4):
                    cols = slice(k * 512, (k + 1) * 512)
                    nc.tensor.matmul(pC[:, cols], upper[:, :], onehot[:, cols], start=True, stop=True)
                    last = nc.tensor.matmul(pS[:, cols], allone[:, :], onehot[:, cols], start=True, stop=True)
                last.then_inc(s["cum"], 1)

            @block.vector
            def _(dve):
                done = [0]

                def link(ins):
                    done[0] += 1
                    ins.then_inc(s["v"], 1)
                    dve.wait_ge(s["v"], done[0])

                top, best, first, total, pos, acc, slot, t2 = (small[:, k, :] for k in range(8))
                lg = LG[:, :, :]
                dve.wait_ge(s["iota"], 1)
                link(nc.vector.tensor_copy(ei[:, :], eint[:, :]))
                link(nc.vector.reduce_max(top, lg, AX.X))
                nc.vector.tensor_tensor(te(w1[:, :]), lg, over_e(top), ALU.subtract).then_inc(s["a"], 1)
                dve.wait_ge(s["a"], 2)
                eis = ei[:, :].unsqueeze(1).broadcast_to([P, NT, E])
                link(nc.vector.tensor_scalar(w3[:, :], w1[:, :], 0.0, None, ALU.is_ge))
                link(nc.vector.tensor_tensor(te(w3[:, :]), te(w3[:, :]), eis, ALU.mult))
                link(nc.vector.tensor_reduce(first, te(w3[:, :]), AX.X, ALU.min))
                nc.vector.tensor_tensor(te(onehot[:, :]), eis, over_e(first), ALU.is_equal).then_inc(s["oh"], 1)
                link(nc.vector.reduce_sum(total, te(w2[:, :]), AX.X))
                link(nc.vector.reciprocal(gate[:, :], total))
                dve.wait_ge(s["cum"], 1)
                link(nc.vector.memset(w1[:, :], 1.0))
                link(nc.vector.memset(w1[:, :].rearrange("p (e t) -> p e t", t=NT)[:, :, 0:1], 0.0))
                link(nc.vector.tensor_copy(w2[:, :].rearrange("p (e t) -> p e t", t=NT),
                                           pS[:, :].rearrange("p (t e) -> p e t", e=E)))
                link(nc.vector.tensor_tensor_scan(w3[:, :], w1[:, :], w2[:, :], 0.0, ALU.mult, ALU.add))
                link(nc.vector.tensor_tensor(w3[:, :], w3[:, :], w2[:, :], ALU.subtract))
                link(nc.vector.tensor_tensor(te(w1[:, :]), w3[:, :].rearrange("p (e t) -> p t e", t=NT),
                                             te(pC[:, :]), ALU.add))
                link(nc.vector.tensor_tensor(w2[:, :], w1[:, :], onehot[:, :], ALU.mult))
                link(nc.vector.reduce_sum(pos, te(w2[:, :]), AX.X))
                link(nc.vector.tensor_scalar(acc, pos, float(CAP), None, ALU.is_le))
                link(nc.vector.tensor_scalar(slot, first, float(CAP), float(E * CAP - 1), ALU.mult, ALU.add))
                link(nc.vector.tensor_tensor(slot, slot, pos, ALU.add))
                link(nc.vector.tensor_scalar(t2, acc, -65536.0, 65536.0, ALU.mult, ALU.add))
                link(nc.vector.tensor_tensor(slot, slot, t2, ALU.add))
                link(nc.vector.tensor_copy(sidx[:, :], slot))
                link(nc.vector.tensor_scalar(t2, slot, float(E * CAP - 1), None, ALU.min))
                link(nc.vector.tensor_copy(gidx[:, :], t2))
                link(nc.vector.tensor_tensor(gate[:, :], gate[:, :], acc, ALU.mult))

        with nc.Block() as block:
            @block.gpsimd
            def _(pool):
                for t in range(NT):
                    nc.gpsimd.indirect_dma_start(
                        out=BUF, out_offset=bass.IndirectOffsetOnAxis(ap=sidx[:, t:t + 1], axis=0),
                        in_=XN[:, t, :], in_offset=None, bounds_check=E * CAP - 1,
                        oob_is_err=False).then_inc(moved[t % MOVES], 16)
                for k in range(MOVES):
                    pool.wait_ge(moved[k], before + 16 * (NT // MOVES))
    give_back()


def experts(nc, name, w, BUF, YD, identF):
    R = 4
    FULL = CAP // P
    LASTR = CAP - FULL * P
    rows_of = [P] * FULL + ([LASTR] if LASTR else [])
    TILES = len(rows_of)
    s, give_back = semaphores(nc, "x_turned xt_ready gu_mm silu hidden down_mm y_ready passed", in_x=R, in_w=R, y_out=2)
    with ExitStack() as ctx:
        def sb(label, shape, dt=F32):
            return ctx.enter_context(nc.sbuf_tensor(f"{name}_{label}", shape, dt))

        xe = sb("xe", [P, R, TILES, D])
        wg, wu, wd = (sb(f"w{k}", [P, R, 2, D]) for k in "gud")
        xT = sb("xT", [P, 2, 2, CAP])
        sg = sb("sg", [P, 2, CAP])
        hid = sb("hid", [P, 2, 2, CAP])
        y = sb("y", [P, 2, TILES, D])

        def psum(label, shape):
            return ctx.enter_context(nc.psum_tensor(f"{name}_{label}", shape, F32))

        pT, pG, pU = psum("pT", [P, 2, 512]), psum("pG", [P, 2, 512]), psum("pU", [P, 2, 512])
        pY = psum("pY", [P, 4, D])

        def expert_loop(eng, stages):
            def body(i):
                for j in range(R):
                    for lag, step in stages:
                        k = j + lag
                        if not isinstance(i, int) or 0 <= R * i + k < E:
                            step(R * i + k, k % R, i + k // R)
            body(-1)
            body(0)
            with eng.Fori(1, E // R - 1) as i:
                body(i)
            body(E // R - 1)
            body(E // R)

        with nc.Block() as block:
            @block.sync
            def _(sp):
                def load(e, slot, body):
                    wait_apart(sp, s, s["x_turned"], e - R + 1)
                    src = BUF.rearrange("(e c) d -> e c d", c=CAP)
                    sp.dma_start(xe[:, slot, 0:FULL, :],
                                 src[e, 0:FULL * P, :].rearrange("(t p) d -> p t d", p=P)).then_inc(s["in_x"][slot], 16)
                    if LASTR:
                        sp.dma_start(xe[0:LASTR, slot, FULL, :], src[e, FULL * P:CAP, :]).then_inc(s["in_x"][slot], 16)
                    wait_apart(sp, s, s["down_mm"], e - R + 1)
                    for dst, weights in ((wg, w["gate"]), (wu, w["up"]), (wd, w["down"])):
                        sp.dma_start(dst[:, slot, :, :],
                                     weights[e].rearrange("(a p) f -> p a f", p=P)).then_inc(s["in_w"][slot], 16)

                def store(e, slot, body):
                    wait_apart(sp, s, s["y_ready"], e + 1)
                    dst = YD.rearrange("(e c) d -> e c d", c=CAP)
                    sp.dma_start(dst[e, 0:FULL * P, :].rearrange("(t p) d -> p t d", p=P),
                                 y[:, slot % 2, 0:FULL, :]).then_inc(s["y_out"][slot % 2], 16)
                    if LASTR:
                        sp.dma_start(dst[e, FULL * P:CAP, :], y[0:LASTR, slot % 2, FULL, :]).then_inc(s["y_out"][slot % 2], 16)

                expert_loop(sp, [(3, load), (-1, store)])
                for k in range(2):
                    sp.wait_ge(s["y_out"][k], 16 * 2 * E // 2)

            @block.tensor
            def _(pe):
                def turn(e, slot, body):
                    pe.wait_ge(s["in_x"][slot], 32 * (body + 1))
                    wait(pe, s["xt_ready"], e)
                    at = 0
                    for t, rows in enumerate(rows_of):
                        for d in range(2):
                            last = nc.tensor.transpose(pT[:, d, at:at + rows], xe[0:rows, slot, t, d * P:(d + 1) * P],
                                                       identF[0:rows, 0:rows])
                        at += rows
                    last.then_inc(s["x_turned"], 1)

                def gate_up(e, slot, body):
                    pe.wait_ge(s["in_w"][slot], 48 * (body + 1))
                    pe.wait_ge(s["xt_ready"], e + 1)
                    wait(pe, s["hidden"], e)
                    for out, weights in ((pG, wg), (pU, wu)):
                        for f in range(2):
                            for d in range(2):
                                last = nc.tensor.matmul(out[:, f, 0:CAP], weights[:, slot, d, f * P:(f + 1) * P],
                                                        xT[:, slot % 2, d, :], start=(d == 0), stop=(d == 1))
                        last.then_inc(s["gu_mm"], 1)

                def down(e, slot, body):
                    pe.wait_ge(s["hidden"], e + 1)
                    wait(pe, s["y_ready"], e)
                    at = 0
                    for t, rows in enumerate(rows_of):
                        for f in range(2):
                            last = nc.tensor.matmul(pY[0:rows, t, :], hid[:, slot % 2, f, at:at + rows],
                                                    wd[:, slot, f, :], start=(f == 0), stop=(f == 1))
                        at += rows
                    last.then_inc(s["down_mm"], 1)

                expert_loop(pe, [(0, gate_up), (-1, down), (1, turn)])

            @block.scalar
            def _(act):
                def copy(e, slot, body):
                    act.wait_ge(s["x_turned"], e + 1)
                    wait(act, s["gu_mm"], 2 * (e - 1))
                    nc.scalar.copy(xT[:, slot % 2, :, :], pT[:, :, 0:CAP]).then_inc(s["xt_ready"], 1)

                def silu(e, slot, body):
                    act.wait_ge(s["gu_mm"], 2 * e + 1)
                    wait(act, s["hidden"], e)
                    nc.scalar.activation(sg[:, :, :], pG[:, :, 0:CAP], ACT.Silu).then_inc(s["silu"], 1)

                expert_loop(act, [(0, silu), (1, copy)])

            @block.vector
            def _(dve):
                def multiply(e, slot, body):
                    dve.wait_ge(s["silu"], e + 1)
                    dve.wait_ge(s["gu_mm"], 2 * e + 2)
                    wait(dve, s["down_mm"], e - 1)
                    nc.vector.tensor_tensor(hid[:, slot % 2, :, :], sg[:, :, :], pU[:, :, 0:CAP],
                                            ALU.mult).then_inc(s["hidden"], 1)

                def copy(e, slot, body):
                    dve.wait_ge(s["down_mm"], e + 1)
                    wait(dve, s["y_out"][slot % 2], 32 * (2 * body + slot // 2))
                    nc.vector.tensor_copy(y[:, slot % 2, 0:FULL, :], pY[:, 0:FULL, :])
                    nc.vector.tensor_copy(y[0:LASTR, slot % 2, FULL, :], pY[0:LASTR, FULL, :]).then_inc(s["y_ready"], 1)

                expert_loop(dve, [(0, multiply), (-1, copy)])
    give_back()


def combine(nc, name, X, YD, gate, gidx, out, moved, before):
    R = MOVES
    s, give_back = semaphores(nc, "combined", out_sent=4)
    with ExitStack() as ctx:
        yt = ctx.enter_context(nc.sbuf_tensor(f"{name}_yt", [P, R, D], F32))
        with nc.Block() as block:
            @block.gpsimd
            def _(pool):
                for t in range(NT):
                    wait(pool, s["combined"], t - R + 1)
                    nc.gpsimd.indirect_dma_start(
                        out=yt[:, t % R, :], out_offset=None, in_=YD,
                        in_offset=bass.IndirectOffsetOnAxis(ap=gidx[:, t:t + 1], axis=0),
                        bounds_check=E * CAP - 1, oob_is_err=False).then_inc(moved[t % MOVES], 16)

            @block.vector
            def _(dve):
                for t in range(NT):
                    dve.wait_ge(moved[t % MOVES], before + 16 * (t // MOVES + 1))
                    nc.vector.scalar_tensor_tensor(out=X[:, t, :], in0=yt[:, t % R, :], scalar=gate[:, t:t + 1],
                                                   in1=X[:, t, :], op0=ALU.mult, op1=ALU.add).then_inc(s["combined"], 1)

            @block.sync
            def _(sp):
                if out is not None:
                    rows = out.rearrange("b (t p) d -> p (b t) d", p=P)
                    for c in range(2 * B):
                        sp.wait_ge(s["combined"], CT * (c + 1))
                        sp.dma_start(rows[:, c * CT:(c + 1) * CT, :],
                                     X[:, c * CT:(c + 1) * CT, :]).then_inc(s["out_sent"][c % 4], 16)
                    for k in range(4):
                        sp.wait_ge(s["out_sent"][k], 16 * (2 * B // 4))
    give_back()


def block_kernel(nc, x, a_wq, a_wk, a_wv, a_wo, emb, b_wq, b_bq, b_wk, b_bk, b_wv, b_bv, b_wo, b_bo,
                 w_router, w_gate, w_up, w_down, out):
    Q = nc.dram_tensor("q_parts", (2 * B, 3, P, T), BF16).ap()
    KA = nc.dram_tensor("ka_parts", (2, 2 * B, 3, 32, T), BF16).ap()
    KB = nc.dram_tensor("kb_parts", (2 * B, 3, P, T), BF16).ap()
    VA = nc.dram_tensor("va", (2 * B, P, 2, KT, VW), F32).ap()
    VB = nc.dram_tensor("vb", (2 * B, P, 2, KT, HG * VW), F32).ap()
    OD = nc.dram_tensor("attended", (2 * B, BODY, P, HALF), F32).ap()
    RR = nc.dram_tensor("relative_rows", (2, STEPS, P, RELROW), F32).ap()
    MD = nc.dram_tensor("maxima", (BODY, 3 * HG * 4, P), BF16).ap()
    BUF = nc.dram_tensor("expert_in", (E * CAP, D), F32).ap()
    YD = nc.dram_tensor("expert_out", (E * CAP, D), F32).ap()
    with ExitStack() as ctx:
        def sb(name, shape, dt=F32):
            return ctx.enter_context(nc.sbuf_tensor(name, shape, dt))

        identF, identB = sb("identF", [P, P]), sb("identB", [P, P], BF16)
        gate, gidx = sb("gate", [P, NT]), sb("gidx", [P, NT], U32)
        s, give_back = semaphores(nc, "id_zero id_one z_set z_out")
        with nc.sbuf_tensor("zeros", [P, 2 * CAP * E * D // P // 16], F32) as zeros:
            with nc.Block() as block:
                @block.gpsimd
                def _(pool):
                    nc.gpsimd.memset(identF[:, :], 0.0).then_inc(s["id_zero"], 1)
                    pool.wait_ge(s["id_zero"], 1)
                    nc.gpsimd.affine_select(out=identF[:, :], in_=identF[:, :], compare_op=ALU.not_equal,
                                            fill=1.0, base=0, pattern=[[-1, P]],
                                            channel_multiplier=1).then_inc(s["id_one"], 1)

                @block.vector
                def _(dve):
                    nc.vector.memset(zeros[:, :], 0.0).then_inc(s["z_set"], 1)
                    dve.wait_ge(s["id_one"], 1)
                    nc.vector.tensor_copy(identB[:, :], identF[:, :])

                @block.sync
                def _(sp):
                    sp.wait_ge(s["z_set"], 1)
                    flat = BUF.rearrange("(n p r) d -> n p (r d)", n=8, p=P)
                    for n in range(8):
                        sp.dma_start(flat[n], zeros[:, :]).then_inc(s["z_out"], 16)
                    sp.wait_ge(s["z_out"], 16 * 8)
        give_back()
        wa = {"q": a_wq, "k": a_wk, "v": a_wv, "E": emb, "o": a_wo, "r": w_router}
        wb = {"q": b_wq, "k": b_wk, "v": b_wv, "bq": b_bq, "bk": b_bk, "bv": b_bv, "o": b_wo, "bo": b_bo,
              "r": w_router}
        we = {"gate": w_gate, "up": w_up, "down": w_down}

        project(nc, "A", x, None, wa, Q, KA, VA, identF)
        attend(nc, "A", Q, KA, VA, OD, emb, RR, MD, identF, identB)
        X = sb("X", [P, NT, D])
        moved = [ctx.enter_context(nc.semaphore(f"moved{k}")) for k in range(MOVES)]
        for kind, w, before in (("A", wa, 0), ("B", wb, 2 * 16 * (NT // MOVES))):
            if kind == "B":
                project(nc, "B", None, X, wb, Q, KB, VB, identF)
                attend(nc, "B", Q, KB, VB, OD, None, None, MD, identF, identB)
            with nc.sbuf_tensor(f"XN_{kind}", [P, NT, D], F32) as XN, \
                    nc.sbuf_tensor(f"LG_{kind}", [P, NT, E], F32) as LG:
                after_attention(nc, kind, x, X, XN, LG, OD, w, identF)
                dispatch(nc, f"r{kind}", XN, LG, BUF, gate, gidx, moved, before)
            experts(nc, f"e{kind}", we, BUF, YD, identF)
            combine(nc, f"c{kind}", X, YD, gate, gidx, out if kind == "B" else None, moved,
                    before + 16 * (NT // MOVES))


_INS = ["L0_attn_a_x", "L0_attn_a_Wq", "L0_attn_a_Wk", "L0_attn_a_Wv", "L0_attn_a_Wo", "L0_attn_a_E",
        "L0_attn_b_wq", "L0_attn_b_bq", "L0_attn_b_wk", "L0_attn_b_bk", "L0_attn_b_wv", "L0_attn_b_bv",
        "L0_attn_b_wo", "L0_attn_b_bo", "L0_ffn_w_router", "L0_ffn_w_gate", "L0_ffn_w_up", "L0_ffn_w_down"]
_OUTS = [((8, 1024, 256), "float32")]


def kernel(**inputs):
    import numpy as _np
    import concourse.bacc as _bacc
    from concourse import mybir as _mybir
    from concourse.bass_utils import run_bass_kernel_spmd as _run

    nc = _bacc.Bacc("TRN2", target_bir_lowering=False, num_devices=1)
    arrays, args = {}, []
    for name in _INS:
        a = _np.ascontiguousarray(inputs[name][::-1] if name == "L0_attn_a_E" else inputs[name])
        arrays[f"in_{name}_dram"] = a
        args.append(nc.dram_tensor(f"in_{name}_dram", a.shape, _mybir.dt.from_np(a.dtype), kind="ExternalInput").ap())
    for i, (shape, dtype) in enumerate(_OUTS):
        dt = _mybir.dt.from_np(_np.dtype(dtype))
        args.append(nc.dram_tensor(f"out_{i}_dram", shape, dt, kind="ExternalOutput").ap())
    block_kernel(nc, *args)
    r = _run(nc, [arrays], core_ids=[0])
    return r.results[0]["out_0_dram"]
```

```python
from contextlib import ExitStack

import concourse.bass as bass
from concourse import mybir

F32 = mybir.dt.float32
BF16 = mybir.dt.bfloat16
I32 = mybir.dt.int32
U32 = mybir.dt.uint32
ALU = mybir.AluOpType
ACT = mybir.ActivationFunctionType
AX = mybir.AxisListType

P = 128
B, T, D = 8, 1024, 256
N = B * T
NT = N // P
H, HD = 16, 16
G = 4
HG = H // G
MAX_POS = 128
NREL = 2 * MAX_POS - 1
EPS = 1e-5
E = 32
CAP = 320
CHUNK = 512
CT = CHUNK // P
KT = T // P
SPLITS = 6
KR = SPLITS * HD
KM = KR + 3
VW = 2 * HD
REL = NREL - 1 + P
RELROW = 512
UNITS = B * G * 2
HALF = T // 2
STEPS = 16
BODY = 4
MOVES = 8


def semaphores(nc, names, **rings):
    stack, made = ExitStack(), {}
    for name in names.split():
        made[name] = stack.enter_context(nc.semaphore(name))
    every = list(made.values())
    for name, n in rings.items():
        made[name] = [stack.enter_context(nc.semaphore(f"{name}{k}")) for k in range(n)]
        every += made[name]

    def give_back():
        with nc.Block() as block:
            @block.sync
            def _(sp):
                for handle in every:
                    sp.sem_clear(handle)
        stack.close()

    return made, give_back


def wait(eng, sem, count):
    if not isinstance(count, int) or count > 0:
        eng.wait_ge(sem, count)


def wait_apart(eng, s, sem, count):
    wait(eng, sem, count)
    if not isinstance(count, int):
        eng.sem_inc(s["passed"], 1)


def load_transposed(nc, kind, weights, ident):
    s, give_back = semaphores(nc, "w_read w_turned w_copied")
    with ExitStack() as ctx:
        raws = [ctx.enter_context(nc.sbuf_tensor(f"{kind}_raw_{k}", [P, 2, D], F32)) for k in range(len(weights))]
        pt = ctx.enter_context(nc.psum_tensor(f"{kind}_w_pt", [P, 2, 4, P], F32))
        jobs = [(k, a) for k, (w, _, _) in enumerate(weights) for a in range(-(-w.shape[0] // P))]
        with nc.Block() as block:
            @block.sync
            def _(sp):
                for k, (w, _, _) in enumerate(weights):
                    rows = min(P, w.shape[0])
                    sp.dma_start(raws[k][0:rows, 0:w.shape[0] // rows, :],
                                 w.rearrange("(a p) d -> p a d", p=rows)).then_inc(s["w_read"], 16)

            @block.tensor
            def _(pe):
                pe.wait_ge(s["w_read"], 16 * len(weights))
                for n, (k, a) in enumerate(jobs):
                    rows = min(P, weights[k][0].shape[0])
                    wait(pe, s["w_copied"], n - 1)
                    for half in range(2):
                        last = nc.tensor.transpose(pt[:, n % 2, half, 0:rows],
                                                   raws[k][0:rows, a, half * P:(half + 1) * P],
                                                   ident[0:rows, 0:rows])
                    last.then_inc(s["w_turned"], 1)

            @block.vector
            def _(dve):
                for n, (k, a) in enumerate(jobs):
                    w, out, view = weights[k]
                    rows = min(P, w.shape[0])
                    dve.wait_ge(s["w_turned"], n + 1)
                    for half in range(2):
                        dst, src = view(out[:, half, a * rows:(a + 1) * rows], pt[:, n % 2, half, 0:rows])
                        last = nc.vector.tensor_copy(dst, src)
                    last.then_inc(s["w_copied"], 1)
    give_back()


def as_is(dst, src):
    return dst, src


def by_width(dst, src):
    return dst.rearrange("p (d h) -> p d h", d=HD), src.rearrange("p (h d) -> p d h", d=HD)


def by_half_width(dst, src):
    return (dst.rearrange("p (a d j) -> p a d j", a=2, d=HD),
            src.rearrange("p (a j d) -> p a d j", a=2, d=HD))


def normalize_steps(nc, s, xc, stats, mv, rstd, xn, k):
    for t in range(CT):
        last = nc.vector.bn_stats(stats[:, t, :], xc[:, t, :])
    last.then_inc(s["stat"], 1)
    wait_apart(nc.vector, s, s["stat"], 2 * k + 1)
    for t in range(CT):
        last = nc.vector.bn_aggr(mv[:, t, :], stats[:, t, :])
    last.then_inc(s["stat"], 1)
    nc.vector.wait_ge(s["stat"], 2 * k + 2)
    nc.vector.tensor_scalar(rstd[:, 0, :], mv[:, :, 1], EPS, None, ALU.add).then_inc(s["var"], 1)
    nc.vector.wait_ge(s["dev"], k + 1)
    nc.vector.reciprocal(rstd[:, 2, :], rstd[:, 1, :]).then_inc(s["rec"], 1)
    nc.vector.wait_ge(s["rec"], k + 1)
    for t in range(CT):
        last = nc.vector.tensor_scalar(xn[:, t, :], xc[:, t, :], mv[:, t, 0:1], rstd[:, 2, t:t + 1],
                                       ALU.subtract, ALU.mult)
    last.then_inc(s["xn_ready"], 1)


def project(nc, kind, x_dram, X, w, Q, K, V, ident, clear=None):
    A = kind == "A"
    heads = G if A else H
    nv = heads * HD
    cols = V.shape[4]
    s, give_back = semaphores(nc, "w_in bias_in stat var dev rec xn_ready turned xt_ready mm v_mm q1 qf r1 q2 q3"
                   " v_ready bias_row bias_mm bias_col ones passed", x_in=2, parts_out=4, v_out=2)
    with ExitStack() as ctx:
        def sb(name, shape, dt=F32):
            return ctx.enter_context(nc.sbuf_tensor(f"{kind}p_{name}", shape, dt))

        def psum(name, shape):
            return ctx.enter_context(nc.psum_tensor(f"{kind}p_{name}", shape, F32))

        nk = 64 if A else D
        wqT, wkT, wvT = sb("wqT", [P, 2, D]), sb("wkT", [P, 2, nk]), sb("wvT", [P, 2, nv])
        load_transposed(nc, kind, [(w["q"], wqT, by_width), (w["k"], wkT, by_half_width if A else by_width),
                             (w["v"], wvT, as_is)], ident)
        if A:
            tensors = [(0, P, 0.25, None), (1, P, 0.25, None), (2, nk, 1.0, 0), (2, nk, 1.0, 1)]
        else:
            tensors = [(0, P, 0.25, 0), (1, P, 0.25, 1), (2, P, 1.0, 2), (3, P, 1.0, 3)]
        products = [(wqT, 0, P), (wqT, P, P)] + ([(wkT, 0, nk)] if A else [(wkT, 0, P), (wkT, P, P)])
        xin = sb("xin", [P, 2, CT, D]) if A else None
        stats, mv, rstd = sb("stats", [P, CT, 6]), sb("mv", [P, CT, 2]), sb("rstd", [P, 3, CT])
        xn = sb("xn", [P, 2, CT, D])
        xT = sb("xT", [P, 2, 2, CHUNK])
        parts = sb("parts", [P, 4, 3, CHUNK], BF16)
        full, rest = sb("full", [P, 4, CHUNK]), sb("rest", [P, 4, CHUNK])
        vs = sb("vs", [P, 2, CT, heads, VW])
        brow, bprm, bcol = sb("brow", [1, 2, D]), sb("bprm", [1, 4, P]), sb("bcol", [P, 4])
        one = sb("one", [1, 1])
        bv = sb("bv", [P, nv])
        pT = psum("pT", [P, 2, CHUNK])
        pR = [psum(f"pR{k}", [P, CHUNK]) for k in range(len(products))]
        pV = psum("pV", [P, CT, nv])

        with nc.Block() as block:
            @block.sync
            def _(sp):
                if A:
                    sp.dma_start(brow[0:1, 0, 0:HD], w["E"][0:1, :]).then_inc(s["bias_in"], 16)
                    sp.dma_start(brow[0:1, 1, 0:HD], w["E"][NREL - 1:NREL, :]).then_inc(s["bias_in"], 16)
                else:
                    sp.dma_start(brow[0:1, 0, :], w["bq"].rearrange("(a n) -> a n", a=1)).then_inc(s["bias_in"], 16)
                    sp.dma_start(brow[0:1, 1, :], w["bk"].rearrange("(a n) -> a n", a=1)).then_inc(s["bias_in"], 16)
                    sp.dma_start(bv[:, :], w["bv"].rearrange("(a n) -> a n", a=1).broadcast_to([P, nv])).then_inc(s["w_in"], 16)
                    sp.wait_ge(s["w_in"], 16)

            @block.vector
            def _(dve):
                nc.vector.memset(one[:, :], 1.0)
                nc.vector.memset(vs[:, :, :, :, :], 1.0).then_inc(s["ones"], 1)
                dve.wait_ge(s["bias_in"], 32)
                for k in range(2 if A else 4):
                    if A:
                        dst = bprm[0:1, k, 0:nk].rearrange("o (a d j) -> o a d j", a=2, d=HD)
                        src = brow[0:1, k, 0:HD].unsqueeze(1).unsqueeze(3).broadcast_to([1, 2, HD, 2])
                    else:
                        dst = bprm[0:1, k, :].rearrange("o (d h) -> o d h", d=HD)
                        src = brow[0:1, k // 2, (k % 2) * P:(k % 2 + 1) * P].rearrange("o (h d) -> o d h", d=HD)
                    last = nc.vector.tensor_scalar(dst, src, 1.0 if A or k > 1 else 0.25, None, ALU.mult)
                last.then_inc(s["bias_row"], 1)
                dve.wait_ge(s["bias_mm"], 1)
                rows = nk if A else P
                nc.vector.tensor_copy(bcol[0:rows, 0:2 if A else 4], pT[0:rows, 0, 0:2 if A else 4]).then_inc(s["bias_col"], 1)

            @block.tensor
            def _(pe):
                pe.wait_ge(s["bias_row"], 1)
                rows = nk if A else P
                for k in range(2 if A else 4):
                    last = nc.tensor.matmul(pT[0:rows, 0, k:k + 1], bprm[0:1, k, 0:rows], one[0:1, 0:1],
                                            start=True, stop=True)
                last.then_inc(s["bias_mm"], 1)

        M = len(tensors)

        def part(m, rows, k):
            return parts[0:rows, m, k if m < 2 else 2 - k, :]


        def chunks(eng, stages):
            def body(i):
                for j in (0, 1):
                    for lag, step in stages:
                        k = j + lag
                        if not isinstance(i, int) or 0 <= 2 * i + k < 2 * B:
                            step(2 * i + k, k % 2, i + k // 2)
            body(-1)
            body(0)
            with eng.Fori(1, B - 1) as i:
                body(i)
            body(B - 1)

        with nc.Block() as block:
            @block.sync
            def _(sp):
                def load(c, half, b):
                    wait_apart(sp, s, s["xn_ready"], c - 1)
                    sp.dma_start(xin[:, half, :, :],
                                 x_dram[b, half * HALF:(half + 1) * HALF, :]
                                 .rearrange("(t p) d -> p t d", p=P)).then_inc(s["x_in"][half], 16)

                def store(c, half, b):
                    wait_apart(sp, s, s["v_ready"], c + 1)
                    for g in range(G):
                        sp.dma_start(V[b * 2 + g // 2, :, g % 2, half * CT:(half + 1) * CT, :],
                                     vs[:, half, :, g * (heads // G):(g + 1) * (heads // G), :]
                                     .rearrange("p t h c -> p t (h c)")).then_inc(s["v_out"][half], 16)
                    tok = slice(half * HALF, (half + 1) * HALF)
                    for m, (_, rows, _, _) in enumerate(tensors):
                        wait_apart(sp, s, s["q3"], M * c + (m + 1))
                        if not A or m < 2:
                            dst = [(Q if m < 2 else K)[b * 2 + m % 2, :, :, tok]]
                            src = [parts[:, m, :, :]]
                        else:
                            dst = [K[m - 2, b * 2 + a, :, :, tok] for a in (0, 1)]
                            src = [parts[a * 32:(a + 1) * 32, m, :, :] for a in (0, 1)]
                        for o, i_ in zip(dst, src):
                            sp.dma_start(o.rearrange("s p t -> p s t"), i_).then_inc(s["parts_out"][m], 16)

                def clear_rows(c, half, b):
                    zeros, zeroed, buf, rel_rows = clear
                    for rows in (buf.rearrange("(b h p r) d -> b h p (r d)", b=B, h=2, p=P),
                                 rel_rows.rearrange("a s p c -> (a s p c)")
                                 .rearrange("(b h p n) -> b h p n", b=B, h=2, p=P)):
                        sp.dma_start(rows[b, half], zeros[:, 0:rows.shape[3]]).then_inc(zeroed, 16)

                chunks(sp, ([(1, load)] if A else []) + [(0, store)] + ([(0, clear_rows)] if clear else []))
                if clear:
                    sp.wait_ge(clear[1], 2 * 16 * 2 * B)
                for m in range(M):
                    sp.wait_ge(s["parts_out"][m], 16 * 2 * B * (2 if A and m > 1 else 1))
                for half in range(2):
                    sp.wait_ge(s["v_out"][half], 16 * G * B)

            @block.vector
            def _(dve):
                def norm(c, half, b):
                    if A:
                        dve.wait_ge(s["x_in"][half], 16 * (b + 1))
                        xc = xin[:, half, :, :]
                    else:
                        xc = X[:, bass.ds(c * CT, CT), :]
                    wait_apart(dve, s, s["turned"], c - 1)
                    normalize_steps(nc, s, xc, stats, mv, rstd, xn[:, half, :, :], c)

                def split(c, half, b):
                    dve.wait_ge(s["v_mm"], c + 1)
                    wait(dve, s["v_out"][half], 16 * G * b)
                    src = pV[:, :, :].rearrange("p t (h d) -> p t h d", d=HD)
                    for t in range(CT):
                        if A:
                            last = nc.vector.tensor_copy(vs[:, half, t, :, 0:HD], src[:, t])
                        else:
                            last = nc.vector.tensor_tensor(vs[:, half, t, :, 0:HD], src[:, t],
                                                           bv[:, :].rearrange("p (h d) -> p h d", d=HD), ALU.add)
                    last.then_inc(s["v_ready"], 1)
                    for m, (prod, rows, scale, col) in enumerate(tensors):
                        dve.wait_ge(s["mm"], len(products) * c + (prod + 1))
                        wait(dve, s["r1"], M * c + (m + 1 - M))
                        nc.vector.tensor_scalar(full[0:rows, m, :], pR[prod][0:rows, :], scale,
                                                0.0 if col is None else bcol[0:rows, col:col + 1],
                                                ALU.mult, ALU.add).then_inc(s["qf"], 1)
                    for m, (prod, rows, scale, col) in enumerate(tensors):
                        dve.wait_ge(s["q2"], M * c + (m + 1))
                        nc.vector.tensor_tensor(part(m, rows, 2), rest[0:rows, m, :],
                                                part(m, rows, 1), ALU.subtract).then_inc(s["q3"], 1)

                chunks(dve, [(1, norm), (0, split)])

            @block.scalar
            def _(act):
                def root(c, half, b):
                    act.wait_ge(s["var"], c + 1)
                    nc.scalar.sqrt(rstd[:, 1, :], rstd[:, 0, :]).then_inc(s["dev"], 1)

                def copy(c, half, b):
                    act.wait_ge(s["turned"], c + 1)
                    wait(act, s["v_mm"], c - 1)
                    nc.scalar.copy(xT[:, half, :, :], pT[:, :, :]).then_inc(s["xt_ready"], 1)

                def split(c, half, b):
                    for m, (prod, rows, scale, col) in enumerate(tensors):
                        act.wait_ge(s["qf"], M * c + (m + 1))
                        wait(act, s["parts_out"][m], (2 * b + half) * (32 if A and m > 1 else 16))
                        nc.scalar.copy(part(m, rows, 0), full[0:rows, m, :]).then_inc(s["q1"], 1)
                    for m, (prod, rows, scale, col) in enumerate(tensors):
                        act.wait_ge(s["r1"], M * c + (m + 1))
                        nc.scalar.copy(part(m, rows, 1), rest[0:rows, m, :]).then_inc(s["q2"], 1)

                chunks(act, [(1, root), (0, split), (1, copy)])

            @block.gpsimd
            def _(pool):
                def split(c, half, b):
                    for m, (prod, rows, scale, col) in enumerate(tensors):
                        pool.wait_ge(s["q1"], M * c + (m + 1))
                        wait(pool, s["q3"], M * c + (m + 1 - M))
                        nc.gpsimd.tensor_tensor(rest[0:rows, m, :], full[0:rows, m, :],
                                                part(m, rows, 0), ALU.subtract).then_inc(s["r1"], 1)

                chunks(pool, [(0, split)])

            @block.tensor
            def _(pe):
                def turn(c, half, b):
                    pe.wait_ge(s["xn_ready"], c + 1)
                    wait(pe, s["xt_ready"], c)
                    for t in range(CT):
                        for d in range(2):
                            last = nc.tensor.transpose(pT[:, d, t * P:(t + 1) * P],
                                                       xn[:, half, t, d * P:(d + 1) * P], ident[:, :])
                    last.then_inc(s["turned"], 1)

                def multiply(c, half, b):
                    pe.wait_ge(s["xt_ready"], c + 1)
                    wait(pe, s["v_ready"], c)
                    for t in range(CT):
                        for d in range(2):
                            last = nc.tensor.matmul(pV[:, t, :], xT[:, half, d, t * P:(t + 1) * P],
                                                    wvT[:, d, :], start=(d == 0), stop=(d == 1))
                    last.then_inc(s["v_mm"], 1)
                    wait(pe, s["qf"], M * c)
                    for k, (wT, at, rows) in enumerate(products):
                        for d in range(2):
                            last = nc.tensor.matmul(pR[k][0:rows, :], wT[:, d, at:at + rows],
                                                    xT[:, half, d, :], start=(d == 0), stop=(d == 1))
                        last.then_inc(s["mm"], 1)

                chunks(pe, [(0, multiply), (1, turn)])
    give_back()


def relative_rows(nc, emb, rel, identF):
    s, give_back = semaphores(nc, "e_in e_turned e_copied e_diff e_parts e_placed")
    with ExitStack() as ctx:
        raw = ctx.enter_context(nc.sbuf_tensor("e_raw", [P, 2, HD], F32))
        eT = ctx.enter_context(nc.sbuf_tensor("e_T", [HD, 2 * P], F32))
        diff = ctx.enter_context(nc.sbuf_tensor("e_diff", [HD, 2, REL], F32))
        parts = ctx.enter_context(nc.sbuf_tensor("e_parts", [HD, 3, REL], BF16))
        pt = ctx.enter_context(nc.psum_tensor("e_pt", [P, 2, P], F32))
        with nc.Block() as block:
            @block.sync
            def _(sp):
                sp.dma_start(raw[:, 0, :], emb[0:P, :]).then_inc(s["e_in"], 16)
                sp.dma_start(raw[0:NREL - P, 1, :], emb[P:NREL, :]).then_inc(s["e_in"], 16)
                sp.wait_ge(s["e_parts"], 3)
                at = 0
                for part, rows in ((2, 1), (1, 1), (0, 1), (1, 1), (0, 1), (0, 1)):
                    sp.dma_start(rel[at:at + HD, :], parts[:, part, :]).then_inc(s["e_placed"], 16)
                    at += HD
                sp.wait_ge(s["e_placed"], 16 * SPLITS)

            @block.tensor
            def _(pe):
                pe.wait_ge(s["e_in"], 32)
                nc.tensor.transpose(pt[0:HD, 0, :], raw[:, 0, :], identF[:, :])
                nc.tensor.transpose(pt[0:HD, 1, 0:NREL - P], raw[0:NREL - P, 1, :],
                                    identF[0:NREL - P, 0:NREL - P]).then_inc(s["e_turned"], 1)

            @block.vector
            def _(dve):
                dve.wait_ge(s["e_turned"], 1)
                nc.vector.tensor_copy(eT[:, 0:NREL], pt[0:HD, :, :].rearrange("p a b -> p (a b)")[:, 0:NREL]).then_inc(s["e_copied"], 1)
                dve.wait_ge(s["e_copied"], 1)
                nc.vector.tensor_scalar(diff[:, 0, 0:NREL - 1], eT[:, 1:NREL], eT[:, 0:1], None, ALU.subtract)
                nc.vector.tensor_scalar(diff[:, 0, NREL - 1:REL], eT[:, NREL - 1:NREL].broadcast_to([HD, P]),
                                        eT[:, 0:1], None, ALU.subtract).then_inc(s["e_diff"], 1)
                dve.wait_ge(s["e_diff"], 1)
                nc.vector.tensor_copy(parts[:, 0, :], diff[:, 0, :]).then_inc(s["e_parts"], 1)
                dve.wait_ge(s["e_parts"], 1)
                nc.vector.tensor_tensor(diff[:, 1, :], diff[:, 0, :], parts[:, 0, :], ALU.subtract).then_inc(s["e_diff"], 1)
                dve.wait_ge(s["e_diff"], 2)
                nc.vector.tensor_copy(parts[:, 1, :], diff[:, 1, :]).then_inc(s["e_parts"], 1)
                dve.wait_ge(s["e_parts"], 2)
                nc.vector.tensor_tensor(parts[:, 2, :], diff[:, 1, :], parts[:, 1, :], ALU.subtract).then_inc(s["e_parts"], 1)
    give_back()


AHEAD_MAX = 24
AHEAD_REL = 34
AHEAD_REL_STORE = 32
AHEAD_REL_LOAD = 27


def attend(nc, kind, Q, K, V, OV, DN, emb, RR, MD, identF, identB):
    A = kind == "A"
    names = "max_full max_free kept nm_ready ms_a ms_ready mt_full mt_copied md_out st_full probs pv_done ot_copied passed"
    rings = dict(qs_in=BODY, m_in=BODY, ks_in=2, v_in=2, od_out=2)
    if A:
        names, rings = names + " rel_full rel_copied band_ready", dict(rings, rel_out=8, bias_in=4)
    s, give_back = semaphores(nc, names, **rings)
    NV = 1 if A else HG
    KV = 2
    with ExitStack() as ctx:
        def sb(name, shape, dt=F32):
            return ctx.enter_context(nc.sbuf_tensor(f"{kind}a_{name}", shape, dt))

        def psum(name, shape):
            return ctx.enter_context(nc.psum_tensor(f"{kind}a_{name}", shape, F32))

        qs = sb("qs", [KM, BODY, HG, HALF], BF16)
        ks = sb("ks", [KM, 2, KV if A else HG, T], BF16)
        vals = sb("vals", [P, 2, KT, NV, VW])
        probs = sb("probs", [P, 4, 2, HALF])
        osb = sb("osb", [P, 2, HALF])
        NPART = 3 if A else 2
        mpart = sb("mpart", [P, 2, HG, 4, NPART])
        nm = sb("nm", [P, 2, HG * 4])
        nrest = sb("nrest", [P, HG * 4])
        ms = sb("ms", [P, 3, HG * 4], BF16)
        mT = sb("mT", [3 * HG * 4, P], BF16)
        if A:
            rel = sb("rel", [KR, REL], BF16)
            relsb = sb("relsb", [P, 2, 2, REL])
            bias = sb("bias", [P, 4, 2, 3 * P])
            near = sb("near", [P, BODY, HG, 4, 3 * P])
            relative_rows(nc, emb, rel, identF)
        pE = psum("pE", [P, 2, 2, HALF])
        pM = psum("pM", [P, 2, HALF])
        pO = psum("pO", [P, HALF])
        pX = psum("pX", [P, HALF])

        with nc.Block() as block:
            @block.vector
            def _(dve):
                nc.vector.memset(ks[KR:KM, :, :, :], 1.0)

        def steps(eng, stages):
            def body(i):
                for k in range(BODY * STEPS):
                    for ahead, every, at, f in stages:
                        kk = k + ahead
                        if kk % every != at:
                            continue
                        if not isinstance(i, int) or 0 <= BODY * STEPS * i + kk < UNITS * STEPS:
                            f(i, kk)
            body(-1)
            body(0)
            with eng.Fori(1, UNITS // BODY - 1) as i:
                body(i)
            body(UNITS // BODY - 1)
            body(UNITS // BODY)

        def unit_of(i, kk):
            return BODY * i + kk // STEPS, (kk // STEPS) % BODY, kk % STEPS

        def step_of(i, kk):
            return BODY * STEPS * i + kk

        def window(kt_or_block, qh_block):
            return [r for r in (-1, 0, 1) if 0 <= qh_block + r < KT]

        with nc.Block() as block:
            @block.sync
            def _(sp):
                def load_queries(i, kk):
                    u, slot, _ = unit_of(i, kk)
                    body = i + kk // (STEPS * BODY)
                    wait_apart(sp, s, s["st_full"], STEPS * (u - BODY + 1))
                    qh, jj = slot % 2, slot // 2
                    at = 0
                    for parts in (3, 2, 1):
                        src = Q.rearrange("i s (d h) t -> i s d h t", d=HD)[
                            body, 0:parts, :, jj * HG:(jj + 1) * HG, qh * HALF:(qh + 1) * HALF]
                        sp.dma_start(qs[at:at + parts * HD, slot, :, :],
                                     src.rearrange("s d h t -> (s d) h t")).then_inc(s["qs_in"][slot], 16)
                        at += parts * HD

                def load_keys(i, kk):
                    u, slot, _ = unit_of(i, kk)
                    body = i + kk // (STEPS * BODY)
                    jj = slot // 2
                    wait_apart(sp, s, s["st_full"], STEPS * (u - 2))
                    at = 0
                    for parts in (3, 2, 1):
                        if A:
                            src = K.rearrange("v i s (d g) t -> i s d g v t", d=HD)[
                                body, 3 - parts:3, :, jj, :, :].rearrange("s d v t -> (s d) v t")
                        else:
                            src = K.rearrange("i s (d h) t -> i s d h t", d=HD)[
                                body, 3 - parts:3, :, jj * HG:(jj + 1) * HG, :].rearrange("s d h t -> (s d) h t")
                        sp.dma_start(ks[at:at + parts * HD, jj, :, :], src).then_inc(s["ks_in"][jj], 16)
                        at += parts * HD

                def load_values(i, kk):
                    u, slot, _ = unit_of(i, kk)
                    body = i + kk // (STEPS * BODY)
                    jj = slot // 2
                    wait_apart(sp, s, s["pv_done"], KT * (u - 2))
                    sp.dma_start(vals[:, jj, :, :, :].rearrange("p k h c -> p (k h c)"),
                                 V[body, :, jj, :, :].rearrange("p k c -> p (k c)")).then_inc(s["v_in"][jj], 16)

                def store_relative(i, kk):
                    u, slot, st = unit_of(i, kk)
                    g = step_of(i, kk)
                    wait_apart(sp, s, s["rel_copied"], g + 1)
                    wait_apart(sp, s, s["max_free"], 2 * (g - 2 * STEPS + 1))
                    sp.dma_start(RR[slot % 2, st - 1:st + 1, :, P + 1:P + 1 + REL].rearrange("q p c -> p q c"),
                                 relsb[:, (kk // 2) % 2, :, :]).then_inc(s["rel_out"][(kk // 2) % 8], 16)

                def load_relative(i, kk):
                    u, slot, st = unit_of(i, kk)
                    body = i + kk // (STEPS * BODY)
                    g = step_of(i, kk)
                    pair = kk // 2
                    wait_apart(sp, s, s["rel_out"][pair % 8], 16 * (4 * i + pair // 8 + 1))
                    wait_apart(sp, s, s["max_free"], 2 * (g - 7))
                    base = RR[slot % 2, st - 1:st + 1, :, :]
                    src = bass.AP(tensor=base.tensor, offset=base.offset + P - 1,
                                  ap=[[RELROW - 1, P], [P * RELROW, 2], [1, 3 * P]])
                    sp.dma_start(bias[:, pair % 4, :, :], src).then_inc(s["bias_in"][pair % 4], 16)

                def store_max(i, kk):
                    u, slot, _ = unit_of(i, kk)
                    wait_apart(sp, s, s["mt_copied"], u + 1)
                    sp.dma_start(MD[slot], mT[:, :]).then_inc(s["md_out"], 16)

                def load_max(i, kk):
                    u, slot, _ = unit_of(i, kk)
                    wait_apart(sp, s, s["md_out"], 16 * (u + 1))
                    wait_apart(sp, s, s["st_full"], STEPS * (u - BODY + 1))
                    sp.dma_start(qs[KR:KM, slot, :, :].rearrange("s h t -> s (h t)"),
                                 MD[slot].rearrange("(s r) q -> s (r q)", s=3)).then_inc(s["m_in"][slot], 16)

                rel_stages = [(AHEAD_REL_STORE, 2, 1, store_relative), (AHEAD_REL_LOAD, 2, 1, load_relative)] if A else []
                steps(sp, rel_stages + [(3 * STEPS - 2, STEPS, 0, load_queries),
                                        (2 * STEPS - 2, 2 * STEPS, 0, load_keys),
                                        (2 * STEPS - 4, 2 * STEPS, 0, load_values),
                                        (5, STEPS, 0, store_max), (3, STEPS, 0, load_max)])
                for k in range(2):
                    sp.wait_ge(s["od_out"][k], 16 * (HG + 1) * UNITS // 2)

            def far_runs(q):
                runs = [(0, 0, q - 1), (1, q + 2, KT - q - 2)]
                return [r for r in runs if r[2] > 0]

            @block.tensor
            def _(pe):
                def relative(i, kk):
                    u, slot, st = unit_of(i, kk)
                    g = step_of(i, kk)
                    if st == 0:
                        wait(pe, s["qs_in"][slot], 48 * (i + kk // (STEPS * BODY) + 1))
                    wait(pe, s["rel_copied"], g)
                    wait(pe, s["mt_copied"], mt_before(i, kk - AHEAD_REL))
                    h, q = st // 4, st % 4
                    nc.tensor.matmul(pX[:, 0:REL], qs[0:KR, slot, h, q * P:(q + 1) * P], rel[:, :],
                                     start=True, stop=True).then_inc(s["rel_full"], 1)

                def mt_before(i, k):
                    return BODY * i + (k + 7 + STEPS - 1) // STEPS

                def maximum(i, kk, half):
                    u, slot, st = unit_of(i, kk)
                    g = step_of(i, kk)
                    h, qb = st // 4, st % 4
                    q = (slot % 2) * 4 + qb
                    jj = slot // 2
                    body = i + kk // (STEPS * BODY)
                    if st == 0 and half == 0:
                        wait(pe, s["qs_in"][slot], 48 * (body + 1))
                        if slot % 2 == 0:
                            wait(pe, s["ks_in"][jj], 48 * (body + 1))
                    query = qs[0:KR, slot, h, qb * P:(qb + 1) * P]
                    if A:
                        runs = []
                        col = 0
                        for v, first, n in far_runs(q):
                            while n:
                                m = min(n, 4 - col % 4)
                                runs.append((col, v, first, m))
                                col, first, n = col + m, first + m, n - m
                        near_blocks = window(0, q)
                        runs.append((8 - len(near_blocks), 0, q + near_blocks[0], len(near_blocks)))
                        wait(pe, s["max_free"], 2 * g + (half - 1))
                        for c, v, first, m in [r for r in runs if r[0] // 4 == half]:
                            last = nc.tensor.matmul(pM[:, half, (c % 4) * P:(c % 4 + m) * P], query,
                                                    ks[0:KR, jj, v, first * P:(first + m) * P],
                                                    start=True, stop=True)
                        last.then_inc(s["max_full"], 1)
                    else:
                        wait(pe, s["max_free"], 2 * g + (half - 1))
                        nc.tensor.matmul(pM[:, half, :], query, ks[0:KR, jj, h, half * HALF:(half + 1) * HALF],
                                         start=True, stop=True).then_inc(s["max_full"], 1)

                def turn_max(i, kk):
                    u, slot, _ = unit_of(i, kk)
                    pe.wait_ge(s["ms_ready"], u + 1)
                    wait(pe, s["mt_copied"], u)
                    if A:
                        wait(pe, s["rel_copied"], min(step_of(i, kk) - 7 + AHEAD_REL + 1, UNITS * STEPS)
                             if isinstance(i, int) else step_of(i, kk) - 7 + AHEAD_REL + 1)
                    nc.tensor.matmul(pX[0:3 * HG * 4, 0:P], ms[:, :, :].rearrange("p s r -> p (s r)"),
                                     identB[:, :], start=True, stop=True).then_inc(s["mt_full"], 1)

                def scores(i, kk, hh):
                    u, slot, st = unit_of(i, kk)
                    g = step_of(i, kk)
                    kt, pair = st // 2, st % 2
                    jj = slot // 2
                    if st == 0 and hh == 0:
                        wait(pe, s["m_in"][slot], 16 * (i + kk // (STEPS * BODY) + 1))
                        if A:
                            wait(pe, s["band_ready"], HG * (u + 1))
                    if hh == 0:
                        wait(pe, s["probs"], g - 1)
                    h = 2 * pair + hh
                    out = pE[:, kk % 2, hh, :]
                    if not A:
                        last = nc.tensor.matmul(out, ks[0:KM, jj, h, kt * P:(kt + 1) * P],
                                                qs[0:KM, slot, h, :], start=True, stop=True)
                        if hh == 1:
                            last.then_inc(s["st_full"], 1)
                        return
                    first = (slot % 2) * 4
                    left = [b for b in range(4) if first + b >= kt + 2]
                    right = [b for b in range(4) if first + b <= kt - 2]
                    for v, blocks in ((0, left), (1, right)):
                        if blocks:
                            cols = slice(blocks[0] * P, (blocks[-1] + 1) * P)
                            last = nc.tensor.matmul(out[:, cols], ks[0:KM, jj, v, kt * P:(kt + 1) * P],
                                                    qs[0:KM, slot, h, cols], start=True, stop=True)
                    for b in range(4):
                        r = kt - (first + b)
                        if abs(r) <= 1:
                            last = nc.tensor.transpose(out[:, b * P:(b + 1) * P],
                                                       near[:, slot, h, b, (r + 1) * P:(r + 2) * P], identF[:, :])
                    if hh == 1:
                        last.then_inc(s["st_full"], 1)

                def weigh(i, kk, part):
                    u, slot, st = unit_of(i, kk)
                    g = step_of(i, kk)
                    kt, jj = st // 2, slot // 2
                    if st == 1 and part == 0:
                        if slot % 2 == 0:
                            wait(pe, s["v_in"][jj], 16 * (i + kk // (STEPS * BODY) + 1))
                        wait(pe, s["ot_copied"], u)
                    if part == 0:
                        pe.wait_ge(s["probs"], g + 1)
                    cols = slice(part * HALF // 2, (part + 1) * HALF // 2)
                    for h in range(HG):
                        last = nc.tensor.matmul(pO[h * VW:(h + 1) * VW, cols], vals[:, jj, kt, 0 if A else h, :],
                                                probs[:, (kk - 1 + h // 2) % 4, h % 2, cols],
                                                start=(kt == 0 and part == 0),
                                                stop=(kt == KT - 1 and part == 1), tile_position=(0, h * VW))
                    if part == 1:
                        last.then_inc(s["pv_done"], 1)

                def halves(step):
                    return [lambda i, kk: step(i, kk, 0), lambda i, kk: step(i, kk, 1)]

                order = []
                for odd in range(2):
                    (s0, s1), (m0, m1) = [[(ahead, 2, odd, f) for f in halves(step)]
                                          for ahead, step in ((0, scores), (AHEAD_MAX, maximum))]
                    w = (-2, 2, 1, halves(weigh)[0]) if odd else (-3, 2, 1, halves(weigh)[1])
                    turn = [(7, STEPS, 0, turn_max)] if odd else []
                    if A:
                        order += [s0, w, (AHEAD_REL, 2, odd, relative), m0, s1, m1] + turn
                    else:
                        order += [s0, m0, s1, m1] + turn + [w]
                steps(pe, order)

            @block.vector
            def _(dve):
                def maximum(i, kk):
                    u, slot, st = unit_of(i, kk)
                    g = step_of(i, kk)
                    h, qb = st // 4, st % 4
                    q = (slot % 2) * 4 + qb
                    s2 = slot % 2
                    if st == 0:
                        wait(dve, s["nm_ready"], HG * (u - 1))
                        if A:
                            wait(dve, s["band_ready"], HG * (u - 1))
                            wait(dve, s["st_full"], STEPS * (u - BODY + 1))
                    part = mpart[:, s2, h, qb, :]
                    dve.wait_ge(s["max_full"], 2 * g + 1)
                    nc.vector.reduce_max(part[:, 0:1], pM[:, 0, :], AX.X).then_inc(s["max_free"], 1)
                    dve.wait_ge(s["max_full"], 2 * g + 2)
                    if A:
                        blocks = window(0, q)
                        far = (4 - len(blocks)) * P
                        lo = (blocks[0] + 1) * P
                        pair = kk // 2
                        wait(dve, s["bias_in"][pair % 4], 16 * (8 * i + pair // 4 + 1))
                        nc.vector.reduce_max(part[:, 1:2], pM[:, 1, 0:far], AX.X)
                        nc.vector.tensor_tensor_reduce(out=near[:, slot, h, qb, lo:lo + len(blocks) * P],
                                                       in0=pM[:, 1, far:HALF],
                                                       in1=bias[:, pair % 4, kk % 2, lo:lo + len(blocks) * P],
                                                       scale=1.0, scalar=-3.0e38, op0=ALU.add, op1=ALU.max,
                                                       accum_out=part[:, 2:3]).then_inc(s["max_free"], 1)
                    else:
                        nc.vector.reduce_max(part[:, 1:2], pM[:, 1, :], AX.X).then_inc(s["max_free"], 1)
                    if qb == 3:
                        dve.wait_ge(s["max_free"], 2 * g + 2)
                        nc.vector.reduce_max(nm[:, s2, h * 4:(h + 1) * 4], mpart[:, s2, h, :, :], AX.X,
                                             negate=True).then_inc(s["nm_ready"], 1)
                    if st == STEPS - 1:
                        dve.wait_ge(s["nm_ready"], HG * (u + 1))
                        wait(dve, s["mt_full"], u)
                        nc.vector.tensor_copy(ms[:, 0, :], nm[:, s2, :]).then_inc(s["ms_a"], 1)
                        dve.wait_ge(s["ms_a"], 3 * u + 1)
                        nc.vector.tensor_tensor(nrest[:, :], nm[:, s2, :], ms[:, 0, :], ALU.subtract).then_inc(s["ms_a"], 1)
                        dve.wait_ge(s["ms_a"], 3 * u + 2)
                        nc.vector.tensor_copy(ms[:, 1, :], nrest[:, :]).then_inc(s["ms_a"], 1)
                        dve.wait_ge(s["ms_a"], 3 * u + 3)
                        nc.vector.tensor_tensor(ms[:, 2, :], nrest[:, :], ms[:, 1, :], ALU.subtract).then_inc(s["ms_ready"], 1)

                steps(dve, [(AHEAD_MAX, 1, 0, maximum)])

            @block.gpsimd
            def _(pool):
                def band(i, kk):
                    u, slot, st = unit_of(i, kk)
                    h, qh = st // 4, slot % 2
                    pool.wait_ge(s["nm_ready"], HG * u + h + 1)
                    edge, lo = (0, P) if qh == 0 else (3, 0)
                    rest = slice(1, 4) if qh == 0 else slice(0, 3)
                    m = nm[:, qh, h * 4:(h + 1) * 4]
                    one = near[:, slot, h, edge, lo:lo + 2 * P]
                    nc.gpsimd.tensor_tensor(one, one, m[:, edge:edge + 1].broadcast_to([P, 2 * P]), ALU.add)
                    three = near[:, slot, h, rest, :]
                    nc.gpsimd.tensor_tensor(three, three, m[:, rest].unsqueeze(2).broadcast_to([P, 3, 3 * P]),
                                            ALU.add).then_inc(s["band_ready"], 1)

                if A:
                    steps(pool, [(AHEAD_MAX, 4, 3, band)])

            @block.scalar
            def _(act):
                def copy_relative(i, kk):
                    g = step_of(i, kk)
                    pair = kk // 2
                    act.wait_ge(s["rel_full"], g + 1)
                    if kk % 2 == 0:
                        wait(act, s["rel_out"][(pair - 2) % 8], 16 * (4 * i + (pair - 2) // 8 + 1))
                    nc.scalar.copy(relsb[:, pair % 2, kk % 2, :], pX[:, 0:REL]).then_inc(s["rel_copied"], 1)

                def copy_max(i, kk):
                    u, slot, _ = unit_of(i, kk)
                    act.wait_ge(s["mt_full"], u + 1)
                    wait(act, s["md_out"], 16 * u)
                    nc.scalar.copy(mT[:, :], pX[0:3 * HG * 4, 0:P]).then_inc(s["mt_copied"], 1)

                def exp(i, kk):
                    g = step_of(i, kk)
                    act.wait_ge(s["st_full"], g + 1)
                    wait(act, s["pv_done"], 32 * i + kk // 2 - 1)
                    nc.scalar.activation(probs[:, kk % 4, :, :], pE[:, kk % 2, :, :], ACT.Exp).then_inc(s["probs"], 1)

                def copy_out(i, kk):
                    u, slot, _ = unit_of(i, kk)
                    act.wait_ge(s["pv_done"], KT * (u + 1))
                    wait(act, s["od_out"][slot % 2], 16 * (HG + 1) * (2 * i + (kk // STEPS) // 2))
                    nc.scalar.copy(osb[:, slot % 2, :], pO[:, :]).then_inc(s["ot_copied"], 1)

                def store_out(i, kk):
                    u, slot, _ = unit_of(i, kk)
                    body = i + kk // (STEPS * BODY)
                    wait_apart(act, s, s["ot_copied"], u + 1)
                    qh, jj, h = slot % 2, slot // 2, kk % STEPS
                    row = (jj * HG + h) * HD
                    act.dma_start(OV[body, qh, row:row + HD],
                                  osb[h * VW:h * VW + HD, slot % 2, :]).then_inc(s["od_out"][slot % 2], 16)
                    if h == HG - 1:
                        act.dma_start(DN[body, qh, jj * HG:(jj + 1) * HG],
                                      osb[HD:P:VW, slot % 2, :]).then_inc(s["od_out"][slot % 2], 16)

                steps(act, ([(AHEAD_REL, 1, 0, copy_relative)] if A else [])
                      + [(7, STEPS, 0, copy_max), (0, 1, 0, exp), (-STEPS - 2, STEPS, 0, copy_out)]
                      + [(-STEPS - 3, STEPS, h, store_out) for h in range(HG)])
    give_back()


def chunk_loop(eng, stages, n):
    def body(i):
        for j in range(n):
            for lag, step in stages:
                k = j + lag
                if not isinstance(i, int) or 0 <= n * i + k < 2 * B:
                    step(n * i + k, k % n, k % 2, (n // 2) * i + k // 2, i + k // n)
    body(-1)
    body(0)
    with eng.Fori(1, 2 * B // n - 1) as i:
        body(i)
    body(2 * B // n - 1)


def after_attention(nc, kind, x_dram, X, XN, LG, OV, DN, RD, w, identF):
    A = kind == "A"
    BN = 4
    ROWS = 2 * B * 2 * 2 * HG // P
    s, give_back = semaphores(
        nc, "w_in dn_in inverted rd_out divided wo_mm added stat var dev rec xn_ready passed turned xt_ready ones"
        " routed kept logits summed", o_in=BN, d_in=2, x_in=2)
    with ExitStack() as ctx:
        def sb(name, shape, dt=F32):
            return ctx.enter_context(nc.sbuf_tensor(f"{kind}o_{name}", shape, dt))

        def psum(name, shape):
            return ctx.enter_context(nc.psum_tensor(f"{kind}o_{name}", shape, F32))

        woT = sb("woT", [P, 2, D])
        wr = sb("wr", [P, 2, E])
        load_transposed(nc, f"{kind}o", [(w["o"], woT, as_is)], identF)
        dens = sb("dens", [P, ROWS, HALF])
        osl, den = sb("osl", [P, BN, 2, CHUNK]), sb("den", [P, 2, 2, CHUNK])
        xin = sb("xin", [P, 2, CT, D]) if A else None
        stats, mv, rstd = sb("stats", [P, CT, 6]), sb("mv", [P, CT, 2]), sb("rstd", [P, 3, CT])
        xn = sb("xn", [P, 2, CT, D])
        xT = sb("xT", [P, 2, CHUNK])
        borow, ones = sb("borow", [1, D]), sb("ones", [1, P])
        pW = psum("pW", [P, 2, CT, D])
        pT = psum("pT", [P, 2, CHUNK])
        pL = psum("pL", [P, CT, E])

        def tiles(c):
            return bass.ds(c * CT, CT)

        with nc.Block() as block:
            @block.sync
            def _(sp):
                flat = [d.rearrange("i q h t -> (i q h) t").rearrange("(a p) t -> p a t", p=P) for d in (DN, RD)]
                sp.dma_start(dens[:, :, :], flat[0]).then_inc(s["dn_in"], 16)
                sp.dma_start(wr[:, :, :], w["r"].rearrange("(a p) e -> p a e", p=P)).then_inc(s["w_in"], 16)
                if not A:
                    sp.dma_start(borow[:, :], w["bo"].rearrange("(a n) -> a n", a=1)).then_inc(s["w_in"], 16)
                sp.wait_ge(s["inverted"], 1)
                sp.dma_start(flat[1], dens[:, :, :]).then_inc(s["rd_out"], 16)
                sp.wait_ge(s["rd_out"], 16)

                def load(c, slot, half, b, body):
                    wait_apart(sp, s, s["wo_mm"], c - BN + 1)
                    sp.dma_start(osl[:, slot, :, :], OV.rearrange("(b g) q p t -> b q p g t", g=2)
                                 [b, half]).then_inc(s["o_in"][slot], 16)

                def load_reciprocals(c, slot, half, b, body):
                    wait_apart(sp, s, s["divided"], c - 1)
                    for g in range(2):
                        src = RD.rearrange("(b g) q h t -> b g q h t", g=2)[b, g, half]
                        sp.dma_start(den[:, half, g, :],
                                     src.unsqueeze(1).broadcast_to([2 * HG, HD, CHUNK])).then_inc(s["d_in"][half], 16)

                def load_x(c, slot, half, b, body):
                    wait_apart(sp, s, s["added"], c - 1)
                    sp.dma_start(xin[:, half, :, :], x_dram[b, half * HALF:(half + 1) * HALF, :]
                                 .rearrange("(t p) d -> p t d", p=P)).then_inc(s["x_in"][half], 16)

                chunk_loop(sp, [(3, load), (2, load_reciprocals)] + ([(1, load_x)] if A else []), BN)

            @block.vector
            def _(dve):
                nc.vector.memset(ones[:, :], 1.0).then_inc(s["ones"], 1)
                dve.wait_ge(s["dn_in"], 16)
                nc.vector.reciprocal(dens[:, :, :], dens[:, :, :]).then_inc(s["inverted"], 1)

                def divide(c, slot, half, b, body):
                    dve.wait_ge(s["o_in"][slot], 16 * (body + 1))
                    dve.wait_ge(s["d_in"][half], 32 * (b + 1))
                    nc.vector.tensor_tensor(osl[:, slot, :, :], osl[:, slot, :, :], den[:, half, :, :],
                                            ALU.mult).then_inc(s["divided"], 1)

                def add(c, slot, half, b, body):
                    dve.wait_ge(s["wo_mm"], c + 1)
                    if A:
                        dve.wait_ge(s["x_in"][half], 16 * (b + 1))
                    nc.vector.tensor_tensor(X[:, tiles(c), :], xin[:, half, :, :] if A else X[:, tiles(c), :],
                                            pW[:, half, :, :], ALU.add).then_inc(s["added"], 1)
                    dve.wait_ge(s["added"], c + 1)
                    wait(dve, s["turned"], c - 1)
                    wait(dve, s["kept"], c - 1)
                    wait_apart(dve, s, s["summed"], c - 1)
                    normalize_steps(nc, s, X[:, tiles(c), :], stats, mv, rstd, xn[:, half, :, :], c)

                chunk_loop(dve, [(2, divide), (0, add)], BN)

            @block.gpsimd
            def _(pool):
                def add_normalized(c, slot, half, b, body):
                    pool.wait_ge(s["xn_ready"], c + 1)
                    nc.gpsimd.tensor_tensor(X[:, tiles(c), :], X[:, tiles(c), :], xn[:, half, :, :],
                                            ALU.add).then_inc(s["summed"], 1)

                chunk_loop(pool, [(0, add_normalized)], BN)

            @block.scalar
            def _(act):
                def root(c, slot, half, b, body):
                    act.wait_ge(s["var"], c + 1)
                    nc.scalar.sqrt(rstd[:, 1, :], rstd[:, 0, :]).then_inc(s["dev"], 1)

                def copy_logits(c, slot, half, b, body):
                    act.wait_ge(s["routed"], c + 1)
                    nc.scalar.copy(LG[:, tiles(c), :], pL[:, :, :]).then_inc(s["logits"], 1)

                def copies(c, slot, half, b, body):
                    act.wait_ge(s["turned"], c + 1)
                    wait(act, s["routed"], c)
                    nc.scalar.copy(xT[:, :, :], pT[:, :, :]).then_inc(s["xt_ready"], 1)
                    nc.scalar.copy(XN[:, tiles(c), :], xn[:, half, :, :]).then_inc(s["kept"], 1)

                chunk_loop(act, [(1, root), (0, copies), (0, copy_logits)], BN)

            @block.tensor
            def _(pe):
                pe.wait_ge(s["w_in"], 16 if A else 32)
                pe.wait_ge(s["ones"], 1)

                def project_out(c, slot, half, b, body):
                    pe.wait_ge(s["divided"], c + 1)
                    wait(pe, s["added"], c - 1)
                    for t in range(CT):
                        for g in range(2):
                            last = nc.tensor.matmul(pW[:, half, t, :], osl[:, slot, g, t * P:(t + 1) * P],
                                                    woT[:, g, :], start=(g == 0), stop=(A and g == 1))
                        if not A:
                            last = nc.tensor.matmul(pW[:, half, t, :], ones[0:1, :], borow[0:1, :],
                                                    start=False, stop=True)
                    last.then_inc(s["wo_mm"], 1)

                def turn(c, slot, half, b, body):
                    pe.wait_ge(s["xn_ready"], c + 1)
                    wait(pe, s["xt_ready"], c)
                    for t in range(CT):
                        for d in range(2):
                            last = nc.tensor.transpose(pT[:, d, t * P:(t + 1) * P], xn[:, half, t, d * P:(d + 1) * P],
                                                       identF[:, :])
                    last.then_inc(s["turned"], 1)

                def route(c, slot, half, b, body):
                    pe.wait_ge(s["xt_ready"], c + 1)
                    wait(pe, s["logits"], c)
                    for t in range(CT):
                        for d in range(2):
                            last = nc.tensor.matmul(pL[:, t, :], xT[:, d, t * P:(t + 1) * P], wr[:, d, :],
                                                    start=(d == 0), stop=(d == 1))
                    last.then_inc(s["routed"], 1)

                chunk_loop(pe, [(1, project_out), (0, turn), (0, route)], BN)
    give_back()


def dispatch(nc, name, XN, LG, BUF, gate, gidx, moved, before):
    s, give_back = semaphores(nc, "mask iota v a oh cum")
    with ExitStack() as ctx:
        def sb(label, shape, dt=F32):
            return ctx.enter_context(nc.sbuf_tensor(f"{name}_{label}", shape, dt))

        upper = sb("upper", [P, P], BF16)
        allone = sb("allone", [P, P], BF16)
        ei = sb("ei", [P, E])
        eint = sb("eint", [P, E], I32)
        w1, w2, w3 = (sb(f"w{k}", [P, NT * E]) for k in range(3))
        onehot = sb("onehot", [P, NT * E], BF16)
        small = sb("small", [P, 8, NT])
        sidx = sb("sidx", [P, NT], U32)
        pC = ctx.enter_context(nc.psum_tensor(f"{name}_pC", [P, NT * E], F32))
        pS = ctx.enter_context(nc.psum_tensor(f"{name}_pS", [P, NT * E], F32))

        def te(ap):
            return ap.rearrange("p (t e) -> p t e", e=E)

        def over_e(ap):
            return ap.unsqueeze(2).broadcast_to([P, NT, E])

        with nc.Block() as block:
            @block.gpsimd
            def _(pool):
                nc.gpsimd.memset(upper[:, :], 1.0)
                nc.gpsimd.memset(allone[:, :], 1.0).then_inc(s["mask"], 1)
                pool.wait_ge(s["mask"], 1)
                nc.gpsimd.affine_select(out=upper[:, :], in_=upper[:, :], compare_op=ALU.is_ge, fill=0.0,
                                        base=0, pattern=[[1, P]], channel_multiplier=-1).then_inc(s["mask"], 1)
                nc.gpsimd.iota(eint[:, :], [[1, E]], base=-E, channel_multiplier=0).then_inc(s["iota"], 1)

            @block.scalar
            def _(act):
                act.wait_ge(s["a"], 1)
                nc.scalar.activation(w2[:, :], w1[:, :], ACT.Exp).then_inc(s["a"], 1)

            @block.tensor
            def _(pe):
                pe.wait_ge(s["mask"], 2)
                pe.wait_ge(s["oh"], 1)
                for k in range(4):
                    cols = slice(k * 512, (k + 1) * 512)
                    nc.tensor.matmul(pC[:, cols], upper[:, :], onehot[:, cols], start=True, stop=True)
                    last = nc.tensor.matmul(pS[:, cols], allone[:, :], onehot[:, cols], start=True, stop=True)
                last.then_inc(s["cum"], 1)

            @block.vector
            def _(dve):
                done = [0]

                def link(ins):
                    done[0] += 1
                    ins.then_inc(s["v"], 1)
                    dve.wait_ge(s["v"], done[0])

                top, best, first, total, pos, acc, slot, t2 = (small[:, k, :] for k in range(8))
                lg = LG[:, :, :]
                dve.wait_ge(s["iota"], 1)
                link(nc.vector.tensor_copy(ei[:, :], eint[:, :]))
                link(nc.vector.reduce_max(top, lg, AX.X))
                nc.vector.tensor_tensor(te(w1[:, :]), lg, over_e(top), ALU.subtract).then_inc(s["a"], 1)
                dve.wait_ge(s["a"], 2)
                eis = ei[:, :].unsqueeze(1).broadcast_to([P, NT, E])
                link(nc.vector.tensor_scalar(w3[:, :], w1[:, :], 0.0, None, ALU.is_ge))
                link(nc.vector.tensor_tensor(te(w3[:, :]), te(w3[:, :]), eis, ALU.mult))
                link(nc.vector.tensor_reduce(first, te(w3[:, :]), AX.X, ALU.min))
                nc.vector.tensor_tensor(te(onehot[:, :]), eis, over_e(first), ALU.is_equal).then_inc(s["oh"], 1)
                link(nc.vector.reduce_sum(total, te(w2[:, :]), AX.X))
                link(nc.vector.reciprocal(gate[:, :], total))
                dve.wait_ge(s["cum"], 1)
                link(nc.vector.memset(w1[:, :], 1.0))
                link(nc.vector.memset(w1[:, :].rearrange("p (e t) -> p e t", t=NT)[:, :, 0:1], 0.0))
                link(nc.vector.tensor_copy(w2[:, :].rearrange("p (e t) -> p e t", t=NT),
                                           pS[:, :].rearrange("p (t e) -> p e t", e=E)))
                link(nc.vector.tensor_tensor_scan(w3[:, :], w1[:, :], w2[:, :], 0.0, ALU.mult, ALU.add))
                link(nc.vector.tensor_tensor(w3[:, :], w3[:, :], w2[:, :], ALU.subtract))
                link(nc.vector.tensor_tensor(te(w1[:, :]), w3[:, :].rearrange("p (e t) -> p t e", t=NT),
                                             te(pC[:, :]), ALU.add))
                link(nc.vector.tensor_tensor(w2[:, :], w1[:, :], onehot[:, :], ALU.mult))
                link(nc.vector.reduce_sum(pos, te(w2[:, :]), AX.X))
                link(nc.vector.tensor_scalar(acc, pos, float(CAP), None, ALU.is_le))
                link(nc.vector.tensor_scalar(slot, first, float(CAP), float(E * CAP - 1), ALU.mult, ALU.add))
                link(nc.vector.tensor_tensor(slot, slot, pos, ALU.add))
                link(nc.vector.tensor_scalar(t2, acc, -65536.0, 65536.0, ALU.mult, ALU.add))
                link(nc.vector.tensor_tensor(slot, slot, t2, ALU.add))
                link(nc.vector.tensor_copy(sidx[:, :], slot))
                link(nc.vector.tensor_scalar(t2, slot, float(E * CAP - 1), None, ALU.min))
                link(nc.vector.tensor_copy(gidx[:, :], t2))
                link(nc.vector.tensor_tensor(gate[:, :], gate[:, :], acc, ALU.mult))

        with nc.Block() as block:
            @block.gpsimd
            def _(pool):
                for t in range(NT):
                    nc.gpsimd.indirect_dma_start(
                        out=BUF, out_offset=bass.IndirectOffsetOnAxis(ap=sidx[:, t:t + 1], axis=0),
                        in_=XN[:, t, :], in_offset=None, bounds_check=E * CAP - 1,
                        oob_is_err=False).then_inc(moved[t % MOVES], 16)
                for k in range(MOVES):
                    pool.wait_ge(moved[k], before + 16 * (NT // MOVES))
    give_back()


def experts(nc, name, w, BUF, YD, identF):
    R = 4
    FULL = CAP // P
    LASTR = CAP - FULL * P
    rows_of = [P] * FULL + ([LASTR] if LASTR else [])
    TILES = len(rows_of)
    s, give_back = semaphores(nc, "x_turned xt_ready gu_mm silu hidden down_mm y_ready passed", in_x=R, in_w=R, y_out=2)
    with ExitStack() as ctx:
        def sb(label, shape, dt=F32):
            return ctx.enter_context(nc.sbuf_tensor(f"{name}_{label}", shape, dt))

        xe = sb("xe", [P, R, TILES, D])
        wg, wu, wd = (sb(f"w{k}", [P, R, 2, D]) for k in "gud")
        xT = sb("xT", [P, 2, 2, CAP])
        sg = sb("sg", [P, 2, CAP])
        hid = sb("hid", [P, 2, 2, CAP])
        y = sb("y", [P, 2, TILES, D])

        def psum(label, shape):
            return ctx.enter_context(nc.psum_tensor(f"{name}_{label}", shape, F32))

        pT, pG, pU = psum("pT", [P, 2, 512]), psum("pG", [P, 2, 512]), psum("pU", [P, 2, 512])
        pY = psum("pY", [P, 4, D])

        def expert_loop(eng, stages):
            def body(i):
                for j in range(R):
                    for lag, step in stages:
                        k = j + lag
                        if not isinstance(i, int) or 0 <= R * i + k < E:
                            step(R * i + k, k % R, i + k // R)
            body(-1)
            body(0)
            with eng.Fori(1, E // R - 1) as i:
                body(i)
            body(E // R - 1)
            body(E // R)

        with nc.Block() as block:
            @block.sync
            def _(sp):
                def load(e, slot, body):
                    wait_apart(sp, s, s["x_turned"], e - R + 1)
                    src = BUF.rearrange("(e c) d -> e c d", c=CAP)
                    sp.dma_start(xe[:, slot, 0:FULL, :],
                                 src[e, 0:FULL * P, :].rearrange("(t p) d -> p t d", p=P)).then_inc(s["in_x"][slot], 16)
                    if LASTR:
                        sp.dma_start(xe[0:LASTR, slot, FULL, :], src[e, FULL * P:CAP, :]).then_inc(s["in_x"][slot], 16)
                    wait_apart(sp, s, s["down_mm"], e - R + 1)
                    for dst, weights in ((wg, w["gate"]), (wu, w["up"]), (wd, w["down"])):
                        sp.dma_start(dst[:, slot, :, :],
                                     weights[e].rearrange("(a p) f -> p a f", p=P)).then_inc(s["in_w"][slot], 16)

                def store(e, slot, body):
                    wait_apart(sp, s, s["y_ready"], e + 1)
                    dst = YD.rearrange("(e c) d -> e c d", c=CAP)
                    sp.dma_start(dst[e, 0:FULL * P, :].rearrange("(t p) d -> p t d", p=P),
                                 y[:, slot % 2, 0:FULL, :]).then_inc(s["y_out"][slot % 2], 16)
                    if LASTR:
                        sp.dma_start(dst[e, FULL * P:CAP, :], y[0:LASTR, slot % 2, FULL, :]).then_inc(s["y_out"][slot % 2], 16)

                expert_loop(sp, [(3, load), (-1, store)])
                for k in range(2):
                    sp.wait_ge(s["y_out"][k], 16 * 2 * E // 2)

            @block.tensor
            def _(pe):
                def turn(e, slot, body):
                    pe.wait_ge(s["in_x"][slot], 32 * (body + 1))
                    wait(pe, s["xt_ready"], e)
                    at = 0
                    for t, rows in enumerate(rows_of):
                        for d in range(2):
                            last = nc.tensor.transpose(pT[:, d, at:at + rows], xe[0:rows, slot, t, d * P:(d + 1) * P],
                                                       identF[0:rows, 0:rows])
                        at += rows
                    last.then_inc(s["x_turned"], 1)

                def gate_up(e, slot, body):
                    pe.wait_ge(s["in_w"][slot], 48 * (body + 1))
                    pe.wait_ge(s["xt_ready"], e + 1)
                    wait(pe, s["hidden"], e)
                    for out, weights in ((pG, wg), (pU, wu)):
                        for f in range(2):
                            for d in range(2):
                                last = nc.tensor.matmul(out[:, f, 0:CAP], weights[:, slot, d, f * P:(f + 1) * P],
                                                        xT[:, slot % 2, d, :], start=(d == 0), stop=(d == 1))
                        last.then_inc(s["gu_mm"], 1)

                def down(e, slot, body):
                    pe.wait_ge(s["hidden"], e + 1)
                    wait(pe, s["y_ready"], e)
                    at = 0
                    for t, rows in enumerate(rows_of):
                        for f in range(2):
                            last = nc.tensor.matmul(pY[0:rows, t, :], hid[:, slot % 2, f, at:at + rows],
                                                    wd[:, slot, f, :], start=(f == 0), stop=(f == 1))
                        at += rows
                    last.then_inc(s["down_mm"], 1)

                expert_loop(pe, [(0, gate_up), (-1, down), (1, turn)])

            @block.scalar
            def _(act):
                def copy(e, slot, body):
                    act.wait_ge(s["x_turned"], e + 1)
                    wait(act, s["gu_mm"], 2 * (e - 1))
                    nc.scalar.copy(xT[:, slot % 2, :, :], pT[:, :, 0:CAP]).then_inc(s["xt_ready"], 1)

                def silu(e, slot, body):
                    act.wait_ge(s["gu_mm"], 2 * e + 1)
                    wait(act, s["hidden"], e)
                    nc.scalar.activation(sg[:, :, :], pG[:, :, 0:CAP], ACT.Silu).then_inc(s["silu"], 1)

                expert_loop(act, [(0, silu), (1, copy)])

            @block.vector
            def _(dve):
                def multiply(e, slot, body):
                    dve.wait_ge(s["silu"], e + 1)
                    dve.wait_ge(s["gu_mm"], 2 * e + 2)
                    wait(dve, s["down_mm"], e - 1)
                    nc.vector.tensor_tensor(hid[:, slot % 2, :, :], sg[:, :, :], pU[:, :, 0:CAP],
                                            ALU.mult).then_inc(s["hidden"], 1)

                def copy(e, slot, body):
                    dve.wait_ge(s["down_mm"], e + 1)
                    wait(dve, s["y_out"][slot % 2], 32 * (2 * body + slot // 2))
                    nc.vector.tensor_copy(y[:, slot % 2, 0:FULL, :], pY[:, 0:FULL, :])
                    nc.vector.tensor_copy(y[0:LASTR, slot % 2, FULL, :], pY[0:LASTR, FULL, :]).then_inc(s["y_ready"], 1)

                expert_loop(dve, [(0, multiply), (-1, copy)])
    give_back()


def combine(nc, name, X, YD, gate, gidx, out, moved, before):
    R = MOVES
    s, give_back = semaphores(nc, "combined", out_sent=4)
    with ExitStack() as ctx:
        yt = ctx.enter_context(nc.sbuf_tensor(f"{name}_yt", [P, R, D], F32))
        with nc.Block() as block:
            @block.gpsimd
            def _(pool):
                for t in range(NT):
                    wait(pool, s["combined"], t - R + 1)
                    nc.gpsimd.indirect_dma_start(
                        out=yt[:, t % R, :], out_offset=None, in_=YD,
                        in_offset=bass.IndirectOffsetOnAxis(ap=gidx[:, t:t + 1], axis=0),
                        bounds_check=E * CAP - 1, oob_is_err=False).then_inc(moved[t % MOVES], 16)

            @block.vector
            def _(dve):
                for t in range(NT):
                    dve.wait_ge(moved[t % MOVES], before + 16 * (t // MOVES + 1))
                    nc.vector.scalar_tensor_tensor(out=X[:, t, :], in0=yt[:, t % R, :], scalar=gate[:, t:t + 1],
                                                   in1=X[:, t, :], op0=ALU.mult, op1=ALU.add).then_inc(s["combined"], 1)

            @block.sync
            def _(sp):
                if out is not None:
                    rows = out.rearrange("b (t p) d -> p (b t) d", p=P)
                    for c in range(2 * B):
                        sp.wait_ge(s["combined"], CT * (c + 1))
                        sp.dma_start(rows[:, c * CT:(c + 1) * CT, :],
                                     X[:, c * CT:(c + 1) * CT, :]).then_inc(s["out_sent"][c % 4], 16)
                    for k in range(4):
                        sp.wait_ge(s["out_sent"][k], 16 * (2 * B // 4))
    give_back()


def block_kernel(nc, x, a_wq, a_wk, a_wv, a_wo, emb, b_wq, b_bq, b_wk, b_bk, b_wv, b_bv, b_wo, b_bo,
                 w_router, w_gate, w_up, w_down, out):
    Q = nc.dram_tensor("q_parts", (2 * B, 3, P, T), BF16).ap()
    KA = nc.dram_tensor("ka_parts", (2, 2 * B, 3, 32, T), BF16).ap()
    KB = nc.dram_tensor("kb_parts", (2 * B, 3, P, T), BF16).ap()
    VA = nc.dram_tensor("va", (2 * B, P, 2, KT, VW), F32).ap()
    VB = nc.dram_tensor("vb", (2 * B, P, 2, KT, HG * VW), F32).ap()
    OV = nc.dram_tensor("attended", (2 * B, 2, P, HALF), F32).ap()
    DN = nc.dram_tensor("denominators", (2 * B, 2, 2 * HG, HALF), F32).ap()
    RD = nc.dram_tensor("reciprocals", (2 * B, 2, 2 * HG, HALF), F32).ap()
    RR = nc.dram_tensor("relative_rows", (2, STEPS, P, RELROW), F32).ap()
    MD = nc.dram_tensor("maxima", (BODY, 3 * HG * 4, P), BF16).ap()
    BUF = nc.dram_tensor("expert_in", (E * CAP, D), F32).ap()
    YD = nc.dram_tensor("expert_out", (E * CAP, D), F32).ap()
    with ExitStack() as ctx:
        def sb(name, shape, dt=F32):
            return ctx.enter_context(nc.sbuf_tensor(name, shape, dt))

        identF, identB = sb("identF", [P, P]), sb("identB", [P, P], BF16)
        gate, gidx = sb("gate", [P, NT]), sb("gidx", [P, NT], U32)
        s, give_back = semaphores(nc, "id_zero id_one")
        once = ExitStack()
        zeros = once.enter_context(nc.sbuf_tensor("zeros", [P, CAP * E * D // P // (2 * B)], F32))
        clearing, clearing_done = semaphores(nc, "zeroed")
        with nc.Block() as block:
            @block.gpsimd
            def _(pool):
                nc.gpsimd.memset(identF[:, :], 0.0).then_inc(s["id_zero"], 1)
                pool.wait_ge(s["id_zero"], 1)
                nc.gpsimd.affine_select(out=identF[:, :], in_=identF[:, :], compare_op=ALU.not_equal,
                                        fill=1.0, base=0, pattern=[[-1, P]],
                                        channel_multiplier=1).then_inc(s["id_one"], 1)

            @block.vector
            def _(dve):
                nc.vector.memset(zeros[:, :], 0.0)
                dve.wait_ge(s["id_one"], 1)
                nc.vector.tensor_copy(identB[:, :], identF[:, :])
        give_back()
        wa = {"q": a_wq, "k": a_wk, "v": a_wv, "E": emb, "o": a_wo, "r": w_router}
        wb = {"q": b_wq, "k": b_wk, "v": b_wv, "bq": b_bq, "bk": b_bk, "bv": b_bv, "o": b_wo, "bo": b_bo,
              "r": w_router}
        we = {"gate": w_gate, "up": w_up, "down": w_down}

        project(nc, "A", x, None, wa, Q, KA, VA, identF, clear=(zeros, clearing["zeroed"], BUF, RR))
        clearing_done()
        once.close()
        attend(nc, "A", Q, KA, VA, OV, DN, emb, RR, MD, identF, identB)
        X = sb("X", [P, NT, D])
        moved = [ctx.enter_context(nc.semaphore(f"moved{k}")) for k in range(MOVES)]
        for kind, w, before in (("A", wa, 0), ("B", wb, 2 * 16 * (NT // MOVES))):
            if kind == "B":
                project(nc, "B", None, X, wb, Q, KB, VB, identF)
                attend(nc, "B", Q, KB, VB, OV, DN, None, None, MD, identF, identB)
            with nc.sbuf_tensor(f"XN_{kind}", [P, NT, D], F32) as XN, \
                    nc.sbuf_tensor(f"LG_{kind}", [P, NT, E], F32) as LG:
                after_attention(nc, kind, x, X, XN, LG, OV, DN, RD, w, identF)
                dispatch(nc, f"r{kind}", XN, LG, BUF, gate, gidx, moved, before)
            experts(nc, f"e{kind}", we, BUF, YD, identF)
            combine(nc, f"c{kind}", X, YD, gate, gidx, out if kind == "B" else None, moved,
                    before + 16 * (NT // MOVES))


_INS = ["L0_attn_a_x", "L0_attn_a_Wq", "L0_attn_a_Wk", "L0_attn_a_Wv", "L0_attn_a_Wo", "L0_attn_a_E",
        "L0_attn_b_wq", "L0_attn_b_bq", "L0_attn_b_wk", "L0_attn_b_bk", "L0_attn_b_wv", "L0_attn_b_bv",
        "L0_attn_b_wo", "L0_attn_b_bo", "L0_ffn_w_router", "L0_ffn_w_gate", "L0_ffn_w_up", "L0_ffn_w_down"]
_OUTS = [((8, 1024, 256), "float32")]


def kernel(**inputs):
    import numpy as _np
    import concourse.bacc as _bacc
    from concourse import mybir as _mybir
    from concourse.bass_utils import run_bass_kernel_spmd as _run

    nc = _bacc.Bacc("TRN2", target_bir_lowering=False, num_devices=1)
    arrays, args = {}, []
    for name in _INS:
        a = _np.ascontiguousarray(inputs[name][::-1] if name == "L0_attn_a_E" else inputs[name])
        arrays[f"in_{name}_dram"] = a
        args.append(nc.dram_tensor(f"in_{name}_dram", a.shape, _mybir.dt.from_np(a.dtype), kind="ExternalInput").ap())
    for i, (shape, dtype) in enumerate(_OUTS):
        dt = _mybir.dt.from_np(_np.dtype(dtype))
        args.append(nc.dram_tensor(f"out_{i}_dram", shape, dt, kind="ExternalOutput").ap())
    block_kernel(nc, *args)
    r = _run(nc, [arrays], core_ids=[0])
    return r.results[0]["out_0_dram"]
```

```python
from contextlib import ExitStack

import concourse.bass as bass
from concourse import mybir

F32 = mybir.dt.float32
BF16 = mybir.dt.bfloat16
I32 = mybir.dt.int32
U32 = mybir.dt.uint32
ALU = mybir.AluOpType
ACT = mybir.ActivationFunctionType
AX = mybir.AxisListType

P = 128
B, T, D = 8, 1024, 256
N = B * T
NT = N // P
H, HD = 16, 16
G = 4
HG = H // G
MAX_POS = 128
NREL = 2 * MAX_POS - 1
EPS = 1e-5
E = 32
CAP = 320
CHUNK = 512
CT = CHUNK // P
KT = T // P
SPLITS = 6
KR = SPLITS * HD
KM = KR + 3
VW = 2 * HD
REL = NREL - 1 + P
RELROW = 512
UNITS = B * G * 2
HALF = T // 2
STEPS = 16
BODY = 4
MOVES = 8


def semaphores(nc, names, **rings):
    stack, made = ExitStack(), {}
    for name in names.split():
        made[name] = stack.enter_context(nc.semaphore(name))
    every = list(made.values())
    for name, n in rings.items():
        made[name] = [stack.enter_context(nc.semaphore(f"{name}{k}")) for k in range(n)]
        every += made[name]

    def give_back():
        with nc.Block() as block:
            @block.sync
            def _(sp):
                for handle in every:
                    sp.sem_clear(handle)
        stack.close()

    return made, give_back


def wait(eng, sem, count):
    if not isinstance(count, int) or count > 0:
        eng.wait_ge(sem, count)


def wait_apart(eng, s, sem, count):
    wait(eng, sem, count)
    if not isinstance(count, int):
        eng.sem_inc(s["passed"], 1)


def load_transposed(nc, kind, weights, ident):
    s, give_back = semaphores(nc, "w_read w_turned w_copied")
    with ExitStack() as ctx:
        raws = [ctx.enter_context(nc.sbuf_tensor(f"{kind}_raw_{k}", [P, 2, D], F32)) for k in range(len(weights))]
        pt = ctx.enter_context(nc.psum_tensor(f"{kind}_w_pt", [P, 2, 4, P], F32))
        jobs = [(k, a) for k, (w, _, _) in enumerate(weights) for a in range(-(-w.shape[0] // P))]
        with nc.Block() as block:
            @block.sync
            def _(sp):
                for k, (w, _, _) in enumerate(weights):
                    rows = min(P, w.shape[0])
                    sp.dma_start(raws[k][0:rows, 0:w.shape[0] // rows, :],
                                 w.rearrange("(a p) d -> p a d", p=rows)).then_inc(s["w_read"], 16)

            @block.tensor
            def _(pe):
                pe.wait_ge(s["w_read"], 16 * len(weights))
                for n, (k, a) in enumerate(jobs):
                    rows = min(P, weights[k][0].shape[0])
                    wait(pe, s["w_copied"], n - 1)
                    for half in range(2):
                        last = nc.tensor.transpose(pt[:, n % 2, half, 0:rows],
                                                   raws[k][0:rows, a, half * P:(half + 1) * P],
                                                   ident[0:rows, 0:rows])
                    last.then_inc(s["w_turned"], 1)

            @block.vector
            def _(dve):
                for n, (k, a) in enumerate(jobs):
                    w, out, view = weights[k]
                    rows = min(P, w.shape[0])
                    dve.wait_ge(s["w_turned"], n + 1)
                    for half in range(2):
                        dst, src = view(out[:, half, a * rows:(a + 1) * rows], pt[:, n % 2, half, 0:rows])
                        last = nc.vector.tensor_copy(dst, src)
                    last.then_inc(s["w_copied"], 1)
    give_back()


def as_is(dst, src):
    return dst, src


def by_width(dst, src):
    return dst.rearrange("p (d h) -> p d h", d=HD), src.rearrange("p (h d) -> p d h", d=HD)


def by_half_width(dst, src):
    return (dst.rearrange("p (a d j) -> p a d j", a=2, d=HD),
            src.rearrange("p (a j d) -> p a d j", a=2, d=HD))


def normalize_steps(nc, s, xc, stats, mv, rstd, xn, k):
    for t in range(CT):
        last = nc.vector.bn_stats(stats[:, t, :], xc[:, t, :])
    last.then_inc(s["stat"], 1)
    wait_apart(nc.vector, s, s["stat"], 2 * k + 1)
    for t in range(CT):
        last = nc.vector.bn_aggr(mv[:, t, :], stats[:, t, :])
    last.then_inc(s["stat"], 1)
    nc.vector.wait_ge(s["stat"], 2 * k + 2)
    nc.vector.tensor_scalar(rstd[:, 0, :], mv[:, :, 1], EPS, None, ALU.add).then_inc(s["var"], 1)
    nc.vector.wait_ge(s["dev"], k + 1)
    nc.vector.reciprocal(rstd[:, 2, :], rstd[:, 1, :]).then_inc(s["rec"], 1)
    nc.vector.wait_ge(s["rec"], k + 1)
    for t in range(CT):
        last = nc.vector.tensor_scalar(xn[:, t, :], xc[:, t, :], mv[:, t, 0:1], rstd[:, 2, t:t + 1],
                                       ALU.subtract, ALU.mult)
    last.then_inc(s["xn_ready"], 1)


def project(nc, kind, x_dram, X, w, Q, K, V, ident, clear=None, tail=None):
    A = kind == "A"
    heads = G if A else H
    nv = heads * HD
    cols = V.shape[4]
    s, give_back = semaphores(nc, "w_in bias_in stat var dev rec xn_ready turned xt_ready mm v_mm q1 qf r1 q2 q3"
                   " v_ready bias_row bias_mm bias_col ones passed scaled combined", x_in=2, parts_out=4, v_out=2)
    with ExitStack() as ctx:
        def sb(name, shape, dt=F32):
            return ctx.enter_context(nc.sbuf_tensor(f"{kind}p_{name}", shape, dt))

        def psum(name, shape):
            return ctx.enter_context(nc.psum_tensor(f"{kind}p_{name}", shape, F32))

        nk = 64 if A else D
        wqT, wkT, wvT = sb("wqT", [P, 2, D]), sb("wkT", [P, 2, nk]), sb("wvT", [P, 2, nv])
        load_transposed(nc, kind, [(w["q"], wqT, by_width), (w["k"], wkT, by_half_width if A else by_width),
                             (w["v"], wvT, as_is)], ident)
        if A:
            tensors = [(0, P, 0.25, None), (1, P, 0.25, None), (2, nk, 1.0, 0), (2, nk, 1.0, 1)]
        else:
            tensors = [(0, P, 0.25, 0), (1, P, 0.25, 1), (2, P, 1.0, 2), (3, P, 1.0, 3)]
        products = [(wqT, 0, P), (wqT, P, P)] + ([(wkT, 0, nk)] if A else [(wkT, 0, P), (wkT, P, P)])
        xin = sb("xin", [P, 2, CT, D]) if A else None
        stats, mv, rstd = sb("stats", [P, CT, 6]), sb("mv", [P, CT, 2]), sb("rstd", [P, 3, CT])
        xn = sb("xn", [P, 2, CT, D])
        yt = None if A else sb("yt", [P, 2, CT, D])
        xT = sb("xT", [P, 2, 2, CHUNK])
        parts = sb("parts", [P, 4, 3, CHUNK], BF16)
        full, rest = sb("full", [P, 4, CHUNK]), sb("rest", [P, 4, CHUNK])
        vs = sb("vs", [P, 2, CT, heads, VW])
        brow, bprm, bcol = sb("brow", [1, 2, D]), sb("bprm", [1, 4, P]), sb("bcol", [P, 4])
        one = sb("one", [1, 1])
        bv = sb("bv", [P, nv])
        pT = psum("pT", [P, 2, CHUNK])
        pR = [psum(f"pR{k}", [P, CHUNK]) for k in range(len(products))]
        pV = psum("pV", [P, CT, nv])

        with nc.Block() as block:
            @block.sync
            def _(sp):
                if A:
                    sp.dma_start(brow[0:1, 0, 0:HD], w["E"][0:1, :]).then_inc(s["bias_in"], 16)
                    sp.dma_start(brow[0:1, 1, 0:HD], w["E"][NREL - 1:NREL, :]).then_inc(s["bias_in"], 16)
                else:
                    sp.dma_start(brow[0:1, 0, :], w["bq"].rearrange("(a n) -> a n", a=1)).then_inc(s["bias_in"], 16)
                    sp.dma_start(brow[0:1, 1, :], w["bk"].rearrange("(a n) -> a n", a=1)).then_inc(s["bias_in"], 16)
                    sp.dma_start(bv[:, :], w["bv"].rearrange("(a n) -> a n", a=1).broadcast_to([P, nv])).then_inc(s["w_in"], 16)
                    sp.wait_ge(s["w_in"], 16)

            @block.vector
            def _(dve):
                nc.vector.memset(one[:, :], 1.0)
                nc.vector.memset(vs[:, :, :, :, :], 1.0).then_inc(s["ones"], 1)
                dve.wait_ge(s["bias_in"], 32)
                for k in range(2 if A else 4):
                    if A:
                        dst = bprm[0:1, k, 0:nk].rearrange("o (a d j) -> o a d j", a=2, d=HD)
                        src = brow[0:1, k, 0:HD].unsqueeze(1).unsqueeze(3).broadcast_to([1, 2, HD, 2])
                    else:
                        dst = bprm[0:1, k, :].rearrange("o (d h) -> o d h", d=HD)
                        src = brow[0:1, k // 2, (k % 2) * P:(k % 2 + 1) * P].rearrange("o (h d) -> o d h", d=HD)
                    last = nc.vector.tensor_scalar(dst, src, 1.0 if A or k > 1 else 0.25, None, ALU.mult)
                last.then_inc(s["bias_row"], 1)
                dve.wait_ge(s["bias_mm"], 1)
                rows = nk if A else P
                nc.vector.tensor_copy(bcol[0:rows, 0:2 if A else 4], pT[0:rows, 0, 0:2 if A else 4]).then_inc(s["bias_col"], 1)

            @block.tensor
            def _(pe):
                pe.wait_ge(s["bias_row"], 1)
                rows = nk if A else P
                for k in range(2 if A else 4):
                    last = nc.tensor.matmul(pT[0:rows, 0, k:k + 1], bprm[0:1, k, 0:rows], one[0:1, 0:1],
                                            start=True, stop=True)
                last.then_inc(s["bias_mm"], 1)

        M = len(tensors)

        def part(m, rows, k):
            return parts[0:rows, m, k if m < 2 else 2 - k, :]


        def chunks(eng, stages, loop=True):
            def body(i):
                for j in (0, 1):
                    for lag, step in stages:
                        k = j + lag
                        if not isinstance(i, int) or 0 <= 2 * i + k < 2 * B:
                            step(2 * i + k, k % 2, i + k // 2)
            body(-1)
            body(0)
            if loop:
                with eng.Fori(1, B - 1) as i:
                    body(i)
            else:
                for i in range(1, B - 1):
                    body(i)
            body(B - 1)

        with nc.Block() as block:
            @block.sync
            def _(sp):
                def load(c, half, b):
                    wait_apart(sp, s, s["xn_ready"], c - 1)
                    sp.dma_start(xin[:, half, :, :],
                                 x_dram[b, half * HALF:(half + 1) * HALF, :]
                                 .rearrange("(t p) d -> p t d", p=P)).then_inc(s["x_in"][half], 16)

                def store(c, half, b):
                    wait_apart(sp, s, s["v_ready"], c + 1)
                    for g in range(G):
                        sp.dma_start(V[b * 2 + g // 2, :, g % 2, half * CT:(half + 1) * CT, :],
                                     vs[:, half, :, g * (heads // G):(g + 1) * (heads // G), :]
                                     .rearrange("p t h c -> p t (h c)")).then_inc(s["v_out"][half], 16)
                    tok = slice(half * HALF, (half + 1) * HALF)
                    for m, (_, rows, _, _) in enumerate(tensors):
                        wait_apart(sp, s, s["q3"], M * c + (m + 1))
                        if not A or m < 2:
                            dst = [(Q if m < 2 else K)[b * 2 + m % 2, :, :, tok]]
                            src = [parts[:, m, :, :]]
                        else:
                            dst = [K[m - 2, b * 2 + a, :, :, tok] for a in (0, 1)]
                            src = [parts[a * 32:(a + 1) * 32, m, :, :] for a in (0, 1)]
                        for o, i_ in zip(dst, src):
                            sp.dma_start(o.rearrange("s p t -> p s t"), i_).then_inc(s["parts_out"][m], 16)

                def clear_rows(c, half, b):
                    zeros, zeroed, buf, rel_rows = clear
                    for rows in (buf.rearrange("(b h p r) d -> b h p (r d)", b=B, h=2, p=P),
                                 rel_rows.rearrange("a s p c -> (a s p c)")
                                 .rearrange("(b h p n) -> b h p n", b=B, h=2, p=P)):
                        sp.dma_start(rows[b, half], zeros[:, 0:rows.shape[3]]).then_inc(zeroed, 16)

                chunks(sp, ([(2, load)] if A else []) + [(0, store)] + ([(0, clear_rows)] if clear else []))
                if clear:
                    sp.wait_ge(clear[1], 2 * 16 * 2 * B)
                for m in range(M):
                    sp.wait_ge(s["parts_out"][m], 16 * 2 * B * (2 if A and m > 1 else 1))
                for half in range(2):
                    sp.wait_ge(s["v_out"][half], 16 * G * B)

            @block.vector
            def _(dve):
                def combine_chunk(c, half, b):
                    _, gate, _, moved, before = tail
                    for t in range(CT):
                        wait_apart(dve, s, moved[half * CT + t], before + 16 * (b + 1))
                    nc.vector.tensor_tensor(yt[:, half, :, :], yt[:, half, :, :], gate[:, bass.ds(c * CT, CT)]
                                            .unsqueeze(2).broadcast_to([P, CT, D]), ALU.mult).then_inc(s["scaled"], 1)
                    wait_apart(dve, s, s["scaled"], c + 1)
                    rows = X[:, bass.ds(c * CT, CT), :]
                    nc.vector.tensor_tensor(rows, rows, yt[:, half, :, :], ALU.add).then_inc(s["combined"], 1)

                def norm(c, half, b):
                    if A:
                        dve.wait_ge(s["x_in"][half], 16 * (b + 1))
                        xc = xin[:, half, :, :]
                    else:
                        xc = X[:, bass.ds(c * CT, CT), :]
                        dve.wait_ge(s["combined"], c + 1)
                    wait_apart(dve, s, s["turned"], c - 1)
                    normalize_steps(nc, s, xc, stats, mv, rstd, xn[:, half, :, :], c)

                def split(c, half, b):
                    dve.wait_ge(s["v_mm"], c + 1)
                    wait(dve, s["v_out"][half], 16 * G * b)
                    src = pV[:, :, :].rearrange("p t (h d) -> p t h d", d=HD)
                    for t in range(CT):
                        if A:
                            last = nc.vector.tensor_copy(vs[:, half, t, :, 0:HD], src[:, t])
                        else:
                            last = nc.vector.tensor_tensor(vs[:, half, t, :, 0:HD], src[:, t],
                                                           bv[:, :].rearrange("p (h d) -> p h d", d=HD), ALU.add)
                    last.then_inc(s["v_ready"], 1)
                    for m, (prod, rows, scale, col) in enumerate(tensors):
                        dve.wait_ge(s["mm"], len(products) * c + (prod + 1))
                        wait(dve, s["r1"], M * c + (m + 1 - M))
                        nc.vector.tensor_scalar(full[0:rows, m, :], pR[prod][0:rows, :], scale,
                                                0.0 if col is None else bcol[0:rows, col:col + 1],
                                                ALU.mult, ALU.add).then_inc(s["qf"], 1)
                    for m, (prod, rows, scale, col) in enumerate(tensors):
                        dve.wait_ge(s["q2"], M * c + (m + 1))
                        nc.vector.tensor_tensor(part(m, rows, 2), rest[0:rows, m, :],
                                                part(m, rows, 1), ALU.subtract).then_inc(s["q3"], 1)

                chunks(dve, [(1, norm), (0, split)] + ([] if A else [(2, combine_chunk)]))

            @block.scalar
            def _(act):
                def root(c, half, b):
                    act.wait_ge(s["var"], c + 1)
                    nc.scalar.sqrt(rstd[:, 1, :], rstd[:, 0, :]).then_inc(s["dev"], 1)

                def copy(c, half, b):
                    act.wait_ge(s["turned"], c + 1)
                    wait(act, s["v_mm"], c - 1)
                    nc.scalar.copy(xT[:, half, :, :], pT[:, :, :]).then_inc(s["xt_ready"], 1)

                def first_parts(c, half, b):
                    for m, (prod, rows, scale, col) in enumerate(tensors):
                        act.wait_ge(s["qf"], M * c + (m + 1))
                        wait(act, s["parts_out"][m], (2 * b + half) * (32 if A and m > 1 else 16))
                        nc.scalar.copy(part(m, rows, 0), full[0:rows, m, :]).then_inc(s["q1"], 1)

                def second_parts(c, half, b):
                    for m, (prod, rows, scale, col) in enumerate(tensors):
                        act.wait_ge(s["r1"], M * c + (m + 1))
                        nc.scalar.copy(part(m, rows, 1), rest[0:rows, m, :]).then_inc(s["q2"], 1)

                chunks(act, [(1, root), (0, first_parts), (1, copy), (0, second_parts)])

            @block.gpsimd
            def _(pool):
                def split(c, half, b):
                    for m, (prod, rows, scale, col) in enumerate(tensors):
                        pool.wait_ge(s["q1"], M * c + (m + 1))
                        wait(pool, s["q3"], M * c + (m + 1 - M))
                        nc.gpsimd.tensor_tensor(rest[0:rows, m, :], full[0:rows, m, :],
                                                part(m, rows, 0), ALU.subtract).then_inc(s["r1"], 1)

                def gather(c, half, b):
                    yd, _, gidx, moved, _ = tail
                    wait(pool, s["combined"], c - 1)
                    for t in range(CT):
                        nc.gpsimd.indirect_dma_start(
                            out=yt[:, half, t, :], out_offset=None, in_=yd,
                            in_offset=bass.IndirectOffsetOnAxis(ap=gidx[:, c * CT + t:c * CT + t + 1], axis=0),
                            bounds_check=E * CAP - 1, oob_is_err=False).then_inc(moved[half * CT + t], 16)

                if A:
                    chunks(pool, [(0, split)])
                else:
                    chunks(pool, [(2, gather), (0, split)], loop=False)

            @block.tensor
            def _(pe):
                def turn(c, half, b):
                    pe.wait_ge(s["xn_ready"], c + 1)
                    wait(pe, s["xt_ready"], c)
                    for t in range(CT):
                        for d in range(2):
                            last = nc.tensor.transpose(pT[:, d, t * P:(t + 1) * P],
                                                       xn[:, half, t, d * P:(d + 1) * P], ident[:, :])
                    last.then_inc(s["turned"], 1)

                def multiply(c, half, b):
                    pe.wait_ge(s["xt_ready"], c + 1)
                    wait(pe, s["v_ready"], c)
                    for t in range(CT):
                        for d in range(2):
                            last = nc.tensor.matmul(pV[:, t, :], xT[:, half, d, t * P:(t + 1) * P],
                                                    wvT[:, d, :], start=(d == 0), stop=(d == 1))
                    last.then_inc(s["v_mm"], 1)
                    wait(pe, s["qf"], M * c)
                    for k, (wT, at, rows) in enumerate(products):
                        for d in range(2):
                            last = nc.tensor.matmul(pR[k][0:rows, :], wT[:, d, at:at + rows],
                                                    xT[:, half, d, :], start=(d == 0), stop=(d == 1))
                        last.then_inc(s["mm"], 1)

                chunks(pe, [(0, multiply), (1, turn)])
    give_back()


def relative_rows(nc, emb, rel, identF):
    s, give_back = semaphores(nc, "e_in e_turned e_copied e_diff e_parts e_placed")
    with ExitStack() as ctx:
        raw = ctx.enter_context(nc.sbuf_tensor("e_raw", [P, 2, HD], F32))
        eT = ctx.enter_context(nc.sbuf_tensor("e_T", [HD, 2 * P], F32))
        diff = ctx.enter_context(nc.sbuf_tensor("e_diff", [HD, 2, REL], F32))
        parts = ctx.enter_context(nc.sbuf_tensor("e_parts", [HD, 3, REL], BF16))
        pt = ctx.enter_context(nc.psum_tensor("e_pt", [P, 2, P], F32))
        with nc.Block() as block:
            @block.sync
            def _(sp):
                sp.dma_start(raw[:, 0, :], emb[0:P, :]).then_inc(s["e_in"], 16)
                sp.dma_start(raw[0:NREL - P, 1, :], emb[P:NREL, :]).then_inc(s["e_in"], 16)
                sp.wait_ge(s["e_parts"], 3)
                at = 0
                for part, rows in ((2, 1), (1, 1), (0, 1), (1, 1), (0, 1), (0, 1)):
                    sp.dma_start(rel[at:at + HD, :], parts[:, part, :]).then_inc(s["e_placed"], 16)
                    at += HD
                sp.wait_ge(s["e_placed"], 16 * SPLITS)

            @block.tensor
            def _(pe):
                pe.wait_ge(s["e_in"], 32)
                nc.tensor.transpose(pt[0:HD, 0, :], raw[:, 0, :], identF[:, :])
                nc.tensor.transpose(pt[0:HD, 1, 0:NREL - P], raw[0:NREL - P, 1, :],
                                    identF[0:NREL - P, 0:NREL - P]).then_inc(s["e_turned"], 1)

            @block.vector
            def _(dve):
                dve.wait_ge(s["e_turned"], 1)
                nc.vector.tensor_copy(eT[:, 0:NREL], pt[0:HD, :, :].rearrange("p a b -> p (a b)")[:, 0:NREL]).then_inc(s["e_copied"], 1)
                dve.wait_ge(s["e_copied"], 1)
                nc.vector.tensor_scalar(diff[:, 0, 0:NREL - 1], eT[:, 1:NREL], eT[:, 0:1], None, ALU.subtract)
                nc.vector.tensor_scalar(diff[:, 0, NREL - 1:REL], eT[:, NREL - 1:NREL].broadcast_to([HD, P]),
                                        eT[:, 0:1], None, ALU.subtract).then_inc(s["e_diff"], 1)
                dve.wait_ge(s["e_diff"], 1)
                nc.vector.tensor_copy(parts[:, 0, :], diff[:, 0, :]).then_inc(s["e_parts"], 1)
                dve.wait_ge(s["e_parts"], 1)
                nc.vector.tensor_tensor(diff[:, 1, :], diff[:, 0, :], parts[:, 0, :], ALU.subtract).then_inc(s["e_diff"], 1)
                dve.wait_ge(s["e_diff"], 2)
                nc.vector.tensor_copy(parts[:, 1, :], diff[:, 1, :]).then_inc(s["e_parts"], 1)
                dve.wait_ge(s["e_parts"], 2)
                nc.vector.tensor_tensor(parts[:, 2, :], diff[:, 1, :], parts[:, 1, :], ALU.subtract).then_inc(s["e_parts"], 1)
    give_back()


AHEAD_MAX = 24
AHEAD_REL = 34
AHEAD_REL_STORE = 32
AHEAD_REL_LOAD = 27


def attend(nc, kind, Q, K, V, OV, DN, emb, RR, MD, identF, identB):
    A = kind == "A"
    names = "max_full max_free kept nm_ready ms_a ms_ready mt_full mt_copied md_out st_full probs pv_done ot_copied passed"
    rings = dict(qs_in=BODY, m_in=BODY, ks_in=2, v_in=2, od_out=2)
    if A:
        names, rings = names + " rel_full rel_copied band_ready", dict(rings, rel_out=8, bias_in=4)
    s, give_back = semaphores(nc, names, **rings)
    NV = 1 if A else HG
    KV = 2
    with ExitStack() as ctx:
        def sb(name, shape, dt=F32):
            return ctx.enter_context(nc.sbuf_tensor(f"{kind}a_{name}", shape, dt))

        def psum(name, shape):
            return ctx.enter_context(nc.psum_tensor(f"{kind}a_{name}", shape, F32))

        qs = sb("qs", [KM, BODY, HG, HALF], BF16)
        ks = sb("ks", [KM, 2, KV if A else HG, T], BF16)
        vals = sb("vals", [P, 2, KT, NV, VW])
        probs = sb("probs", [P, 4, 2, HALF])
        osb = sb("osb", [P, 2, HALF])
        NPART = 3 if A else 2
        mpart = sb("mpart", [P, 2, HG, 4, NPART])
        nm = sb("nm", [P, 2, HG * 4])
        nrest = sb("nrest", [P, HG * 4])
        ms = sb("ms", [P, 3, HG * 4], BF16)
        mT = sb("mT", [3 * HG * 4, P], BF16)
        if A:
            rel = sb("rel", [KR, REL], BF16)
            relsb = sb("relsb", [P, 2, 2, REL])
            bias = sb("bias", [P, 4, 2, 3 * P])
            near = sb("near", [P, BODY, HG, 4, 3 * P])
            relative_rows(nc, emb, rel, identF)
        pE = psum("pE", [P, 2, 2, HALF])
        pM = psum("pM", [P, 2, HALF])
        pO = psum("pO", [P, HALF])
        pX = psum("pX", [P, HALF])

        with nc.Block() as block:
            @block.vector
            def _(dve):
                nc.vector.memset(ks[KR:KM, :, :, :], 1.0)

        def steps(eng, stages):
            def body(i):
                for k in range(BODY * STEPS):
                    for ahead, every, at, f in stages:
                        kk = k + ahead
                        if kk % every != at:
                            continue
                        if not isinstance(i, int) or 0 <= BODY * STEPS * i + kk < UNITS * STEPS:
                            f(i, kk)
            body(-1)
            body(0)
            with eng.Fori(1, UNITS // BODY - 1) as i:
                body(i)
            body(UNITS // BODY - 1)
            body(UNITS // BODY)

        def unit_of(i, kk):
            return BODY * i + kk // STEPS, (kk // STEPS) % BODY, kk % STEPS

        def step_of(i, kk):
            return BODY * STEPS * i + kk

        def window(kt_or_block, qh_block):
            return [r for r in (-1, 0, 1) if 0 <= qh_block + r < KT]

        with nc.Block() as block:
            @block.sync
            def _(sp):
                def load_queries(i, kk):
                    u, slot, _ = unit_of(i, kk)
                    body = i + kk // (STEPS * BODY)
                    wait_apart(sp, s, s["st_full"], STEPS * (u - BODY + 1))
                    qh, jj = slot % 2, slot // 2
                    at = 0
                    for parts in (3, 2, 1):
                        src = Q.rearrange("i s (d h) t -> i s d h t", d=HD)[
                            body, 0:parts, :, jj * HG:(jj + 1) * HG, qh * HALF:(qh + 1) * HALF]
                        sp.dma_start(qs[at:at + parts * HD, slot, :, :],
                                     src.rearrange("s d h t -> (s d) h t")).then_inc(s["qs_in"][slot], 16)
                        at += parts * HD

                def load_keys(i, kk):
                    u, slot, _ = unit_of(i, kk)
                    body = i + kk // (STEPS * BODY)
                    jj = slot // 2
                    wait_apart(sp, s, s["st_full"], STEPS * (u - 2))
                    at = 0
                    for parts in (3, 2, 1):
                        if A:
                            src = K.rearrange("v i s (d g) t -> i s d g v t", d=HD)[
                                body, 3 - parts:3, :, jj, :, :].rearrange("s d v t -> (s d) v t")
                        else:
                            src = K.rearrange("i s (d h) t -> i s d h t", d=HD)[
                                body, 3 - parts:3, :, jj * HG:(jj + 1) * HG, :].rearrange("s d h t -> (s d) h t")
                        sp.dma_start(ks[at:at + parts * HD, jj, :, :], src).then_inc(s["ks_in"][jj], 16)
                        at += parts * HD

                def load_values(i, kk):
                    u, slot, _ = unit_of(i, kk)
                    body = i + kk // (STEPS * BODY)
                    jj = slot // 2
                    wait_apart(sp, s, s["pv_done"], KT * (u - 2))
                    sp.dma_start(vals[:, jj, :, :, :].rearrange("p k h c -> p (k h c)"),
                                 V[body, :, jj, :, :].rearrange("p k c -> p (k c)")).then_inc(s["v_in"][jj], 16)

                def store_relative(i, kk):
                    u, slot, st = unit_of(i, kk)
                    g = step_of(i, kk)
                    wait_apart(sp, s, s["rel_copied"], g + 1)
                    wait_apart(sp, s, s["max_free"], 2 * (g - 2 * STEPS + 1))
                    sp.dma_start(RR[slot % 2, st - 1:st + 1, :, P + 1:P + 1 + REL].rearrange("q p c -> p q c"),
                                 relsb[:, (kk // 2) % 2, :, :]).then_inc(s["rel_out"][(kk // 2) % 8], 16)

                def load_relative(i, kk):
                    u, slot, st = unit_of(i, kk)
                    body = i + kk // (STEPS * BODY)
                    g = step_of(i, kk)
                    pair = kk // 2
                    wait_apart(sp, s, s["rel_out"][pair % 8], 16 * (4 * i + pair // 8 + 1))
                    wait_apart(sp, s, s["max_free"], 2 * (g - 7))
                    base = RR[slot % 2, st - 1:st + 1, :, :]
                    src = bass.AP(tensor=base.tensor, offset=base.offset + P - 1,
                                  ap=[[RELROW - 1, P], [P * RELROW, 2], [1, 3 * P]])
                    sp.dma_start(bias[:, pair % 4, :, :], src).then_inc(s["bias_in"][pair % 4], 16)

                def store_max(i, kk):
                    u, slot, _ = unit_of(i, kk)
                    wait_apart(sp, s, s["mt_copied"], u + 1)
                    sp.dma_start(MD[slot], mT[:, :]).then_inc(s["md_out"], 16)

                def load_max(i, kk):
                    u, slot, _ = unit_of(i, kk)
                    wait_apart(sp, s, s["md_out"], 16 * (u + 1))
                    wait_apart(sp, s, s["st_full"], STEPS * (u - BODY + 1))
                    sp.dma_start(qs[KR:KM, slot, :, :].rearrange("s h t -> s (h t)"),
                                 MD[slot].rearrange("(s r) q -> s (r q)", s=3)).then_inc(s["m_in"][slot], 16)

                rel_stages = [(AHEAD_REL_STORE, 2, 1, store_relative), (AHEAD_REL_LOAD, 2, 1, load_relative)] if A else []
                steps(sp, rel_stages + [(3 * STEPS - 2, STEPS, 0, load_queries),
                                        (2 * STEPS - 2, 2 * STEPS, 0, load_keys),
                                        (2 * STEPS - 4, 2 * STEPS, 0, load_values),
                                        (5, STEPS, 0, store_max), (3, STEPS, 0, load_max)])
                for k in range(2):
                    sp.wait_ge(s["od_out"][k], 16 * (HG + 1) * UNITS // 2)

            def far_runs(q):
                runs = [(0, 0, q - 1), (1, q + 2, KT - q - 2)]
                return [r for r in runs if r[2] > 0]

            @block.tensor
            def _(pe):
                def relative(i, kk):
                    u, slot, st = unit_of(i, kk)
                    g = step_of(i, kk)
                    if st == 0:
                        wait(pe, s["qs_in"][slot], 48 * (i + kk // (STEPS * BODY) + 1))
                    wait(pe, s["rel_copied"], g)
                    wait(pe, s["mt_copied"], mt_before(i, kk - AHEAD_REL))
                    h, q = st // 4, st % 4
                    nc.tensor.matmul(pX[:, 0:REL], qs[0:KR, slot, h, q * P:(q + 1) * P], rel[:, :],
                                     start=True, stop=True).then_inc(s["rel_full"], 1)

                def mt_before(i, k):
                    return BODY * i + (k + 7 + STEPS - 1) // STEPS

                def maximum(i, kk, half):
                    u, slot, st = unit_of(i, kk)
                    g = step_of(i, kk)
                    h, qb = st // 4, st % 4
                    q = (slot % 2) * 4 + qb
                    jj = slot // 2
                    body = i + kk // (STEPS * BODY)
                    if st == 0 and half == 0:
                        wait(pe, s["qs_in"][slot], 48 * (body + 1))
                        if slot % 2 == 0:
                            wait(pe, s["ks_in"][jj], 48 * (body + 1))
                    query = qs[0:KR, slot, h, qb * P:(qb + 1) * P]
                    if A:
                        runs = []
                        col = 0
                        for v, first, n in far_runs(q):
                            while n:
                                m = min(n, 4 - col % 4)
                                runs.append((col, v, first, m))
                                col, first, n = col + m, first + m, n - m
                        near_blocks = window(0, q)
                        runs.append((8 - len(near_blocks), 0, q + near_blocks[0], len(near_blocks)))
                        wait(pe, s["max_free"], 2 * g + (half - 1))
                        for c, v, first, m in [r for r in runs if r[0] // 4 == half]:
                            last = nc.tensor.matmul(pM[:, half, (c % 4) * P:(c % 4 + m) * P], query,
                                                    ks[0:KR, jj, v, first * P:(first + m) * P],
                                                    start=True, stop=True)
                        last.then_inc(s["max_full"], 1)
                    else:
                        wait(pe, s["max_free"], 2 * g + (half - 1))
                        nc.tensor.matmul(pM[:, half, :], query, ks[0:KR, jj, h, half * HALF:(half + 1) * HALF],
                                         start=True, stop=True).then_inc(s["max_full"], 1)

                def turn_max(i, kk):
                    u, slot, _ = unit_of(i, kk)
                    pe.wait_ge(s["ms_ready"], u + 1)
                    wait(pe, s["mt_copied"], u)
                    if A:
                        wait(pe, s["rel_copied"], min(step_of(i, kk) - 7 + AHEAD_REL + 1, UNITS * STEPS)
                             if isinstance(i, int) else step_of(i, kk) - 7 + AHEAD_REL + 1)
                    nc.tensor.matmul(pX[0:3 * HG * 4, 0:P], ms[:, :, :].rearrange("p s r -> p (s r)"),
                                     identB[:, :], start=True, stop=True).then_inc(s["mt_full"], 1)

                def scores(i, kk, hh):
                    u, slot, st = unit_of(i, kk)
                    g = step_of(i, kk)
                    kt, pair = st // 2, st % 2
                    jj = slot // 2
                    if st == 0 and hh == 0:
                        wait(pe, s["m_in"][slot], 16 * (i + kk // (STEPS * BODY) + 1))
                        if A:
                            wait(pe, s["band_ready"], HG * (u + 1))
                    if hh == 0:
                        wait(pe, s["probs"], g - 1)
                    h = 2 * pair + hh
                    out = pE[:, kk % 2, hh, :]
                    if not A:
                        last = nc.tensor.matmul(out, ks[0:KM, jj, h, kt * P:(kt + 1) * P],
                                                qs[0:KM, slot, h, :], start=True, stop=True)
                        if hh == 1:
                            last.then_inc(s["st_full"], 1)
                        return
                    first = (slot % 2) * 4
                    left = [b for b in range(4) if first + b >= kt + 2]
                    right = [b for b in range(4) if first + b <= kt - 2]
                    for v, blocks in ((0, left), (1, right)):
                        if blocks:
                            cols = slice(blocks[0] * P, (blocks[-1] + 1) * P)
                            last = nc.tensor.matmul(out[:, cols], ks[0:KM, jj, v, kt * P:(kt + 1) * P],
                                                    qs[0:KM, slot, h, cols], start=True, stop=True)
                    for b in range(4):
                        r = kt - (first + b)
                        if abs(r) <= 1:
                            last = nc.tensor.transpose(out[:, b * P:(b + 1) * P],
                                                       near[:, slot, h, b, (r + 1) * P:(r + 2) * P], identF[:, :])
                    if hh == 1:
                        last.then_inc(s["st_full"], 1)

                def weigh(i, kk, part):
                    u, slot, st = unit_of(i, kk)
                    g = step_of(i, kk)
                    kt, jj = st // 2, slot // 2
                    if st == 1 and part == 0:
                        if slot % 2 == 0:
                            wait(pe, s["v_in"][jj], 16 * (i + kk // (STEPS * BODY) + 1))
                        wait(pe, s["ot_copied"], u)
                    if part == 0:
                        pe.wait_ge(s["probs"], g + 1)
                    cols = slice(part * HALF // 2, (part + 1) * HALF // 2)
                    for h in range(HG):
                        last = nc.tensor.matmul(pO[h * VW:(h + 1) * VW, cols], vals[:, jj, kt, 0 if A else h, :],
                                                probs[:, (kk - 1 + h // 2) % 4, h % 2, cols],
                                                start=(kt == 0 and part == 0),
                                                stop=(kt == KT - 1 and part == 1), tile_position=(0, h * VW))
                    if part == 1:
                        last.then_inc(s["pv_done"], 1)

                def halves(step):
                    return [lambda i, kk: step(i, kk, 0), lambda i, kk: step(i, kk, 1)]

                order = []
                for odd in range(2):
                    (s0, s1), (m0, m1) = [[(ahead, 2, odd, f) for f in halves(step)]
                                          for ahead, step in ((0, scores), (AHEAD_MAX, maximum))]
                    w = (-2, 2, 1, halves(weigh)[0]) if odd else (-3, 2, 1, halves(weigh)[1])
                    turn = [(7, STEPS, 0, turn_max)] if odd else []
                    if A:
                        order += [s0, w, (AHEAD_REL, 2, odd, relative), m0, s1, m1] + turn
                    else:
                        order += [s0, m0, s1, m1] + turn + [w]
                steps(pe, order)

            @block.vector
            def _(dve):
                def maximum(i, kk):
                    u, slot, st = unit_of(i, kk)
                    g = step_of(i, kk)
                    h, qb = st // 4, st % 4
                    q = (slot % 2) * 4 + qb
                    s2 = slot % 2
                    if st == 0:
                        wait(dve, s["nm_ready"], HG * (u - 1))
                        if A:
                            wait(dve, s["band_ready"], HG * (u - 1))
                            wait(dve, s["st_full"], STEPS * (u - BODY + 1))
                    part = mpart[:, s2, h, qb, :]
                    dve.wait_ge(s["max_full"], 2 * g + 1)
                    nc.vector.reduce_max(part[:, 0:1], pM[:, 0, :], AX.X).then_inc(s["max_free"], 1)
                    dve.wait_ge(s["max_full"], 2 * g + 2)
                    if A:
                        blocks = window(0, q)
                        far = (4 - len(blocks)) * P
                        lo = (blocks[0] + 1) * P
                        pair = kk // 2
                        wait(dve, s["bias_in"][pair % 4], 16 * (8 * i + pair // 4 + 1))
                        nc.vector.reduce_max(part[:, 1:2], pM[:, 1, 0:far], AX.X)
                        nc.vector.tensor_tensor_reduce(out=near[:, slot, h, qb, lo:lo + len(blocks) * P],
                                                       in0=pM[:, 1, far:HALF],
                                                       in1=bias[:, pair % 4, kk % 2, lo:lo + len(blocks) * P],
                                                       scale=1.0, scalar=-3.0e38, op0=ALU.add, op1=ALU.max,
                                                       accum_out=part[:, 2:3]).then_inc(s["max_free"], 1)
                    else:
                        nc.vector.reduce_max(part[:, 1:2], pM[:, 1, :], AX.X).then_inc(s["max_free"], 1)
                    if qb == 3:
                        dve.wait_ge(s["max_free"], 2 * g + 2)
                        nc.vector.reduce_max(nm[:, s2, h * 4:(h + 1) * 4], mpart[:, s2, h, :, :], AX.X,
                                             negate=True).then_inc(s["nm_ready"], 1)
                    if st == STEPS - 1:
                        dve.wait_ge(s["nm_ready"], HG * (u + 1))
                        wait(dve, s["mt_full"], u)
                        nc.vector.tensor_copy(ms[:, 0, :], nm[:, s2, :]).then_inc(s["ms_a"], 1)
                        dve.wait_ge(s["ms_a"], 3 * u + 1)
                        nc.vector.tensor_tensor(nrest[:, :], nm[:, s2, :], ms[:, 0, :], ALU.subtract).then_inc(s["ms_a"], 1)
                        dve.wait_ge(s["ms_a"], 3 * u + 2)
                        nc.vector.tensor_copy(ms[:, 1, :], nrest[:, :]).then_inc(s["ms_a"], 1)
                        dve.wait_ge(s["ms_a"], 3 * u + 3)
                        nc.vector.tensor_tensor(ms[:, 2, :], nrest[:, :], ms[:, 1, :], ALU.subtract).then_inc(s["ms_ready"], 1)

                steps(dve, [(AHEAD_MAX, 1, 0, maximum)])

            @block.gpsimd
            def _(pool):
                def band(i, kk):
                    u, slot, st = unit_of(i, kk)
                    h, qh = st // 4, slot % 2
                    pool.wait_ge(s["nm_ready"], HG * u + h + 1)
                    edge, lo = (0, P) if qh == 0 else (3, 0)
                    rest = slice(1, 4) if qh == 0 else slice(0, 3)
                    m = nm[:, qh, h * 4:(h + 1) * 4]
                    one = near[:, slot, h, edge, lo:lo + 2 * P]
                    nc.gpsimd.tensor_tensor(one, one, m[:, edge:edge + 1].broadcast_to([P, 2 * P]), ALU.add)
                    three = near[:, slot, h, rest, :]
                    nc.gpsimd.tensor_tensor(three, three, m[:, rest].unsqueeze(2).broadcast_to([P, 3, 3 * P]),
                                            ALU.add).then_inc(s["band_ready"], 1)

                if A:
                    steps(pool, [(AHEAD_MAX, 4, 3, band)])

            @block.scalar
            def _(act):
                def copy_relative(i, kk):
                    g = step_of(i, kk)
                    pair = kk // 2
                    act.wait_ge(s["rel_full"], g + 1)
                    if kk % 2 == 0:
                        wait(act, s["rel_out"][(pair - 2) % 8], 16 * (4 * i + (pair - 2) // 8 + 1))
                    nc.scalar.copy(relsb[:, pair % 2, kk % 2, :], pX[:, 0:REL]).then_inc(s["rel_copied"], 1)

                def copy_max(i, kk):
                    u, slot, _ = unit_of(i, kk)
                    act.wait_ge(s["mt_full"], u + 1)
                    wait(act, s["md_out"], 16 * u)
                    nc.scalar.copy(mT[:, :], pX[0:3 * HG * 4, 0:P]).then_inc(s["mt_copied"], 1)

                def exp(i, kk):
                    g = step_of(i, kk)
                    act.wait_ge(s["st_full"], g + 1)
                    wait(act, s["pv_done"], 32 * i + kk // 2 - 1)
                    nc.scalar.activation(probs[:, kk % 4, :, :], pE[:, kk % 2, :, :], ACT.Exp).then_inc(s["probs"], 1)

                def copy_out(i, kk):
                    u, slot, _ = unit_of(i, kk)
                    act.wait_ge(s["pv_done"], KT * (u + 1))
                    wait(act, s["od_out"][slot % 2], 16 * (HG + 1) * (2 * i + (kk // STEPS) // 2))
                    nc.scalar.copy(osb[:, slot % 2, :], pO[:, :]).then_inc(s["ot_copied"], 1)

                def store_out(i, kk):
                    u, slot, _ = unit_of(i, kk)
                    body = i + kk // (STEPS * BODY)
                    wait_apart(act, s, s["ot_copied"], u + 1)
                    qh, jj, h = slot % 2, slot // 2, kk % STEPS
                    row = (jj * HG + h) * HD
                    act.dma_start(OV[body, qh, row:row + HD],
                                  osb[h * VW:h * VW + HD, slot % 2, :]).then_inc(s["od_out"][slot % 2], 16)
                    if h == HG - 1:
                        act.dma_start(DN[body, qh, jj * HG:(jj + 1) * HG],
                                      osb[HD:P:VW, slot % 2, :]).then_inc(s["od_out"][slot % 2], 16)

                steps(act, ([(AHEAD_REL, 1, 0, copy_relative)] if A else [])
                      + [(7, STEPS, 0, copy_max), (0, 1, 0, exp), (-STEPS - 2, STEPS, 0, copy_out)]
                      + [(-STEPS - 3, STEPS, h, store_out) for h in range(HG)])
    give_back()


def chunk_loop(eng, stages, n, loop=True):
    def body(i):
        for j in range(n):
            for lag, step in stages:
                k = j + lag
                if not isinstance(i, int) or 0 <= n * i + k < 2 * B:
                    step(n * i + k, k % n, k % 2, (n // 2) * i + k // 2, i + k // n)
    body(-1)
    body(0)
    if loop:
        with eng.Fori(1, 2 * B // n - 1) as i:
            body(i)
    else:
        for i in range(1, 2 * B // n - 1):
            body(i)
    body(2 * B // n - 1)
    body(2 * B // n)


def after_attention(nc, kind, x_dram, X, OV, DN, RD, w, identF, BUF, gate, gidx, sent, before):
    A = kind == "A"
    BN = 4
    ROWS = 2 * B * 2 * 2 * HG // P
    s, give_back = semaphores(
        nc, "w_in dn_in inverted rd_out divided wo_mm added stat var dev rec xn_ready passed turned xt_ready"
        " routed shifted summed bias_in biased"
        " mask iota set choosing ranking oh cum ranked row placed weighed", o_in=BN, d_in=2, x_in=2)
    with ExitStack() as ctx:
        def sb(name, shape, dt=F32):
            return ctx.enter_context(nc.sbuf_tensor(f"{kind}o_{name}", shape, dt))

        def psum(name, shape):
            return ctx.enter_context(nc.psum_tensor(f"{kind}o_{name}", shape, F32))

        woT = sb("woT", [P, 2, D])
        wr = sb("wr", [P, 2, E])
        load_transposed(nc, f"{kind}o", [(w["o"], woT, as_is)], identF)
        dens = sb("dens", [P, ROWS, HALF])
        osl, den = sb("osl", [P, BN, 2, CHUNK]), sb("den", [P, 2, 2, CHUNK])
        xin = sb("xin", [P, 2, CT, D]) if A else None
        stats, mv, rstd = sb("stats", [P, CT, 6]), sb("mv", [P, CT, 2]), sb("rstd", [P, 3, CT])
        xn = sb("xn", [P, BN, CT, D])
        xT = sb("xT", [P, 2, CHUNK])
        LG = sb("LG", [P, NT, E])
        upper = sb("upper", [P, P], BF16)
        allone = sb("allone", [P, P], BF16)
        ei = sb("ei", [P, E])
        eint = sb("eint", [P, E], I32)
        w3, w1 = sb("w3", [P, CT, E]), sb("w1", [P, CT, E])
        weights, total = sb("weights", [P, NT, E]), sb("total", [P, 2, NT])
        onehot = sb("onehot", [P, 2, CT * E], BF16)
        carry = sb("carry", [P, E])
        choice = sb("choice", [P, 2, 2, CT])
        small = sb("small", [P, 4, CT])
        sidx = sb("sidx", [P, NT], U32)
        bo = sb("bo", [P, D])
        pW = psum("pW", [P, 2, CT, D])
        pT = psum("pT", [P, 2, CHUNK])
        pL = psum("pL", [P, CT, E])
        pC = psum("pC", [P, (CT + 1) * E])

        def tiles(c):
            return bass.ds(c * CT, CT)

        with nc.Block() as block:
            @block.sync
            def _(sp):
                flat = [d.rearrange("i q h t -> (i q h) t").rearrange("(a p) t -> p a t", p=P) for d in (DN, RD)]
                sp.dma_start(dens[:, :, :], flat[0]).then_inc(s["dn_in"], 16)
                sp.dma_start(wr[:, :, :], w["r"].rearrange("(a p) e -> p a e", p=P)).then_inc(s["w_in"], 16)
                if not A:
                    sp.dma_start(bo[:, :], w["bo"].rearrange("(a n) -> a n", a=1)
                                 .broadcast_to([P, D])).then_inc(s["bias_in"], 16)
                sp.wait_ge(s["inverted"], 1)
                sp.dma_start(flat[1], dens[:, :, :]).then_inc(s["rd_out"], 16)
                sp.wait_ge(s["rd_out"], 16)

                def load(c, slot, half, b, body):
                    wait_apart(sp, s, s["wo_mm"], c - BN + 1)
                    sp.dma_start(osl[:, slot, :, :], OV.rearrange("(b g) q p t -> b q p g t", g=2)
                                 [b, half]).then_inc(s["o_in"][slot], 16)

                def load_reciprocals(c, slot, half, b, body):
                    wait_apart(sp, s, s["divided"], c - 1)
                    for g in range(2):
                        src = RD.rearrange("(b g) q h t -> b g q h t", g=2)[b, g, half]
                        sp.dma_start(den[:, half, g, :],
                                     src.unsqueeze(1).broadcast_to([2 * HG, HD, CHUNK])).then_inc(s["d_in"][half], 16)

                def load_x(c, slot, half, b, body):
                    wait_apart(sp, s, s["added"], c - 1)
                    sp.dma_start(xin[:, half, :, :], x_dram[b, half * HALF:(half + 1) * HALF, :]
                                 .rearrange("(t p) d -> p t d", p=P)).then_inc(s["x_in"][half], 16)

                chunk_loop(sp, [(3, load), (2, load_reciprocals)] + ([(1, load_x)] if A else []), BN)

            @block.vector
            def _(dve):
                dve.wait_ge(s["dn_in"], 16)
                nc.vector.reciprocal(dens[:, :, :], dens[:, :, :]).then_inc(s["inverted"], 1)

                def link(sem, count, ins):
                    ins.then_inc(sem, 1)
                    wait_apart(dve, s, sem, count)

                top = small[:, 0, :]
                eis = ei[:, :].unsqueeze(1).broadcast_to([P, CT, E])

                def over_e(ap):
                    return ap.unsqueeze(2).broadcast_to([P, CT, E])

                nc.vector.memset(carry[:, :], 0.0)
                dve.wait_ge(s["iota"], 1)
                nc.vector.tensor_copy(ei[:, :], eint[:, :]).then_inc(s["set"], 1)
                dve.wait_ge(s["set"], 1)

                def choose(c, slot, half, b, body):
                    dve.wait_ge(s["routed"], c + 1)
                    link(s["choosing"], 4 * c + 1, nc.vector.reduce_max(top, pL[:, :, :], AX.X))
                    nc.vector.tensor_tensor(LG[:, tiles(c), :], pL[:, :, :], over_e(top),
                                            ALU.subtract).then_inc(s["shifted"], 1)
                    wait_apart(dve, s, s["shifted"], c + 1)
                    link(s["choosing"], 4 * c + 2, nc.vector.tensor_scalar(w3[:, :, :], LG[:, tiles(c), :], 0.0, None, ALU.is_ge))
                    link(s["choosing"], 4 * c + 3, nc.vector.tensor_tensor(w3[:, :, :], w3[:, :, :], eis, ALU.mult))
                    wait(dve, s["placed"], c - 1)
                    first = choice[:, half, 0, :]
                    link(s["choosing"], 4 * c + 4, nc.vector.tensor_reduce(first, w3[:, :, :], AX.X, ALU.min))
                    nc.vector.tensor_tensor(onehot[:, half, :].rearrange("p (t e) -> p t e", e=E), eis, over_e(first),
                                            ALU.is_equal).then_inc(s["oh"], 1)

                def rank(c, slot, half, b, body):
                    dve.wait_ge(s["cum"], c + 1)
                    wait_apart(dve, s, s["ranked"], c)
                    counts = pC[:, 0:CT * E].rearrange("p (t e) -> p t e", e=E)
                    link(s["ranking"], 3 * c + 1, nc.vector.tensor_tensor(w1[:, :, :], counts,
                                                       carry[:, :].unsqueeze(1).broadcast_to([P, CT, E]), ALU.add))
                    link(s["ranking"], 3 * c + 2, nc.vector.tensor_tensor(carry[:, :], carry[:, :], pC[:, CT * E:], ALU.add))
                    link(s["ranking"], 3 * c + 3, nc.vector.tensor_tensor(w1[:, :, :], w1[:, :, :],
                                                       onehot[:, half, :].rearrange("p (t e) -> p t e", e=E), ALU.mult))
                    nc.vector.reduce_sum(choice[:, half, 1, :], w1[:, :, :], AX.X).then_inc(s["ranked"], 1)

                def divide(c, slot, half, b, body):
                    dve.wait_ge(s["o_in"][slot], 16 * (body + 1))
                    dve.wait_ge(s["d_in"][half], 32 * (b + 1))
                    nc.vector.tensor_tensor(osl[:, slot, :, :], osl[:, slot, :, :], den[:, half, :, :],
                                            ALU.mult).then_inc(s["divided"], 1)

                def add(c, slot, half, b, body):
                    dve.wait_ge(s["wo_mm"], c + 1)
                    if A:
                        dve.wait_ge(s["x_in"][half], 16 * (b + 1))
                    else:
                        dve.wait_ge(s["biased"], c + 1)
                    nc.vector.tensor_tensor(X[:, tiles(c), :], xin[:, half, :, :] if A else X[:, tiles(c), :],
                                            pW[:, half, :, :], ALU.add).then_inc(s["added"], 1)
                    dve.wait_ge(s["added"], c + 1)
                    wait(dve, s["turned"], c - BN + 1)
                    if not isinstance(body, int) or body > 0:
                        for t in range(CT):
                            wait_apart(dve, s, sent[slot * CT + t], before + 16 * body)
                    wait_apart(dve, s, s["summed"], c - BN + 1)
                    normalize_steps(nc, s, X[:, tiles(c), :], stats, mv, rstd, xn[:, slot, :, :], c)

                chunk_loop(dve, [(2, divide), (0, add), (-1, choose), (-2, rank)], BN)
                dve.wait_ge(s["weighed"], 1)
                nc.vector.reduce_sum(total[:, 0, :], weights[:, :, :], AX.X).then_inc(s["weighed"], 1)
                dve.wait_ge(s["weighed"], 2)
                nc.vector.reciprocal(total[:, 1, :], total[:, 0, :]).then_inc(s["weighed"], 1)
                dve.wait_ge(s["weighed"], 3)
                dve.wait_ge(s["placed"], 2 * B)
                nc.vector.tensor_tensor(gate[:, :], gate[:, :], total[:, 1, :], ALU.mult)

            @block.gpsimd
            def _(pool):
                def add_normalized(c, slot, half, b, body):
                    wait_apart(pool, s, s["xn_ready"], c + 1)
                    nc.gpsimd.tensor_tensor(X[:, tiles(c), :], X[:, tiles(c), :], xn[:, slot, :, :],
                                            ALU.add).then_inc(s["summed"], 1)

                def add_bias(c, slot, half, b, body):
                    nc.gpsimd.tensor_tensor(X[:, tiles(c), :], X[:, tiles(c), :],
                                            bo[:, :].unsqueeze(1).broadcast_to([P, CT, D]),
                                            ALU.add).then_inc(s["biased"], 1)

                def place(c, slot, half, b, body):
                    def link(n, ins):
                        ins.then_inc(s["row"], 1)
                        pool.wait_ge(s["row"], 4 * c + n)

                    first, rank, row, past, last_row = choice[:, half, 0, :], choice[:, half, 1, :], *(
                        small[:, k, :] for k in (1, 2, 3))
                    here = slice(c * CT, (c + 1) * CT)
                    pool.wait_ge(s["ranked"], c + 1)
                    nc.gpsimd.tensor_scalar(gate[:, here], rank, float(CAP), None, ALU.is_le)
                    link(1, nc.gpsimd.tensor_scalar(row, first, float(CAP), float(E * CAP - 1), ALU.mult, ALU.add))
                    nc.gpsimd.tensor_tensor(row, row, rank, ALU.add)
                    link(2, nc.gpsimd.tensor_scalar(past, gate[:, here], -65536.0, 65536.0, ALU.mult, ALU.add))
                    link(3, nc.gpsimd.tensor_tensor(row, row, past, ALU.add))
                    link(4, nc.gpsimd.tensor_scalar(last_row, row, float(E * CAP - 1), None, ALU.min))
                    nc.gpsimd.tensor_copy(gidx[:, here], last_row)
                    nc.gpsimd.tensor_copy(sidx[:, here], row).then_inc(s["placed"], 1)

                def scatter(c, slot, half, b, body):
                    pool.wait_ge(s["placed"], c + 1)
                    for t in range(CT):
                        nc.gpsimd.indirect_dma_start(
                            out=BUF, out_offset=bass.IndirectOffsetOnAxis(ap=sidx[:, c * CT + t:c * CT + t + 1], axis=0),
                            in_=xn[:, slot, t, :], in_offset=None, bounds_check=E * CAP - 1,
                            oob_is_err=False).then_inc(sent[slot * CT + t], 16)

                nc.gpsimd.iota(eint[:, :], [[1, E]], base=-E, channel_multiplier=0).then_inc(s["iota"], 1)
                nc.gpsimd.memset(upper[:, :], 1.0)
                nc.gpsimd.memset(allone[:, :], 1.0).then_inc(s["mask"], 1)
                pool.wait_ge(s["mask"], 1)
                nc.gpsimd.affine_select(out=upper[:, :], in_=upper[:, :], compare_op=ALU.is_ge, fill=0.0,
                                        base=0, pattern=[[1, P]], channel_multiplier=-1).then_inc(s["mask"], 1)
                if not A:
                    pool.wait_ge(s["bias_in"], 16)
                chunk_loop(pool, ([] if A else [(2, add_bias)]) + [(-2, place), (-2, scatter), (0, add_normalized)], BN, loop=False)
                for sem in sent:
                    pool.wait_ge(sem, before + 16 * (NT // len(sent)))

            @block.scalar
            def _(act):
                def root(c, slot, half, b, body):
                    act.wait_ge(s["var"], c + 1)
                    nc.scalar.sqrt(rstd[:, 1, :], rstd[:, 0, :]).then_inc(s["dev"], 1)

                def copy_turned(c, slot, half, b, body):
                    act.wait_ge(s["turned"], c + 1)
                    wait(act, s["routed"], c)
                    nc.scalar.copy(xT[:, :, :], pT[:, :, :]).then_inc(s["xt_ready"], 1)

                chunk_loop(act, [(0, copy_turned), (1, root)], BN)
                act.wait_ge(s["shifted"], 2 * B)
                nc.scalar.activation(weights[:, :, :], LG[:, :, :], ACT.Exp).then_inc(s["weighed"], 1)

            @block.tensor
            def _(pe):
                pe.wait_ge(s["w_in"], 16)

                def project_out(c, slot, half, b, body):
                    pe.wait_ge(s["divided"], c + 1)
                    wait(pe, s["added"], c - 1)
                    for t in range(CT):
                        for g in range(2):
                            last = nc.tensor.matmul(pW[:, half, t, :], osl[:, slot, g, t * P:(t + 1) * P],
                                                    woT[:, g, :], start=(g == 0), stop=(g == 1))
                    last.then_inc(s["wo_mm"], 1)

                def turn(c, slot, half, b, body):
                    pe.wait_ge(s["xn_ready"], c + 1)
                    wait(pe, s["xt_ready"], c)
                    for t in range(CT):
                        for d in range(2):
                            last = nc.tensor.transpose(pT[:, d, t * P:(t + 1) * P], xn[:, slot, t, d * P:(d + 1) * P],
                                                       identF[:, :])
                    last.then_inc(s["turned"], 1)

                def route(c, slot, half, b, body):
                    pe.wait_ge(s["xt_ready"], c + 1)
                    wait(pe, s["shifted"], c)
                    for t in range(CT):
                        for d in range(2):
                            last = nc.tensor.matmul(pL[:, t, :], xT[:, d, t * P:(t + 1) * P], wr[:, d, :],
                                                    start=(d == 0), stop=(d == 1))
                    last.then_inc(s["routed"], 1)

                def count(c, slot, half, b, body):
                    pe.wait_ge(s["oh"], c + 1)
                    wait(pe, s["ranked"], c)
                    nc.tensor.matmul(pC[:, 0:CT * E], upper[:, :], onehot[:, half, :], start=True, stop=False)
                    for t in range(1, CT):
                        nc.tensor.matmul(pC[:, t * E:CT * E], allone[:, :], onehot[:, half, 0:(CT - t) * E],
                                         start=False, stop=(t == CT - 1))
                    for t in range(CT):
                        last = nc.tensor.matmul(pC[:, CT * E:], allone[:, :], onehot[:, half, t * E:(t + 1) * E],
                                                start=(t == 0), stop=(t == CT - 1))
                    last.then_inc(s["cum"], 1)

                pe.wait_ge(s["mask"], 2)
                chunk_loop(pe, [(1, project_out), (0, turn), (0, route), (-1, count)], BN)
    give_back()


def experts(nc, name, w, BUF, YD, identF):
    R = 4
    FULL = CAP // P
    LASTR = CAP - FULL * P
    rows_of = [P] * FULL + ([LASTR] if LASTR else [])
    TILES = len(rows_of)
    s, give_back = semaphores(nc, "x_turned xt_ready gu_mm silu hidden down_mm y_ready passed", in_x=R, in_w=R, y_out=2)
    with ExitStack() as ctx:
        def sb(label, shape, dt=F32):
            return ctx.enter_context(nc.sbuf_tensor(f"{name}_{label}", shape, dt))

        xe = sb("xe", [P, R, TILES, D])
        wg, wu, wd = (sb(f"w{k}", [P, R, 2, D]) for k in "gud")
        xT = sb("xT", [P, 2, 2, CAP])
        sg = sb("sg", [P, 2, CAP])
        hid = sb("hid", [P, 2, 2, CAP])
        y = sb("y", [P, 2, TILES, D])

        def psum(label, shape):
            return ctx.enter_context(nc.psum_tensor(f"{name}_{label}", shape, F32))

        pT, pG, pU = psum("pT", [P, 2, 512]), psum("pG", [P, 2, 512]), psum("pU", [P, 2, 512])
        pY = psum("pY", [P, 4, D])

        def expert_loop(eng, stages):
            def body(i):
                for j in range(R):
                    for lag, step in stages:
                        k = j + lag
                        if not isinstance(i, int) or 0 <= R * i + k < E:
                            step(R * i + k, k % R, i + k // R)
            body(-1)
            body(0)
            with eng.Fori(1, E // R - 1) as i:
                body(i)
            body(E // R - 1)
            body(E // R)

        with nc.Block() as block:
            @block.sync
            def _(sp):
                def load(e, slot, body):
                    wait_apart(sp, s, s["x_turned"], e - R + 1)
                    src = BUF.rearrange("(e c) d -> e c d", c=CAP)
                    sp.dma_start(xe[:, slot, 0:FULL, :],
                                 src[e, 0:FULL * P, :].rearrange("(t p) d -> p t d", p=P)).then_inc(s["in_x"][slot], 16)
                    if LASTR:
                        sp.dma_start(xe[0:LASTR, slot, FULL, :], src[e, FULL * P:CAP, :]).then_inc(s["in_x"][slot], 16)
                    wait_apart(sp, s, s["down_mm"], e - R + 1)
                    for dst, weights in ((wg, w["gate"]), (wu, w["up"]), (wd, w["down"])):
                        sp.dma_start(dst[:, slot, :, :],
                                     weights[e].rearrange("(a p) f -> p a f", p=P)).then_inc(s["in_w"][slot], 16)

                def store(e, slot, body):
                    wait_apart(sp, s, s["y_ready"], e + 1)
                    dst = YD.rearrange("(e c) d -> e c d", c=CAP)
                    sp.dma_start(dst[e, 0:FULL * P, :].rearrange("(t p) d -> p t d", p=P),
                                 y[:, slot % 2, 0:FULL, :]).then_inc(s["y_out"][slot % 2], 16)
                    if LASTR:
                        sp.dma_start(dst[e, FULL * P:CAP, :], y[0:LASTR, slot % 2, FULL, :]).then_inc(s["y_out"][slot % 2], 16)

                expert_loop(sp, [(3, load), (-1, store)])
                for k in range(2):
                    sp.wait_ge(s["y_out"][k], 16 * 2 * E // 2)

            @block.tensor
            def _(pe):
                def turn(e, slot, body):
                    pe.wait_ge(s["in_x"][slot], 32 * (body + 1))
                    wait(pe, s["xt_ready"], e)
                    at = 0
                    for t, rows in enumerate(rows_of):
                        for d in range(2):
                            last = nc.tensor.transpose(pT[:, d, at:at + rows], xe[0:rows, slot, t, d * P:(d + 1) * P],
                                                       identF[0:rows, 0:rows])
                        at += rows
                    last.then_inc(s["x_turned"], 1)

                def gate_up(e, slot, body):
                    pe.wait_ge(s["in_w"][slot], 48 * (body + 1))
                    pe.wait_ge(s["xt_ready"], e + 1)
                    wait(pe, s["hidden"], e)
                    for out, weights in ((pG, wg), (pU, wu)):
                        for f in range(2):
                            for d in range(2):
                                last = nc.tensor.matmul(out[:, f, 0:CAP], weights[:, slot, d, f * P:(f + 1) * P],
                                                        xT[:, slot % 2, d, :], start=(d == 0), stop=(d == 1))
                        last.then_inc(s["gu_mm"], 1)

                def down(e, slot, body):
                    pe.wait_ge(s["hidden"], e + 1)
                    wait(pe, s["y_ready"], e)
                    at = 0
                    for t, rows in enumerate(rows_of):
                        for f in range(2):
                            last = nc.tensor.matmul(pY[0:rows, t, :], hid[:, slot % 2, f, at:at + rows],
                                                    wd[:, slot, f, :], start=(f == 0), stop=(f == 1))
                        at += rows
                    last.then_inc(s["down_mm"], 1)

                expert_loop(pe, [(0, gate_up), (1, turn), (-1, down)])

            @block.scalar
            def _(act):
                def copy(e, slot, body):
                    act.wait_ge(s["x_turned"], e + 1)
                    wait(act, s["gu_mm"], 2 * (e - 1))
                    nc.scalar.copy(xT[:, slot % 2, :, :], pT[:, :, 0:CAP]).then_inc(s["xt_ready"], 1)

                def silu(e, slot, body):
                    act.wait_ge(s["gu_mm"], 2 * e + 1)
                    wait(act, s["hidden"], e)
                    nc.scalar.activation(sg[:, :, :], pG[:, :, 0:CAP], ACT.Silu).then_inc(s["silu"], 1)

                expert_loop(act, [(0, silu), (1, copy)])

            @block.vector
            def _(dve):
                def multiply(e, slot, body):
                    dve.wait_ge(s["silu"], e + 1)
                    dve.wait_ge(s["gu_mm"], 2 * e + 2)
                    wait(dve, s["down_mm"], e - 1)
                    nc.vector.tensor_tensor(hid[:, slot % 2, :, :], sg[:, :, :], pU[:, :, 0:CAP],
                                            ALU.mult).then_inc(s["hidden"], 1)

                def copy(e, slot, body):
                    dve.wait_ge(s["down_mm"], e + 1)
                    wait(dve, s["y_out"][slot % 2], 32 * (2 * body + slot // 2))
                    nc.vector.tensor_copy(y[:, slot % 2, 0:FULL, :], pY[:, 0:FULL, :])
                    nc.vector.tensor_copy(y[0:LASTR, slot % 2, FULL, :], pY[0:LASTR, FULL, :]).then_inc(s["y_ready"], 1)

                expert_loop(dve, [(0, multiply), (-1, copy)])
    give_back()


def combine(nc, X, YD, gate, gidx, out, moved, before):
    R = MOVES
    s, give_back = semaphores(nc, "combined", out_sent=4)
    with ExitStack() as ctx:
        yt = ctx.enter_context(nc.sbuf_tensor("final_yt", [P, R, D], F32))
        with nc.Block() as block:
            @block.gpsimd
            def _(pool):
                for t in range(NT):
                    wait(pool, s["combined"], t - R + 1)
                    nc.gpsimd.indirect_dma_start(
                        out=yt[:, t % R, :], out_offset=None, in_=YD,
                        in_offset=bass.IndirectOffsetOnAxis(ap=gidx[:, t:t + 1], axis=0),
                        bounds_check=E * CAP - 1, oob_is_err=False).then_inc(moved[t % MOVES], 16)

            @block.vector
            def _(dve):
                for t in range(NT):
                    dve.wait_ge(moved[t % MOVES], before + 16 * (t // MOVES + 1))
                    nc.vector.scalar_tensor_tensor(out=X[:, t, :], in0=yt[:, t % R, :], scalar=gate[:, t:t + 1],
                                                   in1=X[:, t, :], op0=ALU.mult, op1=ALU.add).then_inc(s["combined"], 1)

            @block.sync
            def _(sp):
                rows = out.rearrange("b (t p) d -> p (b t) d", p=P)
                for c in range(2 * B):
                    sp.wait_ge(s["combined"], CT * (c + 1))
                    sp.dma_start(rows[:, c * CT:(c + 1) * CT, :],
                                 X[:, c * CT:(c + 1) * CT, :]).then_inc(s["out_sent"][c % 4], 16)
                for k in range(4):
                    sp.wait_ge(s["out_sent"][k], 16 * (2 * B // 4))
    give_back()


def block_kernel(nc, x, a_wq, a_wk, a_wv, a_wo, emb, b_wq, b_bq, b_wk, b_bk, b_wv, b_bv, b_wo, b_bo,
                 w_router, w_gate, w_up, w_down, out):
    Q = nc.dram_tensor("q_parts", (2 * B, 3, P, T), BF16).ap()
    KA = nc.dram_tensor("ka_parts", (2, 2 * B, 3, 32, T), BF16).ap()
    KB = nc.dram_tensor("kb_parts", (2 * B, 3, P, T), BF16).ap()
    VA = nc.dram_tensor("va", (2 * B, P, 2, KT, VW), F32).ap()
    VB = nc.dram_tensor("vb", (2 * B, P, 2, KT, HG * VW), F32).ap()
    OV = nc.dram_tensor("attended", (2 * B, 2, P, HALF), F32).ap()
    DN = nc.dram_tensor("denominators", (2 * B, 2, 2 * HG, HALF), F32).ap()
    RD = nc.dram_tensor("reciprocals", (2 * B, 2, 2 * HG, HALF), F32).ap()
    RR = nc.dram_tensor("relative_rows", (2, STEPS, P, RELROW), F32).ap()
    MD = nc.dram_tensor("maxima", (BODY, 3 * HG * 4, P), BF16).ap()
    BUF = nc.dram_tensor("expert_in", (E * CAP, D), F32).ap()
    YD = nc.dram_tensor("expert_out", (E * CAP, D), F32).ap()
    with ExitStack() as ctx:
        def sb(name, shape, dt=F32):
            return ctx.enter_context(nc.sbuf_tensor(name, shape, dt))

        identF, identB = sb("identF", [P, P]), sb("identB", [P, P], BF16)
        gate, gidx = sb("gate", [P, NT]), sb("gidx", [P, NT], U32)
        s, give_back = semaphores(nc, "id_zero id_one")
        once = ExitStack()
        zeros = once.enter_context(nc.sbuf_tensor("zeros", [P, CAP * E * D // P // (2 * B)], F32))
        clearing, clearing_done = semaphores(nc, "zeroed")
        with nc.Block() as block:
            @block.gpsimd
            def _(pool):
                nc.gpsimd.memset(identF[:, :], 0.0).then_inc(s["id_zero"], 1)
                pool.wait_ge(s["id_zero"], 1)
                nc.gpsimd.affine_select(out=identF[:, :], in_=identF[:, :], compare_op=ALU.not_equal,
                                        fill=1.0, base=0, pattern=[[-1, P]],
                                        channel_multiplier=1).then_inc(s["id_one"], 1)

            @block.vector
            def _(dve):
                nc.vector.memset(zeros[:, :], 0.0)
                dve.wait_ge(s["id_one"], 1)
                nc.vector.tensor_copy(identB[:, :], identF[:, :])
        give_back()
        wa = {"q": a_wq, "k": a_wk, "v": a_wv, "E": emb, "o": a_wo, "r": w_router}
        wb = {"q": b_wq, "k": b_wk, "v": b_wv, "bq": b_bq, "bk": b_bk, "bv": b_bv, "o": b_wo, "bo": b_bo,
              "r": w_router}
        we = {"gate": w_gate, "up": w_up, "down": w_down}

        project(nc, "A", x, None, wa, Q, KA, VA, identF, clear=(zeros, clearing["zeroed"], BUF, RR))
        clearing_done()
        once.close()
        attend(nc, "A", Q, KA, VA, OV, DN, emb, RR, MD, identF, identB)
        X = sb("X", [P, NT, D])
        moved = [ctx.enter_context(nc.semaphore(f"moved{k}")) for k in range(MOVES)]
        sent = [ctx.enter_context(nc.semaphore(f"sent{k}")) for k in range(2 * MOVES)]
        for kind, w, before in (("A", wa, 0), ("B", wb, 16 * (NT // (2 * MOVES)))):
            if kind == "B":
                project(nc, "B", None, X, wb, Q, KB, VB, identF,
                        tail=(YD, gate, gidx, moved, 0))
                attend(nc, "B", Q, KB, VB, OV, DN, None, None, MD, identF, identB)
            after_attention(nc, kind, x, X, OV, DN, RD, w, identF, BUF, gate, gidx, sent, before)
            experts(nc, f"e{kind}", we, BUF, YD, identF)
        combine(nc, X, YD, gate, gidx, out, moved, 16 * (NT // MOVES))


_INS = ["L0_attn_a_x", "L0_attn_a_Wq", "L0_attn_a_Wk", "L0_attn_a_Wv", "L0_attn_a_Wo", "L0_attn_a_E",
        "L0_attn_b_wq", "L0_attn_b_bq", "L0_attn_b_wk", "L0_attn_b_bk", "L0_attn_b_wv", "L0_attn_b_bv",
        "L0_attn_b_wo", "L0_attn_b_bo", "L0_ffn_w_router", "L0_ffn_w_gate", "L0_ffn_w_up", "L0_ffn_w_down"]
_OUTS = [((8, 1024, 256), "float32")]


def kernel(**inputs):
    import numpy as _np
    import concourse.bacc as _bacc
    from concourse import mybir as _mybir
    from concourse.bass_utils import run_bass_kernel_spmd as _run

    nc = _bacc.Bacc("TRN2", target_bir_lowering=False, num_devices=1)
    arrays, args = {}, []
    for name in _INS:
        a = _np.ascontiguousarray(inputs[name][::-1] if name == "L0_attn_a_E" else inputs[name])
        arrays[f"in_{name}_dram"] = a
        args.append(nc.dram_tensor(f"in_{name}_dram", a.shape, _mybir.dt.from_np(a.dtype), kind="ExternalInput").ap())
    for i, (shape, dtype) in enumerate(_OUTS):
        dt = _mybir.dt.from_np(_np.dtype(dtype))
        args.append(nc.dram_tensor(f"out_{i}_dram", shape, dt, kind="ExternalOutput").ap())
    block_kernel(nc, *args)
    r = _run(nc, [arrays], core_ids=[0])
    return r.results[0]["out_0_dram"]
```
